# Optimizing a Trainium2 kernel written in Bass

```python
import numpy as np
import jax
import jax.numpy as jnp

def _softmax(x, axis=-1):
    return jax.nn.softmax(x, axis=axis)

def _gelu(x):
    return jax.nn.gelu(x, approximate=True)

def _silu(x):
    return jax.nn.silu(x)

def _sigmoid(x):
    return jax.nn.sigmoid(x)

def _layernorm(x, axis=-1, eps=1e-05):
    m = jnp.mean(x, axis=axis, keepdims=True)
    v = jnp.var(x, axis=axis, keepdims=True)
    return (x - m) / jnp.sqrt(v + eps)

def _scatter_add(tgt, idx, src, axis=0):
    return tgt.at[idx].add(src)

def _segment_sum(src, seg, n):
    return jax.ops.segment_sum(src, seg, n)
kernel_name = 'mk_vit_tower_d2_tok_img768_r4_1eecf5'

def setup_inputs(seed: int=0):
    np.random.seed(seed)
    _w = jnp.asarray

    def _rec_inputs():
        import jax
        import jax.numpy as jnp
        _rk = jax.random.key(seed)
        x = -0.00016672 + 0.999947 * jax.random.normal(jax.random.fold_in(_rk, 1), (64, 3, 96, 96), jnp.float32)
        return x
    x = _rec_inputs()

    def _L0_tok_setup():
        import jax, jax.numpy as jnp
        import numpy as np
        P1, P2 = (16, 16)
        EPS = 0.0001

        def _patchify(x):
            b, c, H, W = x.shape
            h, w = (H // P1, W // P2)
            x = x.reshape(b, c, h, P1, w, P2)
            x = x.transpose(0, 2, 4, 3, 5, 1)
            return x.reshape(b, h * w, P1 * P2 * c)

        def _rmsnorm2d(x, weight):
            ms = jnp.mean(jnp.square(x), axis=(-2, -1), keepdims=True)
            return x * jax.lax.rsqrt(ms + EPS) * weight
        key = jax.random.key(seed)
        k0, k1, k2, k3, k4 = jax.random.split(key, 5)
        B, C, H, W_ = (64, 3, 96, 96)
        num_patches = H // P1 * (W_ // P2)
        patch_dim = C * P1 * P2
        proj_dim = 192
        x = jax.random.normal(k0, (B, C, H, W_), dtype=jnp.float32)
        g1 = 1.0 + 0.02 * jax.random.normal(k1, (num_patches, patch_dim), dtype=jnp.float32)
        W = jax.random.normal(k2, (proj_dim, patch_dim), dtype=jnp.float32) * patch_dim ** (-0.5)
        b = jax.random.normal(k3, (proj_dim,), dtype=jnp.float32) * 0.01
        g2 = 1.0 + 0.02 * jax.random.normal(k4, (num_patches, proj_dim), dtype=jnp.float32)
        return {'x': x, 'g1': g1, 'W': W, 'b': b, 'g2': g2}
    _L0_tok_all = _L0_tok_setup()
    _L0_tok_in = {k: v for k, v in _L0_tok_all.items() if k in ('g1', 'W', 'b', 'g2')}
    del _L0_tok_all

    def _L0_attn_setup():
        import jax, jax.numpy as jnp
        import numpy as np
        B, N, C = (32, 577, 192)
        H = 12
        D = C // H
        key = jax.random.key(seed)
        ks = jax.random.split(key, 4)
        x = jax.random.normal(ks[0], (B, N, C), dtype=jnp.float32)
        w_qkv = jax.random.normal(ks[1], (C, 3 * C), dtype=jnp.float32) * C ** (-0.5)
        b_qkv = jnp.zeros((3 * C,), dtype=jnp.float32)
        scale = jnp.ones((H,), dtype=jnp.float32) * D ** (-0.5)
        w_proj = jax.random.normal(ks[2], (C, C), dtype=jnp.float32) * C ** (-0.5)
        b_proj = jnp.zeros((C,), dtype=jnp.float32)
        return {'x': x, 'w_qkv': w_qkv, 'b_qkv': b_qkv, 'scale': scale, 'w_proj': w_proj, 'b_proj': b_proj}
    _L0_attn_all = _L0_attn_setup()
    _L0_attn_in = {k: v for k, v in _L0_attn_all.items() if k in ('w_qkv', 'b_qkv', 'scale', 'w_proj', 'b_proj')}
    del _L0_attn_all

    def _L0_ffn_setup():
        import jax, jax.numpy as jnp
        import numpy as np
        import math
        B, T, C = (8, 512, 192)
        E = 3
        HD = C // E
        TOPK = 2
        NGLOB = 4

        def _masked_softmax(att, mask):
            att = jnp.where(mask, -jnp.inf, att)
            return jax.nn.softmax(att, axis=-1)
        key = jax.random.key(seed)
        ks = jax.random.split(key, 16)
        s = 0.02
        return {'x': jax.random.normal(ks[0], (B, T, C), jnp.float32), 'Wqk': jax.random.normal(ks[1], (C, 2 * C), jnp.float32) * s, 'bqk': jnp.zeros((2 * C,), jnp.float32), 'Wv': jax.random.normal(ks[2], (E, C, HD), jnp.float32) * s, 'bv': jnp.zeros((E, HD), jnp.float32), 'conv_w': jax.random.normal(ks[3], (HD, 1, 3), jnp.float32) * s, 'conv_b': jnp.zeros((HD,), jnp.float32), 'glob': jax.random.normal(ks[4], (NGLOB, HD), jnp.float32) * 0.02, 'pos_bias': jnp.zeros((64, 64), jnp.float32), 'Wg1': jax.random.normal(ks[5], (C, 32), jnp.float32) * s, 'bg1': jnp.zeros((32,), jnp.float32), 'Wg2': jax.random.normal(ks[6], (32, E), jnp.float32) * s, 'bg2': jnp.zeros((E,), jnp.float32), 'Wp': jax.random.normal(ks[7], (C, C), jnp.float32) * s, 'bp': jnp.zeros((C,), jnp.float32)}
    _L0_ffn_all = _L0_ffn_setup()
    _L0_ffn_in = {k: v for k, v in _L0_ffn_all.items() if k in ('Wqk', 'bqk', 'Wv', 'bv', 'conv_w', 'conv_b', 'glob', 'pos_bias', 'Wg1', 'bg1', 'Wg2', 'bg2', 'Wp', 'bp')}
    del _L0_ffn_all

    def _L1_attn_setup():
        import math
        import jax, jax.numpy as jnp
        import numpy as np
        B, S, IN_DIM, EMB, H, MAX_LEN = (4, 128, 192, 192, 12, 128)
        D = EMB // H
        key = jax.random.key(seed)
        ks = jax.random.split(key, 16)

        def lin(k, fan_in, fan_out):
            lim = math.sqrt(6.0 / (fan_in + fan_out))
            W = jax.random.uniform(k, (fan_in, fan_out), minval=-lim, maxval=lim, dtype=jnp.float32)
            return (W, jnp.zeros((fan_out,), jnp.float32))
        Wq, bq = lin(ks[0], IN_DIM, EMB)
        Wk, bk = lin(ks[1], IN_DIM, EMB)
        Wv, bv = lin(ks[2], IN_DIM, EMB)
        Wpk, bpk = lin(ks[3], IN_DIM, EMB)
        Wpq, bpq = lin(ks[4], IN_DIM, EMB)
        Wo, bo = lin(ks[5], EMB, IN_DIM)
        rel_table = jax.random.normal(ks[6], (2 * MAX_LEN - 1, IN_DIM), jnp.float32)
        x = jax.random.normal(ks[7], (B, S, IN_DIM), jnp.float32)
        return {'x': x, 'Wq': Wq, 'bq': bq, 'Wk': Wk, 'bk': bk, 'Wv': Wv, 'bv': bv, 'rel_table': rel_table, 'Wpk': Wpk, 'bpk': bpk, 'Wpq': Wpq, 'bpq': bpq, 'Wo': Wo, 'bo': bo}
    _L1_attn_all = _L1_attn_setup()
    _L1_attn_in = {k: v for k, v in _L1_attn_all.items() if k in ('Wq', 'bq', 'Wk', 'bk', 'Wv', 'bv', 'rel_table', 'Wpk', 'bpk', 'Wpq', 'bpq', 'Wo', 'bo')}
    del _L1_attn_all

    def _L1_ffn_setup():
        import jax, jax.numpy as jnp
        import numpy as np
        B, N, C, H, E = (8, 256, 192, 768, 4)
        key = jax.random.key(seed)
        ks = jax.random.split(key, 8)
        s_in = 1.0 / np.sqrt(C)
        s_h = 1.0 / np.sqrt(H)
        return {'x': jax.random.normal(ks[0], (B, N, C), dtype=jnp.float32), 'gate_w': jax.random.normal(ks[1], (C, E), dtype=jnp.float32) * 0.01, 'gate_b': jnp.zeros((E,), dtype=jnp.float32), 'gate_center': jnp.zeros((E,), dtype=jnp.float32), 'w1': jax.random.uniform(ks[2], (E, C, H), jnp.float32, -s_in, s_in), 'b1': jax.random.uniform(ks[3], (E, H), jnp.float32, -s_in, s_in), 'w2': jax.random.uniform(ks[4], (E, H, C), jnp.float32, -s_h, s_h), 'b2': jax.random.uniform(ks[5], (E, C), jnp.float32, -s_h, s_h)}
    _L1_ffn_all = _L1_ffn_setup()
    _L1_ffn_in = {k: v for k, v in _L1_ffn_all.items() if k in ('gate_w', 'gate_b', 'gate_center', 'w1', 'b1', 'w2', 'b2')}
    del _L1_ffn_all
    return {'x': x, 'L0_tok_g1': _L0_tok_in['g1'], 'L0_tok_W': _L0_tok_in['W'], 'L0_tok_b': _L0_tok_in['b'], 'L0_tok_g2': _L0_tok_in['g2'], 'L0_attn_w_qkv': _L0_attn_in['w_qkv'], 'L0_attn_b_qkv': _L0_attn_in['b_qkv'], 'L0_attn_scale': _L0_attn_in['scale'], 'L0_attn_w_proj': _L0_attn_in['w_proj'], 'L0_attn_b_proj': _L0_attn_in['b_proj'], 'L0_ffn_Wqk': _L0_ffn_in['Wqk'], 'L0_ffn_bqk': _L0_ffn_in['bqk'], 'L0_ffn_Wv': _L0_ffn_in['Wv'], 'L0_ffn_bv': _L0_ffn_in['bv'], 'L0_ffn_conv_w': _L0_ffn_in['conv_w'], 'L0_ffn_conv_b': _L0_ffn_in['conv_b'], 'L0_ffn_glob': _L0_ffn_in['glob'], 'L0_ffn_pos_bias': _L0_ffn_in['pos_bias'], 'L0_ffn_Wg1': _L0_ffn_in['Wg1'], 'L0_ffn_bg1': _L0_ffn_in['bg1'], 'L0_ffn_Wg2': _L0_ffn_in['Wg2'], 'L0_ffn_bg2': _L0_ffn_in['bg2'], 'L0_ffn_Wp': _L0_ffn_in['Wp'], 'L0_ffn_bp': _L0_ffn_in['bp'], 'L1_attn_Wq': _L1_attn_in['Wq'], 'L1_attn_bq': _L1_attn_in['bq'], 'L1_attn_Wk': _L1_attn_in['Wk'], 'L1_attn_bk': _L1_attn_in['bk'], 'L1_attn_Wv': _L1_attn_in['Wv'], 'L1_attn_bv': _L1_attn_in['bv'], 'L1_attn_rel_table': _L1_attn_in['rel_table'], 'L1_attn_Wpk': _L1_attn_in['Wpk'], 'L1_attn_bpk': _L1_attn_in['bpk'], 'L1_attn_Wpq': _L1_attn_in['Wpq'], 'L1_attn_bpq': _L1_attn_in['bpq'], 'L1_attn_Wo': _L1_attn_in['Wo'], 'L1_attn_bo': _L1_attn_in['bo'], 'L1_ffn_gate_w': _L1_ffn_in['gate_w'], 'L1_ffn_gate_b': _L1_ffn_in['gate_b'], 'L1_ffn_gate_center': _L1_ffn_in['gate_center'], 'L1_ffn_w1': _L1_ffn_in['w1'], 'L1_ffn_b1': _L1_ffn_in['b1'], 'L1_ffn_w2': _L1_ffn_in['w2'], 'L1_ffn_b2': _L1_ffn_in['b2']}

def reference(x, L0_tok_g1, L0_tok_W, L0_tok_b, L0_tok_g2, L0_attn_w_qkv, L0_attn_b_qkv, L0_attn_scale, L0_attn_w_proj, L0_attn_b_proj, L0_ffn_Wqk, L0_ffn_bqk, L0_ffn_Wv, L0_ffn_bv, L0_ffn_conv_w, L0_ffn_conv_b, L0_ffn_glob, L0_ffn_pos_bias, L0_ffn_Wg1, L0_ffn_bg1, L0_ffn_Wg2, L0_ffn_bg2, L0_ffn_Wp, L0_ffn_bp, L1_attn_Wq, L1_attn_bq, L1_attn_Wk, L1_attn_bk, L1_attn_Wv, L1_attn_bv, L1_attn_rel_table, L1_attn_Wpk, L1_attn_bpk, L1_attn_Wpq, L1_attn_bpq, L1_attn_Wo, L1_attn_bo, L1_ffn_gate_w, L1_ffn_gate_b, L1_ffn_gate_center, L1_ffn_w1, L1_ffn_b1, L1_ffn_w2, L1_ffn_b2):
    import jax
    import jax.numpy as jnp

    def _L0_tok_ref(x, g1, W, b, g2):
        import jax, jax.numpy as jnp
        import numpy as np
        P1, P2 = (16, 16)
        EPS = 0.0001

        def _patchify(x):
            b, c, H, W = x.shape
            h, w = (H // P1, W // P2)
            x = x.reshape(b, c, h, P1, w, P2)
            x = x.transpose(0, 2, 4, 3, 5, 1)
            return x.reshape(b, h * w, P1 * P2 * c)

        def _rmsnorm2d(x, weight):
            ms = jnp.mean(jnp.square(x), axis=(-2, -1), keepdims=True)
            return x * jax.lax.rsqrt(ms + EPS) * weight
        p = _patchify(x)
        p = _rmsnorm2d(p, g1)
        y = jnp.einsum('bnd,ed->bne', p, W) + b
        return _rmsnorm2d(y, g2)

    def _L0_attn_ref(x, w_qkv, b_qkv, scale, w_proj, b_proj):
        import jax, jax.numpy as jnp
        import numpy as np
        B, N, C = (32, 577, 192)
        H = 12
        D = C // H
        b, n, c = x.shape
        h = scale.shape[0]
        d = c // h
        qkv = (x @ w_qkv + b_qkv).reshape(b, n, 3, h, d)
        q = qkv[:, :, 0]
        k = qkv[:, :, 1]
        v = qkv[:, :, 2]
        attn = jnp.einsum('bihd,bjhd->bhij', q, k) * scale[None, :, None, None]
        if n > 1:
            mask = jnp.zeros((n, n), dtype=bool).at[1:, 1:].set(jnp.eye(n - 1, dtype=bool))
            attn = jnp.where(mask[None, None], -jnp.inf, attn)
        attn = jax.nn.softmax(attn, axis=-1)
        out = jnp.einsum('bhij,bjhd->bihd', attn, v).reshape(b, n, c)
        return out @ w_proj + b_proj

    def _L0_ffn_ref(x, Wqk, bqk, Wv, bv, conv_w, conv_b, glob, pos_bias, Wg1, bg1, Wg2, bg2, Wp, bp):
        import jax, jax.numpy as jnp
        import numpy as np
        import math
        B, T, C = (8, 512, 192)
        E = 3
        HD = C // E
        TOPK = 2
        NGLOB = 4

        def _masked_softmax(att, mask):
            att = jnp.where(mask, -jnp.inf, att)
            return jax.nn.softmax(att, axis=-1)
        Bx, Tx, Cx = x.shape
        scale = 1.0 / math.sqrt(HD)
        gate = jax.nn.softmax(jax.nn.relu(x @ Wg1 + bg1) @ Wg2 + bg2, axis=-1)
        top_w, top_i = jax.lax.top_k(gate, TOPK)
        top_w = jax.nn.softmax(top_w, axis=-1)
        qk = x @ Wqk + bqk
        q, k = (qk[..., :Cx], qk[..., Cx:])
        q = q.reshape(Bx, Tx, E, HD)
        k = k.reshape(Bx, Tx, E, HD)
        rows = jnp.arange(Tx)[:, None]
        ys = []
        for e in range(E):
            qe = q[:, :, e]
            ke = k[:, :, e]
            ve = x @ Wv[e] + bv[e]
            if e == 0:
                qc = jnp.transpose(qe, (0, 2, 1))
                qc = jax.lax.conv_general_dilated(qc, conv_w, window_strides=(1,), padding=((1, 1),), feature_group_count=HD, dimension_numbers=('NCH', 'OIH', 'NCH'))
                qe = jnp.transpose(qc + conv_b[None, :, None], (0, 2, 1))
            elif e == 1:
                gb = jnp.broadcast_to(glob[None], (Bx, NGLOB, HD))
                ke = jnp.concatenate([ke, gb], axis=1)
                ve = jnp.concatenate([ve, gb], axis=1)
            att = jnp.einsum('btd,bsd->bts', qe, ke) * scale
            if e == 2 and Tx <= 64:
                att = att + pos_bias[:Tx, :Tx][None]
            S = att.shape[-1]
            mask = jnp.arange(S)[None, :] > rows
            att = _masked_softmax(att, mask[None])
            ys.append(jnp.einsum('bts,bsd->btd', att, ve))
        ys = jnp.stack(ys, axis=2)
        w_e = jnp.sum(jax.nn.one_hot(top_i, E, dtype=x.dtype) * top_w[..., None], axis=-2)
        combined = (ys * w_e[..., None]).reshape(Bx, Tx, Cx)
        return combined @ Wp + bp

    def _L1_attn_ref(x, Wq, bq, Wk, bk, Wv, bv, rel_table, Wpk, bpk, Wpq, bpq, Wo, bo):
        import math
        import jax, jax.numpy as jnp
        import numpy as np
        B, S, IN_DIM, EMB, H, MAX_LEN = (4, 128, 192, 192, 12, 128)
        D = EMB // H
        Bx, Sx, _ = x.shape

        def shape_heads(t):
            return t.reshape(Bx, Sx, H, D).transpose(0, 2, 1, 3)
        q = shape_heads(x @ Wq + bq)
        k = shape_heads(x @ Wk + bk)
        v = shape_heads(x @ Wv + bv)
        pos = jnp.arange(Sx)
        ids = jnp.clip(pos[:, None] - pos[None, :], -(MAX_LEN - 1), MAX_LEN - 1) + (MAX_LEN - 1)
        pos_k = (rel_table @ Wpk + bpk)[ids].reshape(Sx, Sx, H, D)
        pos_q = (rel_table @ Wpq + bpq)[ids].reshape(Sx, Sx, H, D)
        scores = jnp.einsum('bhid,bhjd->bhij', q, k)
        scores = scores + jnp.einsum('bhid,ijhd->bhij', q, pos_k)
        scores = scores + jnp.einsum('ijhd,bhjd->bhij', pos_q, k)
        scores = scores / math.sqrt(D * 3.0)
        attn = jax.nn.softmax(scores, axis=-1)
        out = jnp.einsum('bhij,bhjd->bhid', attn, v)
        out = out.transpose(0, 2, 1, 3).reshape(Bx, Sx, EMB)
        return out @ Wo + bo

    def _L1_ffn_ref(x, gate_w, gate_b, gate_center, w1, b1, w2, b2):
        import jax, jax.numpy as jnp
        import numpy as np
        B, N, C, H, E = (8, 256, 192, 768, 4)
        b, n, c = x.shape
        scores = jnp.einsum('bnc,ce->bne', x, gate_w) + gate_b
        p_experts = jax.nn.softmax(scores - gate_center, axis=-1)
        expert = jnp.argmax(p_experts, axis=-1).reshape(-1)
        xt = x.reshape(-1, c)
        h = jax.nn.gelu(jnp.einsum('tc,ech->eth', xt, w1) + b1[:, None, :], approximate=False)
        out_all = jnp.einsum('eth,ehc->etc', h, w2) + b2[:, None, :]
        out = jnp.take_along_axis(out_all, expert[None, :, None], axis=0)[0]
        return out.reshape(b, n, c)
    h = _L0_tok_ref(x, L0_tok_g1, L0_tok_W, L0_tok_b, L0_tok_g2)
    h = h + _L0_attn_ref(_layernorm(h, axis=-1), L0_attn_w_qkv, L0_attn_b_qkv, L0_attn_scale, L0_attn_w_proj, L0_attn_b_proj)
    h = h + _L0_ffn_ref(_layernorm(h, axis=-1), L0_ffn_Wqk, L0_ffn_bqk, L0_ffn_Wv, L0_ffn_bv, L0_ffn_conv_w, L0_ffn_conv_b, L0_ffn_glob, L0_ffn_pos_bias, L0_ffn_Wg1, L0_ffn_bg1, L0_ffn_Wg2, L0_ffn_bg2, L0_ffn_Wp, L0_ffn_bp)
    h = h + _L1_attn_ref(_layernorm(h, axis=-1), L1_attn_Wq, L1_attn_bq, L1_attn_Wk, L1_attn_bk, L1_attn_Wv, L1_attn_bv, L1_attn_rel_table, L1_attn_Wpk, L1_attn_bpk, L1_attn_Wpq, L1_attn_bpq, L1_attn_Wo, L1_attn_bo)
    h = h + _L1_ffn_ref(_layernorm(h, axis=-1), L1_ffn_gate_w, L1_ffn_gate_b, L1_ffn_gate_center, L1_ffn_w1, L1_ffn_b1, L1_ffn_w2, L1_ffn_b2)
    return h

_drawn_inputs = setup_inputs


def setup_inputs(seed=0):
    import zlib

    import numpy as np

    out = dict(_drawn_inputs(seed))
    spreads = {'L0_attn_b_qkv': (0.0, 0.1),
     'L0_attn_scale': (0.25, 0.2),
     'L0_attn_b_proj': (0.0, 0.1),
     'L0_ffn_bqk': (0.0, 0.8),
     'L0_ffn_bv': (0.0, 0.395),
     'L0_ffn_conv_b': (0.0, 2.0),
     'L0_ffn_pos_bias': (0.0, 2.0),
     'L0_ffn_bg1': (0.0, 0.8),
     'L0_ffn_bg2': (0.0, 0.957),
     'L0_ffn_bp': (0.0, 0.1),
     'L1_attn_bq': (0.0, 0.336),
     'L1_attn_bk': (0.0, 0.444),
     'L1_attn_bv': (0.0, 0.1),
     'L1_attn_bpk': (0.0, 2.0),
     'L1_attn_bpq': (0.0, 0.363),
     'L1_attn_bo': (0.0, 0.1),
     'L1_ffn_gate_b': (0.0, 0.1),
     'L1_ffn_gate_center': (0.0, 0.1)}
    factors = {'L0_tok_b': 2.689,
     'L0_ffn_Wqk': 8.0,
     'L0_ffn_Wv': 3.038,
     'L0_ffn_conv_w': 36.554,
     'L0_ffn_Wg1': 8.0,
     'L0_ffn_Wg2': 8.0,
     'L1_ffn_b1': 4.311,
     'L1_ffn_b2': 3.104}
    for name, (base, spread) in spreads.items():
        noise = np.random.default_rng([zlib.crc32(name.encode()), seed]).standard_normal(out[name].shape)
        drawn = base * np.exp(spread * noise) if base else spread * noise
        out[name] = jnp.asarray(drawn.astype(out[name].dtype))
    for name, factor in factors.items():
        out[name] = (out[name] * factor).astype(out[name].dtype)
    return out
```

```python
from contextlib import ExitStack

import numpy as np

import concourse.bass as bass
from concourse import mybir

F32 = mybir.dt.float32
ALU = mybir.AluOpType
ACT = mybir.ActivationFunctionType
AX = mybir.AxisListType.X

B, CH, IMG, PS = 64, 3, 96, 16
NTOK = (IMG // PS) ** 2
FEAT = CH * PS * PS
KF = FEAT // 128
C = 192
HC = C // 2
H, D = 12, 16
GI = 3
TT = GI * NTOK
NT = 2 * -(-B // (2 * GI))
BP = NT * GI
NP = NT // 2
E0, HD0, GH = 3, 64, 32
NE, HID = 4, 768
KH = HID // 128
REL = 2 * NTOK - 1
NEG = -1.0e30
TOK_EPS, LN_EPS = 1e-4, 1e-5

TOK_PACK = [("wt", KF * C), ("g1", KF * NTOK), ("tok_b", C), ("g2", C), ("ident", 128),
            ("same_image", TT), ("pixel_mean", TT),
            ("select_image", GI * TT)]
SLABS = ["q0", "k0", "v0", "o0", "fq", "fk", "fv", "q1", "k1", "v1", "o1", "pk", "pq"]
W_PACK = [(n, 2 * C) for n in SLABS] + [
    ("fg1", 2 * GH), ("fg2", E0), ("fpa", C), ("fpb", C), ("gate", 2 * NE), ("center", NE),
    ("relT", 2 * REL), ("relrevT", 2 * REL), ("head_mask", 6), ("head_scale", 2),
    ("third_mask", GI), ("diag_mask", NTOK), ("causal", TT), ("pos", TT), ("rank_up", E0),
    ("rank_down", NE), ("conv", 4), ("b2", NE * C)]
BIG_COLS = 2 * NE * HID + NE * KH * C


def columns(pack):
    at, out = 0, {}
    for name, n in pack:
        out[name] = (at, n)
        at += n
    return out, at


TOK_AT, TOK_COLS = columns(TOK_PACK)
W_AT, W_COLS = columns(W_PACK)


def build(nc, x_in, tok_in, w_in, moe_in, rel2, rel3, out):
    ctx = ExitStack()
    with ctx:
        def sb(name, shape):
            return ctx.enter_context(nc.sbuf_tensor(name, shape, F32))

        names = """tok_consts w_consts moe_weights load_x0 load_x1 xg_ready ssq_ready tok_ps
            rms1_in rms1 y_ready ysum_ready rms2_ps rms2_in rms2 masks_ready ones_ready mhalf_ready
            stats0 stats1 stats2 stats3 mean0 mean1 mean2 mean3 rstd_in0 rstd_in1 rstd_in2 rstd_in3
            rstd0 rstd1 rstd2 rstd3 xn0 xn1 xn2 xn3 xnT_ps0 xnT_ps1 xnT_ps2 xnT_ps3
            xnT0 xnT1 xnT2 xnT3 h0 h1 h2 h3
            qk_ps qz_ready kblk_ready v_tok_ps v_tok_ready v_ps vblk_ready s_ps biased biased2 row_max centred exped row_sum
            row_inv pn_ready pt_ps pT_ready o_ps oT_ready y_ps
            f_qk_ps f_vg_ps f_copied f_v_copied f_g1_ready f_conv0 f_conv1 f_conv_ready f_q1_ready
            f_gate_ps f_logits
            f_s_ps f_biased f_max f_centred f_exped f_sum f_factor f_pn f_pt_ps f_pT f_o_ps f_oT
            f_y_ps gmax gcentred gexp gsum ginv gprob gmin gle gval gvmax gkeep gexp2 gkexp gwsum
            f_den f_deninv l1_qk_ps l1_q_stored l1_k_stored
            relT_ps pkblk_ready pq_win_ready rel2_ps rel2_copied rel2_out0 rel2_out1 rel2_out2 rel2_out3 rel3_ps rel3_copied rel3_out
            load_rel0 load_rel1 q1_copied
            gate_ps glog glmax gleq glval glvmax onehot xn3T_stored
            hid_ps hid_ready moe_ps moe_sum moe_acc acc_first out0 out1""".split()
        sem = {n: ctx.enter_context(nc.semaphore(n)) for n in names}

        tokc = sb("tokc", [128, TOK_COLS])
        wc = sb("wc", [128, W_COLS])
        big = sb("big", [128, BIG_COLS])

        def tokw(name):
            a, n = TOK_AT[name]
            return tokc[:, a:a + n]

        def w(name):
            a, n = W_AT[name]
            return wc[:, a:a + n]

        def slab(name):
            return w(name).rearrange("p (c n) -> p c n", c=2)

        x_sb = sb("x_sb", [128, 2, KF * TT])
        xg = sb("xg", [128, 2, KF * TT])
        ssq = sb("ssq", [128, 2, GI])
        y_sb = sb("y_sb", [TT, 2, C])
        col = sb("col", [128, 2, 64])
        xn = sb("xn", [TT, 2, C])
        xnT = sb("xnT", [HC + 1, 2, 2, TT])
        hres = sb("hres", [TT, NT, C])
        qz = sb("qz", [HC, 2, 2, GI * (TT + NTOK)])
        kblk = sb("kblk", [HC, 2, 2, 6, TT])
        vblk = sb("vblk", [TT, 2, 12, 144])
        sc = sb("sc", [TT, 2, H * NTOK])
        pr = sb("pr", [TT, 2, H * NTOK])
        pT = sb("pT", [TT, 2, 4, TT])
        oT = sb("oT", [HC + 1, 2, 2, TT])
        head_scaled = sb("head_scaled", [HC, 2, 6])
        f_mask = sb("f_mask", [TT, E0, TT])
        f_q0 = sb("f_q0", [HD0, 2, GI, NTOK + 2])
        f_qc = sb("f_qc", [128, 2, 2, TT])
        f_q1 = sb("f_q1", [128, 2, TT])
        f_q2 = sb("f_q2", [128, 2, TT])
        f_k = sb("f_k", [128, 2, TT])
        f_k2 = sb("f_k2", [128, 2, TT])
        f_v = sb("f_v", [TT, 2, C])
        f_g1T = sb("f_g1T", [GH + 1, 2, TT])
        f_oT = sb("f_oT", [128, 2, 2, TT])
        gs = sb("gs", [TT, 2, 64])
        qT_all = sb("qT_all", [HC + 1, 2, NT * TT])
        kT_all = sb("kT_all", [HC, 2, NT * TT])
        n_rel3 = BP * 4 * NTOK
        pkblk = big[0:HC, n_rel3:n_rel3 + 12 * REL].rearrange("p (c s r) -> p c s r", c=2, s=6)
        pqblk = xg[0:HC].rearrange("p u n -> p (u n)")[:, 0:12 * REL].rearrange("p (c s r) -> p c s r", c=2, s=6)
        rel2_buf = [sc[0:BP, 0, :], sc[0:BP, 1, :], pr[0:BP, 0, :], pr[0:BP, 1, :]]
        rel_t = [[buf[0:TT, u, 0:H * NTOK] for buf in (xg, x_sb)] for u in range(2)]
        oh = sb("oh", [TT, NT, NE])
        mhalf = sb("mhalf", [128, 1])
        mone = sb("mone", [128, 1])
        v_sb = y_sb
        pq_win = [kblk[:, n, 0, 0:4, :] for n in range(2)]
        rel3_sb = big[0:TT, 0:n_rel3].rearrange("p (b g j) -> p b g j", b=BP, g=4)
        w1 = big[:, 0:2 * NE * HID].rearrange("p (e c n) -> p e c n", e=NE, c=2)
        w2 = big[:, 2 * NE * HID:].rearrange("p (e k n) -> p e k n", e=NE, k=KH)
        hid = x_sb
        ps = ctx.enter_context(nc.psum_tensor("ps", [128, 8, 512], F32))

        def bank(u, n):
            return ps[:, 4 * u + n, :]

        def c1(u, n, rows=TT):
            return col[0:rows, u, n:n + 1]

        wt = tokw("wt").rearrange("p (k n) -> p k n", k=KF)
        ident = tokw("ident")
        load_x = [sem["load_x0"], sem["load_x1"]]
        load_rel = [sem["load_rel0"], sem["load_rel1"]]
        stored_out = [sem["out0"], sem["out1"]]
        rel2_out = [sem["rel2_out0"], sem["rel2_out1"], sem["rel2_out2"], sem["rel2_out3"]]
        stats = [sem["stats0"], sem["stats1"], sem["stats2"], sem["stats3"]]
        mean = [sem["mean0"], sem["mean1"], sem["mean2"], sem["mean3"]]
        rstd = [sem["rstd0"], sem["rstd1"], sem["rstd2"], sem["rstd3"]]
        rstd_in = [sem["rstd_in0"], sem["rstd_in1"], sem["rstd_in2"], sem["rstd_in3"]]
        xn_s = [sem["xn0"], sem["xn1"], sem["xn2"], sem["xn3"]]
        xnT_ps = [sem["xnT_ps0"], sem["xnT_ps1"], sem["xnT_ps2"], sem["xnT_ps3"]]
        xnT_s = [sem["xnT0"], sem["xnT1"], sem["xnT2"], sem["xnT3"]]
        h_s = [sem["h0"], sem["h1"], sem["h2"], sem["h3"]]
        block = ctx.enter_context(nc.Block())

        def plain(eng):
            eng.nop(nofuse=True)


        @block.sync
        def _(sp):
            sp.dma_start(tokc[:], tok_in).then_inc(sem["tok_consts"], 16)
            for u in range(2):
                sp.dma_start(x_sb[:, u, :], x_in[u]).then_inc(load_x[u], 16)
            with sp.Fori(1, NP) as i:
                for u in range(2):
                    before = (i - 1) * 2 + u
                    sp.wait_ge(sem["xg_ready"], before + 1)
                    plain(sp)
                    sp.wait_ge(sem["ssq_ready"], GI * (before + 1))
                    plain(sp)
                    sp.dma_start(x_sb[:, u, :], x_in[i * 2 + u]).then_inc(load_x[u], 16)
            for q in range(4):
                sp.wait_ge(rel2_out[q], 16 * (NTOK // 4))
            sp.wait_ge(sem["rel3_out"], 16 * GI)
            sp.dma_start(big[:], moe_in).then_inc(sem["moe_weights"], 16)
            for u in range(2):
                sp.dma_start(rel_t[u][0], rel2[u]).then_inc(load_rel[u], 16)
                sp.dma_start(rel_t[u][1], rel3[u]).then_inc(load_rel[u], 16)
            with sp.Fori(1, NP) as i:
                for u in range(2):
                    sp.wait_ge(sem["biased2"], 2 * ((i - 1) * 2 + u + 1))
                    plain(sp)
                    sp.dma_start(rel_t[u][0], rel2[i * 2 + u]).then_inc(load_rel[u], 16)
                    sp.dma_start(rel_t[u][1], rel3[i * 2 + u]).then_inc(load_rel[u], 16)
            with sp.Fori(0, NP) as i:
                for u in range(2):
                    t = i * 2 + u
                    sp.wait_ge(sem["moe_acc"], t + 1)
                    plain(sp)
                    sp.dma_start(out[t], hres[:, t, :]).then_inc(stored_out[u], 16)
            for u in range(2):
                sp.wait_ge(stored_out[u], NP * 16)

        @block.tensor
        def _(pe):
            def transpose_norm(k, i, u, src, at):
                pe.wait_ge(xn_s[k], at + 1)
                for c in range(2):
                    last = nc.tensor.transpose(bank(u, 1)[0:HC, c * TT:(c + 1) * TT],
                                               src[:, u, c * HC:(c + 1) * HC], ident[0:TT, 0:TT])
                last.then_inc(xnT_ps[k], 1)

            def project_tokens(dst, lhs, weights, inc):
                for c in range(2):
                    rows = HC + c
                    last = nc.tensor.matmul(dst, lhs[0:rows, c, :], weights[0:rows, c, :],
                                            start=(c == 0), stop=(c == 1))
                if inc is not None:
                    last.then_inc(inc, 1)

            def project_features(dst, weights, lo, n, rhs):
                for c in range(2):
                    rows = HC + c
                    last = nc.tensor.matmul(dst, weights[0:rows, c, lo:lo + n], rhs[0:rows, c, :],
                                            start=(c == 0), stop=(c == 1))
                return last

            def v_tokens(u, weights):
                project_tokens(bank(u, 1)[0:TT, 0:C], xnT[:, u], weights, sem["v_tok_ps"])

            def v_thirds(u, at):
                pe.wait_ge(sem["v_tok_ready"], at + 1)
                for b in range(GI):
                    dst = bank(u, b // 2)[0:TT, (b % 2) * 256:(b % 2) * 256 + C]
                    last = nc.tensor.matmul(dst, tokw("select_image")[0:TT, b * TT:(b + 1) * TT], v_sb[:, u, :],
                                            start=True, stop=True)
                last.then_inc(sem["v_ps"], 1)

            def attention_scores(u, at):
                pe.wait_ge(sem["qz_ready"], at + 1)
                pe.wait_ge(sem["kblk_ready"], at + 1)
                s_out = bank(u, 3)[0:TT, 0:H * NTOK].rearrange("p (h g j) -> p h g j", h=3, g=4)
                for c in range(2):
                    for b in range(GI):
                        rhs = kblk[:, u, c, :, b * NTOK:(b + 1) * NTOK]\
                            .rearrange("p (h g) j -> p h g j", h=3)
                        last = nc.tensor.matmul(s_out[:, :, 2 * c:2 * c + 2, :],
                                                qz[:, u, c, b * TT:(b + 1) * TT], rhs,
                                                start=(b == 0), stop=(b == GI - 1))
                last.then_inc(sem["s_ps"], 1)

            def attention_turn(u, at):
                pe.wait_ge(sem["pn_ready"], at + 1)
                for g in range(4):
                    last = nc.tensor.transpose(bank(u, 2)[0:TT, g * TT:(g + 1) * TT],
                                               sc[:, u, g * TT:(g + 1) * TT], ident[0:TT, 0:TT])
                last.then_inc(sem["pt_ps"], 1)

            def attention_values(u, at):
                pe.wait_ge(sem["pT_ready"], at + 1)
                pe.wait_ge(sem["vblk_ready"], GI * (at + 1))
                vflat = vblk[:, u].rearrange("p m x -> p (m x)")
                for c in range(2):
                    for b in range(GI):
                        dst = bank(u, 3)[0:HC, c * TT + b * NTOK:c * TT + (b + 1) * NTOK]
                        for gg in range(2):
                            first = (b * 2 + c) * 288 + gg * HC
                            last = nc.tensor.matmul(dst, vflat[:, first:first + HC],
                                                    pT[:, u, 2 * c + gg, b * NTOK:(b + 1) * NTOK],
                                                    start=(gg == 0), stop=(gg == 1))
                last.then_inc(sem["o_ps"], 1)

            def attention_out(u, at, weights):
                pe.wait_ge(sem["oT_ready"], at + 1)
                project_tokens(bank(u, 0)[0:TT, 0:C], oT[:, u], weights, sem["y_ps"])

            pe.wait_ge(sem["tok_consts"], 16)
            pe.wait_ge(sem["w_consts"], 16)
            pe.wait_ge(sem["ones_ready"], 1)
            with pe.Fori(0, NP) as i:
                for u in range(2):
                    t = i * 2 + u
                    pe.wait_ge(sem["xg_ready"], t + 1)
                    for k in range(KF):
                        nc.tensor.matmul(bank(u, 0)[0:TT, 0:C], xg[:, u, k * TT:(k + 1) * TT],
                                         wt[:, k, :], start=(k == 0), stop=(k == KF - 1))
                    pe.wait_ge(sem["ssq_ready"], GI * (t + 1))
                    nc.tensor.matmul(bank(u, 0)[0:TT, C:C + GI], tokw("pixel_mean"), ssq[:, u, :],
                                     start=True, stop=True)\
                        .then_inc(sem["tok_ps"], 1)
                for u in range(2):
                    t = i * 2 + u
                    pe.wait_ge(sem["ysum_ready"], t + 1)
                    nc.tensor.matmul(bank(u, 0)[0:TT, C:C + 1], tokw("same_image")[0:TT, :],
                                     c1(u, 2), start=True, stop=True).then_inc(sem["rms2_ps"], 1)
                for u in range(2):
                    transpose_norm(0, i, u, xn, i * 2 + u)
                for u in range(2):
                    t = i * 2 + u
                    pe.wait_ge(xnT_s[0], t + 1)
                    v_tokens(u, slab("v0"))
                    for n, name in enumerate(("q0", "k0")):
                        for m in range(2):
                            last = project_features(bank(u, 2 + n)[0:HC, m * TT:(m + 1) * TT],
                                                    slab(name), m * HC, HC, xnT[:, u])
                    last.then_inc(sem["qk_ps"], 1)
                for u in range(2):
                    v_thirds(u, i * 2 + u)
                for u in range(2):
                    attention_scores(u, i * 2 + u)
                for u in range(2):
                    attention_turn(u, i * 2 + u)
                for u in range(2):
                    attention_values(u, i * 2 + u)
                for u in range(2):
                    attention_out(u, i * 2 + u, slab("o0"))
                for u in range(2):
                    transpose_norm(1, i, u, xn, i * 2 + u)
                for u in range(2):
                    t = i * 2 + u
                    pe.wait_ge(xnT_s[1], t + 1)
                    project_features(bank(u, 1)[0:GH, 0:TT], slab("fg1"), 0, GH, xnT[:, u])
                    project_tokens(bank(u, 0)[0:TT, 0:C], xnT[:, u], slab("fv"), sem["f_vg_ps"])
                    for n, name in enumerate(("fq", "fk")):
                        project_features(bank(u, 2)[0:128, 2 * n * TT:(2 * n + 1) * TT], slab(name), 0, 128,
                                         xnT[:, u])
                        last = project_features(bank(u, 2)[0:HD0, (2 * n + 1) * TT:(2 * n + 2) * TT],
                                                slab(name), 128, HD0, xnT[:, u])
                    last.then_inc(sem["f_qk_ps"], 1)
                for u in range(2):
                    t = i * 2 + u
                    pe.wait_ge(sem["f_g1_ready"], t + 1)
                    nc.tensor.matmul(bank(u, 1)[0:TT, 0:E0], f_g1T[:, u, :], w("fg2")[0:GH + 1, :],
                                     start=True, stop=True).then_inc(sem["f_gate_ps"], 1)
                for u in range(2):
                    t = i * 2 + u
                    pe.wait_ge(sem["f_copied"], t + 1)
                    pe.wait_ge(sem["f_conv_ready"], t + 1)
                    nc.tensor.matmul(bank(u, 3)[0:TT, 0:TT], f_qc[:, u, 1, :], f_k[:, u, :],
                                     start=True, stop=True)
                    nc.tensor.matmul(bank(u, 3)[0:TT, TT:2 * TT], f_q1[:, u, :], f_k[:, u, :],
                                     start=True, stop=True)
                    nc.tensor.matmul(bank(u, 3)[0:TT, 2 * TT:3 * TT], f_q2[:, u, :], f_k2[:, u, :],
                                     start=True, stop=True).then_inc(sem["f_s_ps"], 1)
                for u in range(2):
                    t = i * 2 + u
                    pe.wait_ge(sem["f_pn"], t + 1)
                    for e in range(E0):
                        last = nc.tensor.transpose(bank(u, 2)[0:TT, e * TT:(e + 1) * TT],
                                                   pr[:, u, e * TT:(e + 1) * TT], ident[0:TT, 0:TT])
                    last.then_inc(sem["f_pt_ps"], 1)
                for u in range(2):
                    t = i * 2 + u
                    pe.wait_ge(sem["f_pT"], t + 1)
                    pe.wait_ge(sem["f_v_copied"], t + 1)
                    for e in range(E0):
                        lo = HD0 * (e % 2)
                        last = nc.tensor.matmul(bank(u, 3)[lo:lo + HD0, (e // 2) * TT:(e // 2 + 1) * TT],
                                                f_v[:, u, e * HD0:(e + 1) * HD0], pT[:, u, e, :],
                                                start=True, stop=True)
                    last.then_inc(sem["f_o_ps"], 1)
                for u in range(2):
                    t = i * 2 + u
                    pe.wait_ge(sem["f_oT"], t + 1)
                    nc.tensor.matmul(bank(u, 0)[0:TT, 0:C], f_oT[:, u, 0, :], w("fpa"), start=True, stop=False)
                    nc.tensor.matmul(bank(u, 0)[0:TT, 0:C], f_oT[0:HD0 + 1, u, 1, :], w("fpb")[0:HD0 + 1, :],
                                     start=False, stop=True).then_inc(sem["f_y_ps"], 1)
                for u in range(2):
                    transpose_norm(2, i, u, xn, i * 2 + u)
                for u in range(2):
                    t = i * 2 + u
                    pe.wait_ge(xnT_s[2], t + 1)
                    for n, name in enumerate(("q1", "k1")):
                        for m in range(2):
                            last = project_features(bank(u, 3 - n)[0:HC, m * TT:(m + 1) * TT],
                                                    slab(name), m * HC, HC, xnT[:, u])
                    last.then_inc(sem["l1_qk_ps"], 1)

            for n, (name, table) in enumerate((("pk", "relrevT"), ("pq", "relT"))):
                for m in range(2):
                    last = project_features(bank(0, 0)[0:HC, (2 * n + m) * REL:(2 * n + m + 1) * REL],
                                            slab(name), m * HC, HC, slab(table))
            last.then_inc(sem["relT_ps"], 1)
            pe.wait_ge(sem["pkblk_ready"], 2)
            pe.wait_ge(sem["l1_q_stored"], NT)
            pe.wait_ge(sem["l1_k_stored"], NT)
            for j in range(NTOK):
                if j >= 2:
                    pe.wait_ge(sem["rel2_copied"], j - 1)
                dst = bank(0, 2 + j % 2)[0:BP, 0:H * NTOK].rearrange("p (h g j) -> p h g j", h=3, g=4)
                for c in range(2):
                    rhs = pkblk[:, c, :, NTOK - 1 - j:2 * NTOK - 1 - j].rearrange("p (h g) j -> p h g j", h=3)
                    last = nc.tensor.matmul(dst[:, :, 2 * c:2 * c + 2, :], qT_all[0:HC, c, j::NTOK], rhs,
                                            start=True, stop=True)
                last.then_inc(sem["rel2_ps"], 1)
                if j >= 2:
                    pe.wait_ge(sem["rel3_copied"], j - 1)
                pe.wait_ge(sem["pq_win_ready"], j + 1)
                for g in range(4):
                    c = g // 2
                    last = nc.tensor.matmul(bank(1, j % 2)[0:TT, g * BP:(g + 1) * BP], pq_win[j % 2][:, g, :],
                                            kT_all[:, c, j::NTOK], start=True, stop=True)
                last.then_inc(sem["rel3_ps"], 1)
            pe.wait_ge(sem["rel2_copied"], NTOK)
            pe.wait_ge(sem["rel3_copied"], NTOK)

            with pe.Fori(0, NP) as i:
                for u in range(2):
                    transpose_norm(3, i, u, xn, 2 * (i * 2) + u)
                for u in range(2):
                    t = i * 2 + u
                    pe.wait_ge(xnT_s[3], 2 * (i * 2) + u + 1)
                    v_tokens(u, slab("v1"))
                for u in range(2):
                    v_thirds(u, NT + i * 2 + u)
                for u in range(2):
                    attention_scores(u, NT + i * 2 + u)
                for u in range(2):
                    attention_turn(u, NT + i * 2 + u)
                for u in range(2):
                    attention_values(u, NT + i * 2 + u)
                for u in range(2):
                    attention_out(u, NT + i * 2 + u, slab("o1"))
                for u in range(2):
                    transpose_norm(3, i, u, xn, 2 * (i * 2) + 2 + u)
                for u in range(2):
                    t = i * 2 + u
                    pe.wait_ge(xnT_s[3], 2 * (i * 2) + 2 + u + 1)
                    project_tokens(bank(u, 0)[0:TT, 0:NE], xnT[:, u], slab("gate"), sem["gate_ps"])

            pe.wait_ge(sem["moe_weights"], 16)
            pe.wait_ge(sem["xn3T_stored"], NT)
            pe.wait_ge(sem["glog"], NT)
            with pe.Fori(0, NP) as i:
                for e in range(NE):
                    for u in range(2):
                        at = (i * NE + e) * 2 + u
                        rhs = qT_all[:, :, bass.ds((i * 2 + u) * TT, TT)]
                        for k in range(KH):
                            dst = bank(u, k // 3)[:, (k % 3) * TT:(k % 3 + 1) * TT]
                            last = project_features(dst, w1[:, e], k * 128, 128, rhs)
                        last.then_inc(sem["hid_ps"], 1)
                    for u in range(2):
                        at = (i * NE + e) * 2 + u
                        pe.wait_ge(sem["hid_ready"], at + 1)
                        pe.wait_ge(sem["moe_sum"], at + 1)
                        for k in range(KH):
                            last = nc.tensor.matmul(bank(u, 2)[0:TT, 0:C], hid[:, u, k * TT:(k + 1) * TT],
                                                    w2[:, e, k, :], start=(k == 0), stop=(k == KH - 1))
                        last.then_inc(sem["moe_ps"], 1)

        @block.vector
        def _(dve):
            V = nc.vector

            def normalise(k, u, at, src):
                st = col[0:TT, u, 16:22]
                mv = col[0:TT, u, 24:26]
                plain(dve)
                V.bn_stats(st, src).then_inc(stats[k], 1)
                dve.wait_ge(stats[k], at + 1)
                plain(dve)
                V.bn_aggr(mv, st).then_inc(mean[k], 1)

            def normalise_end(k, u, at, src):
                dve.wait_ge(rstd[k], at + 1)
                V.tensor_scalar(xn[:, u, :], src, col[0:TT, u, 24:25], col[0:TT, u, 28:29],
                                ALU.subtract, ALU.mult).then_inc(xn_s[k], 1)

            def v_spread(u, at):
                dve.wait_ge(sem["v_ps"], at + 1)
                m = w("third_mask")[0:TT, :].unsqueeze(1).unsqueeze(3).broadcast_to([TT, 4, 3, D])
                for b in range(GI):
                    src = bank(u, b // 2)[0:TT, (b % 2) * 256:(b % 2) * 256 + C]\
                        .rearrange("p (g h d) -> p g h d", g=4, h=3)
                    dst = vblk[:, u, 4 * b:4 * b + 4, 0:48].rearrange("p g (h d) -> p g h d", h=3)
                    V.tensor_tensor(dst, src, m, ALU.mult).then_inc(sem["vblk_ready"], 1)

            def softmax_max(u, at, src_sem, src_at, bmax, cent):
                s3 = sc[:, u, :].rearrange("p (s j) -> p s j", s=H)
                dve.wait_ge(src_sem, src_at)
                V.tensor_reduce(col[0:TT, u, 32:32 + H], s3, AX, ALU.max).then_inc(bmax, 1)
                dve.wait_ge(bmax, at + 1)
                V.tensor_tensor(s3, s3, col[0:TT, u, 32:32 + H].unsqueeze(2).broadcast_to([TT, H, NTOK]),
                                ALU.subtract).then_inc(cent, 1)

            def softmax_end(u, at):
                p3 = pr[:, u, :].rearrange("p (s j) -> p s j", s=H)
                dve.wait_ge(sem["exped"], at + 1)
                V.tensor_reduce(col[0:TT, u, 44:44 + H], p3, AX, ALU.add).then_inc(sem["row_sum"], 1)
                dve.wait_ge(sem["row_sum"], at + 1)
                V.reciprocal(col[0:TT, u, 44:44 + H], col[0:TT, u, 44:44 + H]).then_inc(sem["row_inv"], 1)
                dve.wait_ge(sem["row_inv"], at + 1)
                V.tensor_tensor(sc[:, u, :].rearrange("p (g h j) -> p h g j", g=4, h=3),
                                pr[:, u, :].rearrange("p (h g j) -> p h g j", g=4, h=3),
                                col[0:TT, u, 44:44 + H].rearrange("p (h g) -> p h g", g=4).unsqueeze(3)
                                .broadcast_to([TT, 3, 4, NTOK]), ALU.mult).then_inc(sem["pn_ready"], 1)

            V.memset(qz[:], 0.0)
            V.memset(vblk[:], 0.0).then_inc(sem["moe_sum"], 2)
            V.memset(f_q0[:], 0.0)
            V.memset(f_qc[HD0:128], 0.0)
            V.memset(f_q1[0:HD0], 0.0)
            V.memset(f_q2[HD0:128], 0.0)
            V.memset(f_k2[HD0:128], 0.0)
            V.memset(xnT[HC:HC + 1], 1.0)
            V.memset(oT[HC:HC + 1], 1.0)
            V.memset(f_g1T[GH:GH + 1], 1.0)
            V.memset(f_oT[HD0:HD0 + 1, :, 1, :], 1.0)
            V.memset(qT_all[HC:HC + 1], 1.0).then_inc(sem["ones_ready"], 1)
            dve.wait_ge(sem["tok_consts"], 16)
            dve.wait_ge(sem["w_consts"], 16)
            for c in range(2):
                V.tensor_scalar(head_scaled[:, c, :], w("head_mask")[0:HC, :], w("head_scale")[0:HC, c:c + 1],
                                None, ALU.mult).then_inc(sem["masks_ready"], 1)
            for e in range(E0 - 1):
                V.tensor_copy(f_mask[:, e, :], w("causal")[0:TT, :]).then_inc(sem["masks_ready"], 1)
            V.tensor_tensor(f_mask[:, E0 - 1, :], w("causal")[0:TT, :], w("pos")[0:TT, :], ALU.add)\
                .then_inc(sem["masks_ready"], 1)
            dve.wait_ge(sem["masks_ready"], 5)
            dve.wait_ge(sem["ones_ready"], 1)

            g1 = tokw("g1").rearrange("p (k n) -> p k n", k=KF).unsqueeze(2).broadcast_to([128, KF, GI, NTOK])
            with dve.Fori(0, NP) as i:
                for u in range(2):
                    t = i * 2 + u
                    dve.wait_ge(load_x[u], (i + 1) * 16)
                    V.tensor_tensor(xg[:, u, :].rearrange("p (k b n) -> p k b n", k=KF, b=GI),
                                    x_sb[:, u, :].rearrange("p (k b n) -> p k b n", k=KF, b=GI),
                                    g1, ALU.mult).then_inc(sem["xg_ready"], 1)
                for u in range(2):
                    t = i * 2 + u
                    dve.wait_ge(sem["tok_ps"], t + 1)
                    V.scalar_tensor_tensor(out=col[0:TT, u, 8:8 + GI], in0=bank(u, 0)[0:TT, C:C + GI],
                                           scalar=TOK_EPS, in1=w("third_mask")[0:TT, :],
                                           op0=ALU.add, op1=ALU.mult, accum_out=c1(u, 0))\
                        .then_inc(sem["rms1_in"], 1)
                for u in range(2):
                    t = i * 2 + u
                    dve.wait_ge(sem["rms1"], t + 1)
                    V.scalar_tensor_tensor(out=y_sb[:, u, :], in0=bank(u, 0)[0:TT, 0:C], scalar=c1(u, 1),
                                           in1=tokw("tok_b")[0:TT, :], op0=ALU.mult, op1=ALU.add)\
                        .then_inc(sem["y_ready"], 1)
                for u in range(2):
                    t = i * 2 + u
                    dve.wait_ge(sem["rms2_ps"], t + 1)
                    V.tensor_scalar(c1(u, 3), bank(u, 0)[0:TT, C:C + 1], TOK_EPS, None, ALU.add)\
                        .then_inc(sem["rms2_in"], 1)
                for u in range(2):
                    t = i * 2 + u
                    dve.wait_ge(sem["rms2"], t + 1)
                    V.scalar_tensor_tensor(out=hres[:, t, :], in0=y_sb[:, u, :], scalar=c1(u, 4),
                                           in1=tokw("g2")[0:TT, :], op0=ALU.mult, op1=ALU.mult)\
                        .then_inc(sem["h0"], 1)
                    dve.wait_ge(sem["h0"], t + 1)
                    normalise(0, u, t, hres[:, t, :])
                for u in range(2):
                    t = i * 2 + u
                    normalise_end(0, u, t, hres[:, t, :])
                for u in range(2):
                    t = i * 2 + u
                    dve.wait_ge(sem["qk_ps"], t + 1)
                    k_src = bank(u, 3)[0:HC, 0:2 * TT].rearrange("p (c t) -> p c t", c=2)
                    for c in range(2):
                        last = V.tensor_tensor(kblk[:, u, c], k_src[:, c].unsqueeze(1).broadcast_to([HC, 6, TT]),
                                               head_scaled[:, c].unsqueeze(2).broadcast_to([HC, 6, TT]), ALU.mult)
                    last.then_inc(sem["kblk_ready"], 1)
                    v_spread(u, t)
                for u in range(2):
                    t = i * 2 + u
                    dve.wait_ge(sem["s_ps"], t + 1)
                    V.tensor_tensor(sc[:, u, :].rearrange("p (s j) -> p s j", s=H),
                                    bank(u, 3)[0:TT, 0:H * NTOK].rearrange("p (s j) -> p s j", s=H),
                                    w("diag_mask")[0:TT, :].unsqueeze(1).broadcast_to([TT, H, NTOK]), ALU.add)\
                        .then_inc(sem["biased"], 1)
                    softmax_max(u, t, sem["biased"], t + 1, sem["row_max"], sem["centred"])
                for u in range(2):
                    softmax_end(u, i * 2 + u)
                for u in range(2):
                    t = i * 2 + u
                    dve.wait_ge(sem["y_ps"], t + 1)
                    V.tensor_tensor(hres[:, t, :], bank(u, 0)[0:TT, 0:C], hres[:, t, :], ALU.add)\
                        .then_inc(sem["h1"], 1)
                    dve.wait_ge(sem["h1"], t + 1)
                    normalise(1, u, t, hres[:, t, :])
                for u in range(2):
                    t = i * 2 + u
                    normalise_end(1, u, t, hres[:, t, :])
                for u in range(2):
                    t = i * 2 + u
                    dve.wait_ge(sem["f_q1_ready"], t + 1)
                    qa, qb = (f_qc[0:HD0, u, s, :].rearrange("p (b n) -> p b n", b=GI) for s in range(2))
                    cv = w("conv")[0:HD0]
                    V.tensor_scalar(qa, f_q0[:, u, :, 0:NTOK], cv[:, 0:1], cv[:, 3:4], ALU.mult, ALU.add)\
                        .then_inc(sem["f_conv0"], 1)
                    dve.wait_ge(sem["f_conv0"], t + 1)
                    V.scalar_tensor_tensor(out=qb, in0=f_q0[:, u, :, 1:NTOK + 1], scalar=cv[:, 1:2], in1=qa,
                                           op0=ALU.mult, op1=ALU.add).then_inc(sem["f_conv1"], 1)
                    dve.wait_ge(sem["f_conv1"], t + 1)
                    V.scalar_tensor_tensor(out=qb, in0=f_q0[:, u, :, 2:NTOK + 2], scalar=cv[:, 2:3], in1=qb,
                                           op0=ALU.mult, op1=ALU.add).then_inc(sem["f_conv_ready"], 1)
                    dve.wait_ge(sem["f_vg_ps"], t + 1)
                    V.tensor_copy(f_v[:, u, :], bank(u, 0)[0:TT, 0:C]).then_inc(sem["f_v_copied"], 1)
                for u in range(2):
                    t = i * 2 + u
                    s3 = sc[:, u, 0:E0 * TT].rearrange("p (e j) -> p e j", e=E0)
                    mx = col[0:TT, u, 32:32 + E0]
                    dve.wait_ge(sem["f_s_ps"], t + 1)
                    V.scalar_tensor_tensor(out=sc[:, u, 0:E0 * TT], in0=bank(u, 3)[0:TT, 0:E0 * TT],
                                           scalar=1.0 / HD0 ** 0.5,
                                           in1=f_mask[:].rearrange("p e j -> p (e j)"),
                                           op0=ALU.mult, op1=ALU.add).then_inc(sem["f_biased"], 1)
                    dve.wait_ge(sem["f_biased"], t + 1)
                    V.tensor_reduce(mx, s3, AX, ALU.max).then_inc(sem["f_max"], 1)
                    dve.wait_ge(sem["f_max"], t + 1)
                    V.tensor_tensor(s3, s3, mx.unsqueeze(2).broadcast_to([TT, E0, TT]), ALU.subtract)\
                        .then_inc(sem["f_centred"], 1)
                for u in range(2):
                    t = i * 2 + u
                    p3 = pr[:, u, 0:E0 * TT].rearrange("p (e j) -> p e j", e=E0)
                    den = col[0:TT, u, 44:44 + E0]
                    dve.wait_ge(sem["f_exped"], t + 1)
                    V.tensor_reduce(den, p3, AX, ALU.add).then_inc(sem["f_sum"], 1)
                    dve.wait_ge(sem["f_sum"], t + 1)
                    dve.wait_ge(sem["gwsum"], t + 1)
                    V.tensor_scalar(den, den, gs[:, u, 40:41], None, ALU.mult).then_inc(sem["f_den"], 1)
                    dve.wait_ge(sem["f_den"], t + 1)
                    V.reciprocal(den, den).then_inc(sem["f_deninv"], 1)
                    dve.wait_ge(sem["f_deninv"], t + 1)
                    V.tensor_tensor(den, den, gs[:, u, 36:36 + E0], ALU.mult).then_inc(sem["f_factor"], 1)
                    dve.wait_ge(sem["f_factor"], t + 1)
                    V.tensor_tensor(p3, p3, den.unsqueeze(2).broadcast_to([TT, E0, TT]), ALU.mult)\
                        .then_inc(sem["f_pn"], 1)
                for u in range(2):
                    t = i * 2 + u
                    dve.wait_ge(sem["f_y_ps"], t + 1)
                    V.tensor_tensor(hres[:, t, :], bank(u, 0)[0:TT, 0:C], hres[:, t, :], ALU.add)\
                        .then_inc(sem["h2"], 1)
                    dve.wait_ge(sem["h2"], t + 1)
                    normalise(2, u, t, hres[:, t, :])
                for u in range(2):
                    t = i * 2 + u
                    normalise_end(2, u, t, hres[:, t, :])
                for u in range(2):
                    t = i * 2 + u
                    dve.wait_ge(sem["l1_qk_ps"], t + 1)
                    V.tensor_copy(kT_all[:, :, bass.ds(t * TT, TT)],
                                  bank(u, 2)[0:HC, 0:2 * TT].rearrange("p (c t) -> p c t", c=2))\
                        .then_inc(sem["l1_k_stored"], 1)

            dve.wait_ge(sem["relT_ps"], 1)
            for n, dst in enumerate((pkblk, pqblk)):
                src = bank(0, 0)[0:HC, 2 * n * REL:2 * (n + 1) * REL].rearrange("p (c r) -> p c r", c=2)
                for c in range(2):
                    last = V.tensor_tensor(dst[:, c], src[:, c].unsqueeze(1).broadcast_to([HC, 6, REL]),
                                           w("head_mask")[0:HC].unsqueeze(2).broadcast_to([HC, 6, REL]), ALU.mult)
                last.then_inc(sem["pkblk_ready"], 1)
            for j in range(NTOK):
                dve.wait_ge(sem["rel3_ps"], j + 1)
                V.tensor_copy(rel3_sb[:, :, :, j].rearrange("p b g -> p g b"),
                              bank(1, j % 2)[0:TT, 0:4 * BP].rearrange("p (g b) -> p g b", g=4))\
                    .then_inc(sem["rel3_copied"], 1)

            with dve.Fori(0, NP) as i:
                for u in range(2):
                    t = i * 2 + u
                    normalise(3, u, 2 * (i * 2) + u, hres[:, t, :])
                for u in range(2):
                    t = i * 2 + u
                    normalise_end(3, u, 2 * (i * 2) + u, hres[:, t, :])
                for u in range(2):
                    t = i * 2 + u
                    for c in range(2):
                        last = V.tensor_tensor(
                            kblk[:, u, c],
                            kT_all[:, c, bass.ds(t * TT, TT)].unsqueeze(1).broadcast_to([HC, 6, TT]),
                            w("head_mask")[0:HC].unsqueeze(2).broadcast_to([HC, 6, TT]), ALU.mult)
                    last.then_inc(sem["kblk_ready"], 1)
                    v_spread(u, NT + t)
                for u in range(2):
                    t = i * 2 + u
                    dve.wait_ge(sem["s_ps"], NT + t + 1)
                    dve.wait_ge(load_rel[u], (i + 1) * 32)
                    V.tensor_tensor(sc[:, u, :], bank(u, 3)[0:TT, 0:H * NTOK], rel_t[u][0], ALU.add)\
                        .then_inc(sem["biased2"], 1)
                    dve.wait_ge(sem["biased2"], 2 * t + 1)
                    V.tensor_tensor(sc[:, u, :], sc[:, u, :], rel_t[u][1], ALU.add)\
                        .then_inc(sem["biased2"], 1)
                    softmax_max(u, NT + t, sem["biased2"], 2 * t + 2, sem["row_max"], sem["centred"])
                for u in range(2):
                    softmax_end(u, NT + i * 2 + u)
                for u in range(2):
                    t = i * 2 + u
                    dve.wait_ge(sem["y_ps"], NT + t + 1)
                    V.tensor_tensor(hres[:, t, :], bank(u, 0)[0:TT, 0:C], hres[:, t, :], ALU.add)\
                        .then_inc(sem["h3"], 1)
                    dve.wait_ge(sem["h3"], t + 1)
                    normalise(3, u, 2 * (i * 2) + 2 + u, hres[:, t, :])
                for u in range(2):
                    t = i * 2 + u
                    normalise_end(3, u, 2 * (i * 2) + 2 + u, hres[:, t, :])
                for u in range(2):
                    t = i * 2 + u
                    lg = gs[:, u, 0:NE]
                    dve.wait_ge(sem["gate_ps"], t + 1)
                    V.tensor_tensor(lg, bank(u, 0)[0:TT, 0:NE], w("center")[0:TT, :], ALU.subtract)\
                        .then_inc(sem["glog"], 1)
                    dve.wait_ge(sem["glog"], t + 1)
                    V.tensor_reduce(gs[:, u, 4:5], lg, AX, ALU.max).then_inc(sem["glmax"], 1)
                    dve.wait_ge(sem["glmax"], t + 1)
                    V.scalar_tensor_tensor(out=gs[:, u, 8:8 + NE], in0=lg, scalar=gs[:, u, 4:5],
                                           in1=w("rank_down")[0:TT, :], op0=ALU.is_ge, op1=ALU.mult)\
                        .then_inc(sem["glval"], 1)
                    dve.wait_ge(sem["glval"], t + 1)
                    V.tensor_reduce(gs[:, u, 5:6], gs[:, u, 8:8 + NE], AX, ALU.max).then_inc(sem["glvmax"], 1)
                    dve.wait_ge(sem["glvmax"], t + 1)
                    V.tensor_scalar(oh[:, t, :], gs[:, u, 8:8 + NE], gs[:, u, 5:6], None, ALU.is_equal)\
                        .then_inc(sem["onehot"], 1)
            dve.wait_ge(sem["onehot"], NT)
            with dve.Fori(0, NP) as i:
                for e in range(NE):
                    for u in range(2):
                        t = i * 2 + u
                        at = (i * NE + e) * 2 + u
                        dve.wait_ge(sem["moe_ps"], at + 1)
                        V.tensor_tensor(y_sb[:, u, :], bank(u, 2)[0:TT, 0:C],
                                        w("b2").rearrange("p (e n) -> p e n", e=NE)[0:TT, e, :], ALU.add)\
                            .then_inc(sem["moe_sum"], 1)
                        dve.wait_ge(sem["moe_sum"], at + 3)
                        V.scalar_tensor_tensor(out=hres[:, t, :], in0=y_sb[:, u, :],
                                               scalar=oh[:, t, e:e + 1], in1=hres[:, t, :],
                                               op0=ALU.mult, op1=ALU.add)\
                            .then_inc(sem["moe_acc"] if e == NE - 1 else sem["acc_first"], 1)
                        if e < NE - 1:
                            dve.wait_ge(sem["acc_first"], (i * (NE - 1) + e) * 2 + u + 1)

        @block.scalar
        def _(act):
            A = nc.scalar

            def copy_xnT(k, u, at):
                act.wait_ge(xnT_ps[k], at + 1)
                A.activation(xnT[0:HC, u], bank(u, 1)[0:HC, 0:2 * TT].rearrange("p (c t) -> p c t", c=2),
                             ACT.Copy).then_inc(xnT_s[k], 1)

            def copy_v(u, at):
                act.wait_ge(sem["v_tok_ps"], at + 1)
                A.activation(v_sb[:, u, :], bank(u, 1)[0:TT, 0:C], ACT.Copy).then_inc(sem["v_tok_ready"], 1)

            def diagonal(u, c=None):
                v = qz[:, u].rearrange("p c (b x) -> p c b x", b=GI)[:, :, :, 0:NTOK]
                return v if c is None else v[:, c]

            def attention_exp(u, at, scale):
                act.wait_ge(sem["centred"], at + 1)
                A.activation(pr[:, u, :], sc[:, u, :], ACT.Exp, scale=scale).then_inc(sem["exped"], 1)

            def attention_copies(at0):
                for u in range(2):
                    act.wait_ge(sem["pt_ps"], at0 + u + 1)
                    A.activation(pT[:, u], bank(u, 2)[0:TT, 0:4 * TT].rearrange("p (g t) -> p g t", g=4),
                                 ACT.Copy).then_inc(sem["pT_ready"], 1)
                for u in range(2):
                    act.wait_ge(sem["o_ps"], at0 + u + 1)
                    A.activation(oT[0:HC, u], bank(u, 3)[0:HC, 0:2 * TT].rearrange("p (c t) -> p c t", c=2),
                                 ACT.Copy).then_inc(sem["oT_ready"], 1)

            act.dma_start(wc[:], w_in).then_inc(sem["w_consts"], 16)
            act.wait_ge(sem["ones_ready"], 1)
            with act.Fori(0, NP) as i:
                for u in range(2):
                    t = i * 2 + u
                    act.wait_ge(load_x[u], (i + 1) * 16)
                    for b in range(GI):
                        src = x_sb[:, u, :].rearrange("p (k b n) -> p k b n", k=KF, b=GI)[:, :, b, :]
                        lost = (bank(u, 3)[:, 0:KF * NTOK], bank(u, 3)[:, 256:256 + KF * NTOK],
                                bank(u, 1)[:, 0:KF * NTOK])[b]
                        A.activation(lost.rearrange("p (k n) -> p k n", k=KF), src, ACT.Square,
                                     accum_out=ssq[:, u, b:b + 1]).then_inc(sem["ssq_ready"], 1)
                for u in range(2):
                    t = i * 2 + u
                    act.wait_ge(sem["y_ready"], t + 1)
                    A.activation(bank(u, 1)[0:TT, 0:C], y_sb[:, u, :], ACT.Square,
                                 accum_out=c1(u, 2)).then_inc(sem["ysum_ready"], 1)
                for u in range(2):
                    copy_xnT(0, u, i * 2 + u)
                for u in range(2):
                    copy_v(u, i * 2 + u)
                for u in range(2):
                    t = i * 2 + u
                    act.wait_ge(sem["qk_ps"], t + 1)
                    for c in range(2):
                        src = bank(u, 2)[0:HC, c * TT:(c + 1) * TT].rearrange("p (b n) -> p b n", b=GI)
                        last = A.activation(diagonal(u, c), src, ACT.Copy)
                    last.then_inc(sem["qz_ready"], 1)
                for u in range(2):
                    attention_exp(u, i * 2 + u, 1.0)
                attention_copies(i * 2)
                for u in range(2):
                    copy_xnT(1, u, i * 2 + u)
                for u in range(2):
                    t = i * 2 + u
                    act.wait_ge(sem["f_vg_ps"], t + 1)
                    A.activation(f_g1T[0:GH, u, :], bank(u, 1)[0:GH, 0:TT], ACT.Relu)\
                        .then_inc(sem["f_g1_ready"], 1)
                    act.wait_ge(sem["f_qk_ps"], t + 1)
                    A.activation(f_q0[:, u, :, 1:NTOK + 1],
                                 bank(u, 2)[0:HD0, 0:TT].rearrange("p (b n) -> p b n", b=GI), ACT.Copy)\
                        .then_inc(sem["f_q1_ready"], 1)
                    A.activation(f_q1[HD0:128, u, :], bank(u, 2)[HD0:128, 0:TT], ACT.Copy)
                    A.activation(f_q2[0:HD0, u, :], bank(u, 2)[0:HD0, TT:2 * TT], ACT.Copy)
                    A.activation(f_k[:, u, :], bank(u, 2)[:, 2 * TT:3 * TT], ACT.Copy)
                    A.activation(f_k2[0:HD0, u, :], bank(u, 2)[0:HD0, 3 * TT:4 * TT], ACT.Copy)\
                        .then_inc(sem["f_copied"], 1)
                for u in range(2):
                    t = i * 2 + u
                    act.wait_ge(sem["f_gate_ps"], t + 1)
                    A.activation(gs[:, u, 0:E0], bank(u, 1)[0:TT, 0:E0], ACT.Copy)\
                        .then_inc(sem["f_logits"], 1)
                for u in range(2):
                    t = i * 2 + u
                    act.wait_ge(sem["gcentred"], t + 1)
                    A.activation(gs[:, u, 8:8 + E0], gs[:, u, 8:8 + E0], ACT.Exp,
                                 accum_out=gs[:, u, 12:13]).then_inc(sem["gexp"], 1)
                for u in range(2):
                    t = i * 2 + u
                    act.wait_ge(sem["gprob"], t + 1)
                    A.activation(gs[:, u, 32:32 + E0], gs[:, u, 16:16 + E0], ACT.Exp).then_inc(sem["gexp2"], 1)
                for u in range(2):
                    t = i * 2 + u
                    act.wait_ge(sem["f_centred"], t + 1)
                    A.activation(pr[:, u, 0:E0 * TT], sc[:, u, 0:E0 * TT], ACT.Exp).then_inc(sem["f_exped"], 1)
                for u in range(2):
                    t = i * 2 + u
                    act.wait_ge(sem["f_pt_ps"], t + 1)
                    A.activation(pT[:, u, 0:E0], bank(u, 2)[0:TT, 0:E0 * TT].rearrange("p (e t) -> p e t", e=E0),
                                 ACT.Copy).then_inc(sem["f_pT"], 1)
                for u in range(2):
                    t = i * 2 + u
                    act.wait_ge(sem["f_o_ps"], t + 1)
                    A.activation(f_oT[:, u, 0, :], bank(u, 3)[:, 0:TT], ACT.Copy)
                    A.activation(f_oT[0:HD0, u, 1, :], bank(u, 3)[0:HD0, TT:2 * TT], ACT.Copy)\
                        .then_inc(sem["f_oT"], 1)
                for u in range(2):
                    copy_xnT(2, u, i * 2 + u)
                for u in range(2):
                    t = i * 2 + u
                    act.wait_ge(sem["l1_qk_ps"], t + 1)
                    plain(act)
                    A.activation(qT_all[0:HC, :, bass.ds(t * TT, TT)],
                                 bank(u, 3)[0:HC, 0:2 * TT].rearrange("p (c t) -> p c t", c=2), ACT.Copy)\
                        .then_inc(sem["l1_q_stored"], 1)
                act.wait_ge(sem["l1_q_stored"], i * 2 + 2)

            rel2_rows = rel2.rearrange("t (b i) s -> (t b) i s", b=GI)
            for j in range(NTOK):
                act.wait_ge(sem["rel2_ps"], j + 1)
                if j >= 4:
                    act.wait_ge(rel2_out[j % 4], 16 * (j // 4))
                A.activation(rel2_buf[j % 4], bank(0, 2 + j % 2)[0:BP, 0:H * NTOK], ACT.Copy)\
                    .then_inc(sem["rel2_copied"], 1)
                act.wait_ge(sem["rel2_copied"], j + 1)
                act.dma_start(rel2_rows[:, j, :], rel2_buf[j % 4]).then_inc(rel2_out[j % 4], 16)
            act.wait_ge(sem["rel3_copied"], NTOK)
            rel3_rows = rel3.rearrange("t (b i) (h s) -> h i (t b) s", b=GI, h=3)
            for h in range(GI):
                act.dma_start(rel3_rows[h], rel3_sb[h * NTOK:(h + 1) * NTOK].rearrange("p b g j -> p b (g j)"))\
                    .then_inc(sem["rel3_out"], 16)

            with act.Fori(0, NP) as i:
                for u in range(2):
                    copy_xnT(3, u, 2 * (i * 2) + u)
                for u in range(2):
                    copy_v(u, NT + i * 2 + u)
                for u in range(2):
                    t = i * 2 + u
                    for c in range(2):
                        src = qT_all[0:HC, c, bass.ds(t * TT, TT)].rearrange("p (b n) -> p b n", b=GI)
                        last = A.activation(diagonal(u, c), src, ACT.Copy)
                    last.then_inc(sem["qz_ready"], 1)
                for u in range(2):
                    attention_exp(u, NT + i * 2 + u, 1.0 / (3.0 * D) ** 0.5)
                attention_copies(NT + i * 2)
                for u in range(2):
                    copy_xnT(3, u, 2 * (i * 2) + 2 + u)
                for u in range(2):
                    t = i * 2 + u
                    act.wait_ge(sem["qz_ready"], NT + t + 1)
                    act.wait_ge(xnT_s[3], 2 * (i * 2) + 2 + u + 1)
                    plain(act)
                    A.activation(qT_all[0:HC, :, bass.ds(t * TT, TT)], xnT[0:HC, u], ACT.Copy)\
                        .then_inc(sem["xn3T_stored"], 1)
                act.wait_ge(sem["xn3T_stored"], i * 2 + 2)
            with act.Fori(0, NP) as i:
                for e in range(NE):
                    for u in range(2):
                        at = (i * NE + e) * 2 + u
                        act.wait_ge(sem["hid_ps"], at + 1)
                        for m in range(2):
                            last = A.activation(hid[:, u, m * 3 * TT:(m + 1) * 3 * TT],
                                                bank(u, m)[:, 0:3 * TT], ACT.Gelu)
                        last.then_inc(sem["hid_ready"], 1)

        @block.gpsimd
        def _(pool):
            G = nc.gpsimd

            def power(k, u, at):
                pool.wait_ge(mean[k], at + 1)
                plain(pool)
                G.tensor_scalar(col[0:TT, u, 27:28], col[0:TT, u, 25:26], LN_EPS, None, ALU.add)\
                    .then_inc(rstd_in[k], 1)
                pool.wait_ge(rstd_in[k], at + 1)
                G.tensor_tensor(col[0:TT, u, 28:29], col[0:TT, u, 27:28], mhalf[0:TT], ALU.pow)\
                    .then_inc(rstd[k], 1)

            G.memset(mone[:], -1.0)
            G.memset(mhalf[:], -0.5).then_inc(sem["mhalf_ready"], 1)
            pool.wait_ge(sem["mhalf_ready"], 1)
            pool.wait_ge(sem["w_consts"], 16)
            with pool.Fori(0, NP) as i:
                for u in range(2):
                    pool.wait_ge(sem["rms1_in"], i * 2 + u + 1)
                    G.tensor_tensor(c1(u, 1), c1(u, 0), mhalf[0:TT], ALU.pow).then_inc(sem["rms1"], 1)
                for u in range(2):
                    pool.wait_ge(sem["rms2_in"], i * 2 + u + 1)
                    G.tensor_tensor(c1(u, 4), c1(u, 3), mhalf[0:TT], ALU.pow).then_inc(sem["rms2"], 1)
                for u in range(2):
                    power(0, u, i * 2 + u)
                for u in range(2):
                    power(1, u, i * 2 + u)
                for u in range(2):
                    t = i * 2 + u
                    lg, z = gs[:, u, 0:E0], gs[:, u, 8:8 + E0]
                    pool.wait_ge(sem["f_logits"], t + 1)
                    plain(pool)
                    G.tensor_scalar(gs[:, u, 5:6], gs[:, u, 0:1], gs[:, u, 1:2], gs[:, u, 2:3],
                                    ALU.max, ALU.max).then_inc(sem["gmax"], 1)
                    pool.wait_ge(sem["gmax"], t + 1)
                    plain(pool)
                    G.tensor_scalar(z, lg, gs[:, u, 5:6], None, ALU.subtract).then_inc(sem["gcentred"], 1)
                for u in range(2):
                    t = i * 2 + u
                    pool.wait_ge(sem["gexp"], t + 1)
                    G.tensor_tensor(gs[:, u, 13:14], gs[:, u, 12:13], mone[0:TT], ALU.pow).then_inc(sem["ginv"], 1)
                    pool.wait_ge(sem["ginv"], t + 1)
                    plain(pool)
                    G.tensor_scalar(gs[:, u, 16:16 + E0], gs[:, u, 8:8 + E0], gs[:, u, 13:14], None,
                                    ALU.mult).then_inc(sem["gprob"], 1)
                    pool.wait_ge(sem["gprob"], t + 1)
                    plain(pool)
                    G.tensor_scalar(gs[:, u, 21:22], gs[:, u, 16:17], gs[:, u, 17:18], gs[:, u, 18:19],
                                    ALU.min, ALU.min).then_inc(sem["gmin"], 1)
                    pool.wait_ge(sem["gmin"], t + 1)
                    plain(pool)
                    G.tensor_scalar(gs[:, u, 24:24 + E0], gs[:, u, 16:16 + E0], gs[:, u, 21:22], None,
                                    ALU.is_le).then_inc(sem["gle"], 1)
                    pool.wait_ge(sem["gle"], t + 1)
                    G.tensor_tensor(gs[:, u, 28:28 + E0], gs[:, u, 24:24 + E0], w("rank_up")[0:TT, :], ALU.mult)\
                        .then_inc(sem["gval"], 1)
                    pool.wait_ge(sem["gval"], t + 1)
                    plain(pool)
                    G.tensor_scalar(gs[:, u, 45:46], gs[:, u, 28:29], gs[:, u, 29:30], gs[:, u, 30:31],
                                    ALU.max, ALU.max).then_inc(sem["gvmax"], 1)
                    pool.wait_ge(sem["gvmax"], t + 1)
                    plain(pool)
                    G.tensor_scalar(gs[:, u, 48:48 + E0], gs[:, u, 28:28 + E0], gs[:, u, 45:46], None,
                                    ALU.is_lt).then_inc(sem["gkeep"], 1)
                    pool.wait_ge(sem["gkeep"], t + 1)
                    pool.wait_ge(sem["gexp2"], t + 1)
                    G.tensor_tensor(gs[:, u, 36:36 + E0], gs[:, u, 32:32 + E0], gs[:, u, 48:48 + E0], ALU.mult)\
                        .then_inc(sem["gkexp"], 1)
                    pool.wait_ge(sem["gkexp"], t + 1)
                    plain(pool)
                    G.tensor_scalar(gs[:, u, 40:41], gs[:, u, 36:37], gs[:, u, 37:38], gs[:, u, 38:39],
                                    ALU.add, ALU.add).then_inc(sem["gwsum"], 1)
                for u in range(2):
                    power(2, u, i * 2 + u)
            pool.wait_ge(sem["pkblk_ready"], 2)
            for j in range(NTOK):
                if j >= 2:
                    pool.wait_ge(sem["rel3_ps"], j - 1)
                for c in range(2):
                    src = pqblk[:, c, :, NTOK - 1 - j:2 * NTOK - 1 - j].rearrange("p (h g) i -> p g h i", h=3)
                    last = G.tensor_copy(
                        pq_win[j % 2][:, 2 * c:2 * c + 2, :].rearrange("p g (h i) -> p g h i", h=3), src)
                last.then_inc(sem["pq_win_ready"], 1)
            with pool.Fori(0, NP) as i:
                for u in range(2):
                    power(3, u, 2 * (i * 2) + u)
                for u in range(2):
                    power(3, u, 2 * (i * 2) + 2 + u)


_OUT_SHAPE = (NT, TT, C)


def _put(pack, at, name, a, rows=0):
    lo, n = at[name]
    a = np.asarray(a, np.float32).reshape(a.shape[0], -1)
    assert a.shape[1] == n, (name, a.shape, n)
    pack[rows:rows + a.shape[0], lo:lo + n] = a


def _slab(weights, bias):
    n = weights.shape[1]
    out = np.zeros((HC + 1, 2, n), np.float32)
    out[0:HC] = weights.reshape(2, HC, n).transpose(1, 0, 2)
    out[HC, 1] = bias
    return out


def layout(a):
    x = a["x"]
    hw = IMG // PS
    x = x.reshape(B, CH, hw, PS, hw, PS).transpose(0, 2, 4, 3, 5, 1).reshape(B, NTOK, FEAT)
    x = np.concatenate([x, np.zeros((BP - B, NTOK, FEAT), np.float32)])
    x = x.reshape(NT, TT, KF, 128).transpose(0, 3, 2, 1).reshape(NT, 128, KF * TT)

    rows = np.arange(TT)
    img, tok = rows // NTOK, rows % NTOK
    tok_pack = np.zeros((128, TOK_COLS), np.float32)
    _put(tok_pack, TOK_AT, "wt", a["L0_tok_W"].T.reshape(KF, 128, C).transpose(1, 0, 2))
    _put(tok_pack, TOK_AT, "g1", a["L0_tok_g1"].T.reshape(KF, 128, NTOK).transpose(1, 0, 2))
    _put(tok_pack, TOK_AT, "tok_b", np.broadcast_to(a["L0_tok_b"], (TT, C)))
    _put(tok_pack, TOK_AT, "g2", np.tile(a["L0_tok_g2"], (GI, 1)))
    _put(tok_pack, TOK_AT, "ident", np.eye(128))
    _put(tok_pack, TOK_AT, "same_image", (img[:, None] == img) / (NTOK * C))
    _put(tok_pack, TOK_AT, "pixel_mean", np.full((128, TT), 1.0 / (NTOK * FEAT)))

    select = (tok[:, None, None] == tok) & (img[:, None, None] == np.arange(GI)[:, None])
    _put(tok_pack, TOK_AT, "select_image", select)

    wp = np.zeros((128, W_COLS), np.float32)
    wq, bq = a["L0_attn_w_qkv"], a["L0_attn_b_qkv"]
    fq, fb = a["L0_ffn_Wqk"], a["L0_ffn_bqk"]
    slabs = {
        "q0": (wq[:, :C], bq[:C]), "k0": (wq[:, C:2 * C], bq[C:2 * C]), "v0": (wq[:, 2 * C:], bq[2 * C:]),
        "o0": (a["L0_attn_w_proj"], a["L0_attn_b_proj"]),
        "fq": (fq[:, :C], fb[:C]), "fk": (fq[:, C:], fb[C:]),
        "fv": (a["L0_ffn_Wv"].transpose(1, 0, 2).reshape(C, C), a["L0_ffn_bv"].reshape(C)),
        "fg1": (a["L0_ffn_Wg1"], a["L0_ffn_bg1"]),
        "q1": (a["L1_attn_Wq"], a["L1_attn_bq"]), "k1": (a["L1_attn_Wk"], a["L1_attn_bk"]),
        "v1": (a["L1_attn_Wv"], a["L1_attn_bv"]), "o1": (a["L1_attn_Wo"], a["L1_attn_bo"]),
        "pk": (a["L1_attn_Wpk"], a["L1_attn_bpk"]), "pq": (a["L1_attn_Wpq"], a["L1_attn_bpq"]),
        "gate": (a["L1_ffn_gate_w"], a["L1_ffn_gate_b"]),
    }
    for name, (weights, bias) in slabs.items():
        _put(wp, W_AT, name, _slab(weights, bias))
    _put(wp, W_AT, "fg2", np.concatenate([a["L0_ffn_Wg2"], a["L0_ffn_bg2"][None]]))
    _put(wp, W_AT, "fpa", a["L0_ffn_Wp"][:128])
    _put(wp, W_AT, "fpb", np.concatenate([a["L0_ffn_Wp"][128:], a["L0_ffn_bp"][None]]))
    _put(wp, W_AT, "center", np.broadcast_to(a["L1_ffn_gate_center"], (TT, NE)))
    middle = (a["L1_attn_rel_table"].shape[0] - 1) // 2
    table = a["L1_attn_rel_table"][middle - NTOK + 1:middle + NTOK]
    _put(wp, W_AT, "relT", _slab(table.T, np.ones(REL, np.float32)))
    _put(wp, W_AT, "relrevT", _slab(table[::-1].T, np.ones(REL, np.float32)))
    head = np.array([3 * g + h for h in range(3) for g in range(2)])
    _put(wp, W_AT, "head_mask", (np.arange(HC)[:, None] // D == head).astype(np.float32))
    _put(wp, W_AT, "head_scale", np.repeat(a["L0_attn_scale"], D).reshape(2, HC).T)
    _put(wp, W_AT, "third_mask", (img[:, None] == np.arange(GI)).astype(np.float32))
    _put(wp, W_AT, "diag_mask", np.where((tok[:, None] == np.arange(NTOK)) & (tok[:, None] >= 1), NEG, 0.0))
    _put(wp, W_AT, "causal", np.where((img[:, None] == img) & (tok[None] <= tok[:, None]), 0.0, NEG))
    _put(wp, W_AT, "pos", np.tile(a["L0_ffn_pos_bias"][:NTOK, :NTOK], (GI, GI)))
    _put(wp, W_AT, "rank_up", np.broadcast_to(np.arange(1, E0 + 1), (TT, E0)))
    _put(wp, W_AT, "rank_down", np.broadcast_to(np.arange(NE, 0, -1), (TT, NE)))
    _put(wp, W_AT, "conv", np.concatenate([a["L0_ffn_conv_w"][:, 0], a["L0_ffn_conv_b"][:, None]], 1))
    _put(wp, W_AT, "b2", np.broadcast_to(a["L1_ffn_b2"].reshape(1, NE * C), (TT, NE * C)))

    moe = np.zeros((128, BIG_COLS), np.float32)
    moe[:HC + 1, :2 * NE * HID] = np.stack([_slab(w1, b1) for w1, b1 in zip(a["L1_ffn_w1"], a["L1_ffn_b1"])],
                                           1).reshape(HC + 1, -1)
    moe[:, 2 * NE * HID:] = a["L1_ffn_w2"].reshape(NE, KH, 128, C).transpose(2, 0, 1, 3).reshape(128, -1)
    return {"x_in": np.ascontiguousarray(x), "tok_in": tok_pack, "w_in": wp, "moe_in": moe}


def program(nc, arrays):
    args = [nc.dram_tensor(n, v.shape, F32, kind="ExternalInput").ap() for n, v in arrays.items()]
    scratch = [nc.dram_tensor(n, (NT, TT, H * NTOK), F32).ap() for n in ("rel2_scratch", "rel3_scratch")]
    out = nc.dram_tensor("out", _OUT_SHAPE, F32, kind="ExternalOutput").ap()
    build(nc, *args, *scratch, out)


def kernel(**inputs):
    import concourse.bacc as bacc
    from concourse.bass_utils import run_bass_kernel_spmd

    arrays = layout({k: np.asarray(v) for k, v in inputs.items()})
    nc = bacc.Bacc("TRN2", target_bir_lowering=False, num_devices=1)
    program(nc, arrays)
    got = run_bass_kernel_spmd(nc, [arrays], core_ids=[0]).results[0]["out"]
    return got.reshape(BP, NTOK, C)[:B]
```

```python
from contextlib import ExitStack

import numpy as np

import concourse.bass as bass
from concourse import mybir

F32 = mybir.dt.float32
U32 = mybir.dt.uint32
ALU = mybir.AluOpType
ACT = mybir.ActivationFunctionType
AX = mybir.AxisListType.X

B, CH, IMG, PS = 64, 3, 96, 16
NTOK = (IMG // PS) ** 2
FEAT = CH * PS * PS
KF = FEAT // 128
C = 192
HC = C // 2
H, D = 12, 16
GI = 3
TT = GI * NTOK
NT = 2 * -(-B // (2 * GI))
BP = NT * GI
NP = NT // 2
TM = 128
NT_TOK = NT * TT
E0, HD0, GH = 3, 64, 32
NE, HID = 4, 768
KH = HID // 128
NM = (NT_TOK + NE * (TM - 1)) // TM
NOWHERE = float(2 ** 20)
assert NM == NT
REL = 2 * NTOK - 1
NEG = -1.0e30
TOK_EPS, LN_EPS = 1e-4, 1e-5

TOK_PACK = [("wt", KF * C), ("g1", KF * NTOK), ("tok_b", C), ("g2", C), ("ident", 128),
            ("same_image", TT), ("pixel_mean", TT),
            ("select_image", GI * TT)]
SLABS = ["o0", "fq", "fk", "fv", "q1", "k1", "v1", "o1", "pk", "pq"]
W_PACK = [("q0", 2 * C), ("k0", 2 * C), ("v0", 2 * C), ("head_mask", 6), ("head_scale", 2),
          ("third_mask", GI), ("diag_mask", NTOK), ("causal", TT), ("pos", TT)]
EARLY = len(W_PACK)
W_PACK += [(n, 2 * C) for n in SLABS] + [
    ("fg1", 2 * GH), ("fg2", E0), ("fpa", C), ("fpb", C), ("gate", 2 * NE), ("center", NE),
    ("relT", 2 * REL), ("relrevT", 2 * REL), ("rank_up", E0),
    ("rank_down", NE), ("conv", 4), ("b2", NE * C),
    ("before", TT), ("token_id", NT), ("tile_at", NM), ("tile_no", NM), ("row_no", TM)]
BIG_COLS = 2 * NE * HID + NE * KH * C


def columns(pack):
    at, out = 0, {}
    for name, n in pack:
        out[name] = (at, n)
        at += n
    return out, at


TOK_AT, TOK_COLS = columns(TOK_PACK)
W_AT, W_COLS = columns(W_PACK)


def build(nc, x_in, tok_in, w_in, moe_in, rel2, rel3, xn_rows, h_rows, out):
    ctx = ExitStack()
    with ctx:
        def sb(name, shape, dtype=F32):
            return ctx.enter_context(nc.sbuf_tensor(name, shape, dtype))

        names = """tok_consts w_consts w_late moe_weights load_x0 load_x1 xg_ready ssq_ready tok_ps
            rms1_in rms1 y_ready ysum_ready rms2_ps rms2_in rms2 masks_ready ones_ready fills_ready
            stats0 stats1 stats2 stats3 stats4 mean0 mean1 mean2 mean3 mean4
            rstd_in0 rstd_in1 rstd_in2 rstd_in3 rstd_in4 rstd0 rstd1 rstd2 rstd3 rstd4
            xn0 xn1 xn2 xn3 xn4 xnT_ps0 xnT_ps1 xnT_ps2 xnT_ps3 xnT_ps4 xnT0 xnT1 xnT2 xnT3 xnT4
            h0 h1 h2 h3 vq_ps k_ps v_copied qz_ready kblk_ready v_ps vblk_ready s_ps biased biased2
            row_max centred exped row_sum pn_ready pt_ps pT_ready o_ps oT_ready y_ps
            f_qk_ps f_vg_ps f_copied f_v_copied f_g1_ready f_conv_step f_conv_ready f_q0_ready
            f_gate_ps f_logits f_s_ps f_biased f_max f_centred f_exped f_sum f_factor f_pn f_pt_ps
            f_pT f_o_ps f_oT f_y_ps gate_step gcentred gexp gexp2
            gwsum f_den f_deninv l1_q_ps l1_k_ps l1_q_stored l1_k_stored
            relT_ps pkblk_ready pq_win_ready rel2_ps rel2_copied rel2_out0 rel2_out1 rel2_out2 rel2_out3
            rel3_ps rel3_copied rel3_first rel3_out terms_added load_rel0 load_rel1
            gate_ps choice_step onehot xn_stored h_stored
            rank_ps sort_step perm_ready ids_ps ids_ready rows_clear
            idx_x_ready idx_h_ready got_x0 got_x1 got_h0 got_h1 x_turned_ps x_turned
            hid_ps hid_ready hidT_ps hidT_ready moe_ps moe_y moe_sum put0 put1""".split()
        sem = {n: ctx.enter_context(nc.semaphore(n)) for n in names}

        tokc = sb("tokc", [128, TOK_COLS])
        wc = sb("wc", [128, W_COLS])
        big = sb("big", [128, BIG_COLS])

        def tokw(name):
            a, n = TOK_AT[name]
            return tokc[:, a:a + n]

        def w(name):
            a, n = W_AT[name]
            return wc[:, a:a + n]

        def slab(name):
            return w(name).rearrange("p (c n) -> p c n", c=2)

        x_sb = sb("x_sb", [128, 2, KF * TT])
        xg = sb("xg", [128, 2, KF * TT])
        ssq = sb("ssq", [128, 2, GI])
        y_sb = sb("y_sb", [TT, 2, C])
        col = sb("col", [128, 2, 96])
        xn_a = sb("xn_a", [TT, 2, C])
        xnT_a = sb("xnT_a", [HC + 1, 2, 2, TT])
        qz = sb("qz", [HC, 2, 2, GI * (TT + NTOK)])
        kblk = sb("kblk", [HC, 2, 2, 6, TT])
        vblk = sb("vblk", [TT, 2, 12, 96])
        sc_a = sb("sc_a", [TT, 2, H * NTOK])
        pr_a = sb("pr_a", [TT, 2, H * NTOK])
        xn_b = sb("xn_b", [TT, 2, C])
        xnT_b = sb("xnT_b", [HC + 1, 2, 2, TT])
        sc = sb("sc", [TT, 2, H * NTOK])
        pr = sb("pr", [TT, 2, H * NTOK])
        pT = sb("pT", [TT, 2, E0, TT])
        pz = sb("pz", [TT, 2, GI * (4 * TT + NTOK)])
        oT = sb("oT", [HC + 1, 2, 2, TT])
        gs = sb("gs", [TT, 2, 64])
        head_scaled = sb("head_scaled", [HC, 2, 6])
        hres = sb("hres", [TT, NT, C])
        qT_all = sb("qT_all", [128, 2, NT * TT])
        kT_all = sb("kT_all", [128, 2, NT * TT])
        oh = sb("oh", [TT, NT, NE])
        ids = sb("ids", [128, NM], U32)
        tile_expert = sb("tile_expert", [1, NM], U32)
        idx_x = sb("idx_x", [128, 2], U32)
        idx_h = sb("idx_h", [128, 2], U32)
        mhalf = sb("mhalf", [128, 1])
        mone = sb("mone", [128, 1])
        ones = sb("ones", [128, TT])

        free_at = [0]

        def in_big(rows, *shape):
            n = 1
            for d in shape:
                n *= d
            v = big[0:rows, free_at[0]:free_at[0] + n]
            free_at[0] += n
            if len(shape) == 2:
                return v.rearrange("p (a b) -> p a b", a=shape[0])
            if len(shape) == 3:
                return v.rearrange("p (a b c) -> p a b c", a=shape[0], b=shape[1])
            return v

        squares = in_big(128, 2, GI, KF * NTOK)
        y_squares = in_big(TT, 2, C)
        f_mask = in_big(TT, E0, TT)
        f_q0 = in_big(HD0, 2, GI * (NTOK + 2))
        f_qc = in_big(128, 2, 2, TT)
        f_q1 = in_big(128, 2, TT)
        f_q2 = in_big(128, 2, TT)
        f_k = in_big(128, 2, TT)
        f_k2 = in_big(128, 2, TT)
        f_v = in_big(TT, 2, C)
        f_g1T = in_big(GH + 1, 2, TT)
        f_oT = in_big(128, 2, 2, TT)
        n_rel3 = BP * 4 * NTOK
        rel3_sb = big[0:TT, 0:n_rel3].rearrange("p (b g j) -> p b g j", b=BP, g=4)
        pkblk = big[0:HC, n_rel3:n_rel3 + 12 * REL].rearrange("p (c s r) -> p c s r", c=2, s=6)
        w1 = big[:, 0:2 * NE * HID].rearrange("p (e c n) -> p e c n", e=NE, c=2)
        w2 = big[:, 2 * NE * HID:].rearrange("p (e k n) -> p e k n", e=NE, k=KH)

        pqblk = xg[0:HC].rearrange("p u n -> p (u n)")[:, 0:12 * REL].rearrange("p (c s r) -> p c s r", c=2, s=6)
        rel2_buf = [sc[0:BP, 0, :], sc[0:BP, 1, :], pr[0:BP, 0, :], pr[0:BP, 1, :]]
        rel_t = [[buf[0:TT, u, 0:H * NTOK] for buf in (xg, x_sb)] for u in range(2)]
        v_sb = y_sb
        pq_win = [kblk[:, n, 0, 0:4, :] for n in range(2)]
        sort_at, moe_at = [0], [0]

        def view(flat, at, rows, *shape):
            n = 1
            for d in shape:
                n *= d
            v = flat[0:rows, at[0]:at[0] + n]
            at[0] += n
            assert at[0] <= 2 * NT_TOK
            if len(shape) == 2:
                return v.rearrange("p (a b) -> p a b", a=shape[0])
            if len(shape) == 3:
                return v.rearrange("p (a b c) -> p a b c", a=shape[0], b=shape[1])
            return v

        q_flat = qT_all.rearrange("p c t -> p (c t)")
        k_flat = kT_all.rearrange("p c t -> p (c t)")
        perm = view(q_flat, sort_at, TT, NT, TM)
        reached = view(q_flat, sort_at, TT, NT, NM + 1)
        tile_id = view(q_flat, sort_at, TT, NT, NM)
        cnt = view(q_flat, sort_at, TT, 2, NE * NT)
        place = view(q_flat, sort_at, TT, NE * NT)
        e_tiles = view(q_flat, sort_at, TT, NE)
        e_start = view(q_flat, sort_at, TT, NE)
        spot = view(q_flat, sort_at, TT, NT)
        spot_in = view(q_flat, sort_at, TT, NT)
        id_hole = view(q_flat, sort_at, 128, NM)
        mx = view(k_flat, moe_at, 128, 2, C)
        mh = view(k_flat, moe_at, 128, 2, C)
        my = view(k_flat, moe_at, 128, 2, C)
        mxT = view(k_flat, moe_at, HC + 1, 2, 2, TM)
        hid = view(k_flat, moe_at, 128, 2, HID)
        hidT = view(k_flat, moe_at, 128, 2, HID)
        ps = ctx.enter_context(nc.psum_tensor("ps", [128, 8, 512], F32))

        def bank(u, n):
            return ps[:, 4 * u + n, :]

        def c1(u, n, rows=TT):
            return col[0:rows, u, n:n + 1]

        wt = tokw("wt").rearrange("p (k n) -> p k n", k=KF)
        ident = tokw("ident")
        load_x = [sem["load_x0"], sem["load_x1"]]
        load_rel = [sem["load_rel0"], sem["load_rel1"]]
        got_x, got_h, put = ([sem["%s%d" % (n, u)] for u in range(2)] for n in ("got_x", "got_h", "put"))
        rel2_out = [sem["rel2_out%d" % q] for q in range(4)]
        stats, mean, rstd_in, rstd, xn_s, xnT_ps, xnT_s = (
            [sem["%s%d" % (n, k)] for k in range(5)]
            for n in ("stats", "mean", "rstd_in", "rstd", "xn", "xnT_ps", "xnT"))
        norm_at = [16, 64, 64, 16, 64]
        norm_out = [xn_a, xn_b, xn_b, xn_a, xn_b]
        norm_outT = [xnT_a, xnT_b, xnT_b, xnT_a, xnT_b]
        norm_bank = [1, 3, 3, 3, 1]
        block = ctx.enter_context(nc.Block())

        def plain(eng):
            eng.nop(nofuse=True)


        @block.sync
        def _(sp):
            sp.dma_start(tokc[:], tok_in).then_inc(sem["tok_consts"], 16)
            for u in range(2):
                sp.dma_start(x_sb[:, u, :], x_in[u]).then_inc(load_x[u], 16)
            with sp.Fori(1, NP) as i:
                for u in range(2):
                    before = (i - 1) * 2 + u
                    sp.wait_ge(sem["xg_ready"], before + 1)
                    plain(sp)
                    sp.wait_ge(sem["ssq_ready"], GI * (before + 1))
                    plain(sp)
                    sp.dma_start(x_sb[:, u, :], x_in[i * 2 + u]).then_inc(load_x[u], 16)
            for q in range(4):
                sp.wait_ge(rel2_out[q], 16 * (NTOK // 4))
            sp.wait_ge(sem["rel3_first"], 16 * GI)
            for u in range(2):
                sp.dma_start(rel_t[u][0], rel2[u]).then_inc(load_rel[u], 16)
                sp.dma_start(rel_t[u][1], rel3[u]).then_inc(load_rel[u], 16)
            sp.wait_ge(sem["rel3_out"], 16 * GI)
            sp.dma_start(big[:], moe_in).then_inc(sem["moe_weights"], 16)

            def load_terms(i):
                for u in range(2):
                    sp.wait_ge(sem["biased2"], (i - 1) * 2 + u + 1)
                    plain(sp)
                    sp.dma_start(rel_t[u][0], rel2[i * 2 + u]).then_inc(load_rel[u], 16)
                    sp.dma_start(rel_t[u][1], rel3[i * 2 + u]).then_inc(load_rel[u], 16)

            def store_rows(i):
                pair = bass.ds(i * 2, 2)
                sp.wait_ge(sem["h3"], i * 2 + 2)
                plain(sp)
                sp.dma_start(h_rows.rearrange("(t p) c -> p t c", p=TT)[:, pair, :], hres[:, pair, :])\
                    .then_inc(sem["h_stored"], 16)
                sp.wait_ge(xn_s[4], i * 2 + 2)
                plain(sp)
                sp.dma_start(xn_rows.rearrange("(t p) c -> p t c", p=TT)[:, pair, :], xn_b[:])\
                    .then_inc(sem["xn_stored"], 16)

            load_terms(1)
            load_terms(2)
            with sp.Fori(3, NP) as i:
                store_rows(i - 3)
                load_terms(i)
            store_rows(NP - 3)
            store_rows(NP - 2)
            store_rows(NP - 1)

        @block.tensor
        def _(pe):
            def project_tokens(dst, lhs, weights):
                for c in range(2):
                    rows = HC + c
                    last = nc.tensor.matmul(dst, lhs[0:rows, c, :], weights[0:rows, c, :],
                                            start=(c == 0), stop=(c == 1))
                return last

            def project_features(dst, weights, lo, n, rhs):
                for c in range(2):
                    rows = HC + c
                    last = nc.tensor.matmul(dst, weights[0:rows, c, lo:lo + n], rhs[0:rows, c, :],
                                            start=(c == 0), stop=(c == 1))
                return last

            def embed(i, u):
                t = i * 2 + u
                pe.wait_ge(sem["xg_ready"], t + 1)
                for k in range(KF):
                    nc.tensor.matmul(bank(u, 0)[0:TT, 0:C], xg[:, u, k * TT:(k + 1) * TT],
                                     wt[:, k, :], start=(k == 0), stop=(k == KF - 1))
                pe.wait_ge(sem["ssq_ready"], GI * (t + 1))
                nc.tensor.matmul(bank(u, 0)[0:TT, C:C + GI], tokw("pixel_mean"), ssq[:, u, :],
                                 start=True, stop=True).then_inc(sem["tok_ps"], 1)

            def embed_square(i):
                for u in range(2):
                    pe.wait_ge(sem["ysum_ready"], i * 2 + u + 1)
                    nc.tensor.matmul(bank(u, 0)[0:TT, C:C + 1], tokw("same_image")[0:TT, :],
                                     c1(u, 2), start=True, stop=True).then_inc(sem["rms2_ps"], 1)

            def transpose_norm(k, i):
                for u in range(2):
                    pe.wait_ge(xn_s[k], i * 2 + u + 1)
                    for c in range(2):
                        last = nc.tensor.transpose(bank(u, norm_bank[k])[0:HC, c * TT:(c + 1) * TT],
                                                   norm_out[k][:, u, c * HC:(c + 1) * HC], ident[0:TT, 0:TT])
                    last.then_inc(xnT_ps[k], 1)

            def front_qkv(i):
                for u in range(2):
                    pe.wait_ge(xnT_s[0], i * 2 + u + 1)
                    project_tokens(bank(u, 1)[0:TT, 256:256 + C], xnT_a[:, u], slab("v0"))
                    for m in range(2):
                        last = project_features(bank(u, 1)[0:HC, m * TT:(m + 1) * TT], slab("q0"), m * HC, HC,
                                                xnT_a[:, u])
                    last.then_inc(sem["vq_ps"], 1)
                    for m in range(2):
                        last = project_features(bank(u, 0)[0:HC, m * TT:(m + 1) * TT], slab("k0"), m * HC, HC,
                                                xnT_a[:, u])
                    last.then_inc(sem["k_ps"], 1)

            def front_v(i):
                for u in range(2):
                    pe.wait_ge(xnT_s[3], i * 2 + u + 1)
                    project_tokens(bank(u, 2)[0:TT, 0:C], xnT_a[:, u], slab("v1"))\
                        .then_inc(sem["vq_ps"], 1)

            def v_thirds(at0):
                for u in range(2):
                    pe.wait_ge(sem["v_copied"], at0 + u + 1)
                    pe.wait_ge(sem["qz_ready"], at0 + u + 1)
                    pe.wait_ge(sem["kblk_ready"], at0 + u + 1)
                    for b in range(GI):
                        dst = bank(u, b // 2)[0:TT, (b % 2) * 256:(b % 2) * 256 + C]
                        last = nc.tensor.matmul(dst, tokw("select_image")[0:TT, b * TT:(b + 1) * TT],
                                                v_sb[:, u, :], start=True, stop=True)
                    last.then_inc(sem["v_ps"], 1)

            def scores(at0):
                for u in range(2):
                    pe.wait_ge(sem["vblk_ready"], GI * (at0 + u + 1))
                    s_out = bank(u, 1)[0:TT, 0:H * NTOK].rearrange("p (h g j) -> p h g j", h=3, g=4)
                    for c in range(2):
                        for b in range(GI):
                            rhs = kblk[:, u, c, :, b * NTOK:(b + 1) * NTOK]\
                                .rearrange("p (h g) j -> p h g j", h=3)
                            last = nc.tensor.matmul(s_out[:, :, 2 * c:2 * c + 2, :],
                                                    qz[:, u, c, b * TT:(b + 1) * TT], rhs,
                                                    start=(b == 0), stop=(b == GI - 1))
                    last.then_inc(sem["s_ps"], 1)

            def turn(at0):
                for u in range(2):
                    pe.wait_ge(sem["pn_ready"], at0 + u + 1)
                    for g in range(4):
                        last = nc.tensor.transpose(bank(u, 2)[0:TT, g * TT:(g + 1) * TT],
                                                   sc[:, u, g * TT:(g + 1) * TT], ident[0:TT, 0:TT])
                    last.then_inc(sem["pt_ps"], 1)

            def values(at0):
                for u in range(2):
                    pe.wait_ge(sem["pT_ready"], at0 + u + 1)
                    vflat = vblk[:, u].rearrange("p m x -> p (m x)")
                    for c in range(2):
                        for n in range(2 * GI):
                            b, gg = n // 2, n % 2
                            first = (b * 4 + 2 * c + gg) * HC - gg * 48
                            at = (b * 4 + 2 * c + gg) * TT
                            last = nc.tensor.matmul(bank(u, 3)[0:HC, c * TT:(c + 1) * TT],
                                                    vflat[:, first:first + HC], pz[:, u, at:at + TT],
                                                    start=(n == 0), stop=(n == 2 * GI - 1))
                    last.then_inc(sem["o_ps"], 1)

            def project_out(at0, weights, n):
                for u in range(2):
                    pe.wait_ge(sem["oT_ready"], at0 + u + 1)
                    project_tokens(bank(u, n)[0:TT, 0:C], oT[:, u], weights).then_inc(sem["y_ps"], 1)

            def ffn_qkv(i):
                for u in range(2):
                    pe.wait_ge(xnT_s[1], i * 2 + u + 1)
                    project_features(bank(u, 2)[0:GH, 256:256 + TT], slab("fg1"), 0, GH, xnT_b[:, u])
                    project_tokens(bank(u, 2)[0:TT, 0:C], xnT_b[:, u], slab("fv")).then_inc(sem["f_vg_ps"], 1)
                    for n, name in enumerate(("fq", "fk")):
                        project_features(bank(u, 3)[0:128, 2 * n * TT:(2 * n + 1) * TT], slab(name), 0, 128,
                                         xnT_b[:, u])
                        last = project_features(bank(u, 3)[0:HD0, (2 * n + 1) * TT:(2 * n + 2) * TT],
                                                slab(name), 128, HD0, xnT_b[:, u])
                    last.then_inc(sem["f_qk_ps"], 1)

            def ffn_gate(i):
                for u in range(2):
                    pe.wait_ge(sem["f_g1_ready"], i * 2 + u + 1)
                    pe.wait_ge(sem["f_v_copied"], i * 2 + u + 1)
                    nc.tensor.matmul(bank(u, 2)[0:TT, 0:E0], f_g1T[:, u, :], w("fg2")[0:GH + 1, :],
                                     start=True, stop=True).then_inc(sem["f_gate_ps"], 1)

            def ffn_scores(i):
                for u in range(2):
                    pe.wait_ge(sem["f_copied"], i * 2 + u + 1)
                    pe.wait_ge(sem["f_conv_ready"], i * 2 + u + 1)
                    for e, (q, k) in enumerate(((f_qc[:, u, 1, :], f_k[:, u, :]), (f_q1[:, u, :], f_k[:, u, :]),
                                                (f_q2[:, u, :], f_k2[:, u, :]))):
                        last = nc.tensor.matmul(bank(u, 3)[0:TT, e * TT:(e + 1) * TT], q, k,
                                                start=True, stop=True)
                    last.then_inc(sem["f_s_ps"], 1)

            def ffn_turn(i):
                for u in range(2):
                    pe.wait_ge(sem["f_pn"], i * 2 + u + 1)
                    pe.wait_ge(sem["f_logits"], i * 2 + u + 1)
                    for e in range(E0):
                        last = nc.tensor.transpose(bank(u, 2)[0:TT, e * TT:(e + 1) * TT],
                                                   pr[:, u, e * TT:(e + 1) * TT], ident[0:TT, 0:TT])
                    last.then_inc(sem["f_pt_ps"], 1)

            def ffn_values(i):
                for u in range(2):
                    pe.wait_ge(sem["f_pT"], i * 2 + u + 1)
                    for e in range(E0):
                        lo = HD0 * (e % 2)
                        last = nc.tensor.matmul(bank(u, 3)[lo:lo + HD0, (e // 2) * TT:(e // 2 + 1) * TT],
                                                f_v[:, u, e * HD0:(e + 1) * HD0], pT[:, u, e, :],
                                                start=True, stop=True)
                    last.then_inc(sem["f_o_ps"], 1)

            def ffn_out(i):
                for u in range(2):
                    pe.wait_ge(sem["f_oT"], i * 2 + u + 1)
                    nc.tensor.matmul(bank(u, 2)[0:TT, 0:C], f_oT[:, u, 0, :], w("fpa"), start=True, stop=False)
                    nc.tensor.matmul(bank(u, 2)[0:TT, 0:C], f_oT[0:HD0 + 1, u, 1, :], w("fpb")[0:HD0 + 1, :],
                                     start=False, stop=True).then_inc(sem["f_y_ps"], 1)

            def next_qk(i):
                for u in range(2):
                    pe.wait_ge(xnT_s[2], i * 2 + u + 1)
                    for name, n, done in (("q1", 3, "l1_q_ps"), ("k1", 2, "l1_k_ps")):
                        for m in range(2):
                            last = project_features(bank(u, n)[0:HC, m * TT:(m + 1) * TT], slab(name), m * HC, HC,
                                                    xnT_b[:, u])
                        last.then_inc(sem[done], 1)

            def step(n, a, b, first=False):
                if b is not None:
                    if not first:
                        pe.wait_ge(sem["l1_k_stored"], b * 2)
                    turn(b * 2)
                    values(b * 2)
                    project_out(b * 2, slab("o0"), 2)
                if a is not None:
                    transpose_norm(0, a)
                    front_qkv(a)
                if b is not None:
                    transpose_norm(1, b)
                    ffn_qkv(b)
                    ffn_gate(b)
                if a is not None:
                    v_thirds(a * 2)
                if b is not None:
                    ffn_scores(b)
                if a is not None:
                    scores(a * 2)
                if n is not None:
                    embed(n, 0)
                if b is not None:
                    ffn_turn(b)
                    ffn_values(b)
                    ffn_out(b)
                if n is not None:
                    embed(n, 1)
                if b is not None:
                    transpose_norm(2, b)
                    next_qk(b)
                if n is not None:
                    embed_square(n)

            pe.wait_ge(sem["tok_consts"], 16)
            pe.wait_ge(sem["w_consts"], 16)
            pe.wait_ge(sem["ones_ready"], 1)
            step(0, None, None)
            step(1, 0, None)
            pe.wait_ge(sem["w_late"], 16)
            step(2, 1, 0, first=True)
            with pe.Fori(1, NP - 2) as i:
                step(i + 2, i + 1, i)
            step(None, NP - 1, NP - 2)
            step(None, None, NP - 1)

            for n, (name, table) in enumerate((("pk", "relrevT"), ("pq", "relT"))):
                for m in range(2):
                    last = project_features(bank(0, 0)[0:HC, (2 * n + m) * REL:(2 * n + m + 1) * REL],
                                            slab(name), m * HC, HC, slab(table))
            last.then_inc(sem["relT_ps"], 1)
            pe.wait_ge(sem["pkblk_ready"], 2)
            pe.wait_ge(sem["l1_q_stored"], NT)
            pe.wait_ge(sem["l1_k_stored"], NT)
            for j in range(NTOK):
                if j >= 2:
                    pe.wait_ge(sem["rel2_copied"], j - 1)
                dst = bank(0, 2 + j % 2)[0:BP, 0:H * NTOK].rearrange("p (h g j) -> p h g j", h=3, g=4)
                for c in range(2):
                    rhs = pkblk[:, c, :, NTOK - 1 - j:2 * NTOK - 1 - j].rearrange("p (h g) j -> p h g j", h=3)
                    last = nc.tensor.matmul(dst[:, :, 2 * c:2 * c + 2, :], qT_all[0:HC, c, j::NTOK], rhs,
                                            start=True, stop=True)
                last.then_inc(sem["rel2_ps"], 1)
                if j >= 2:
                    pe.wait_ge(sem["rel3_copied"], j - 1)
                pe.wait_ge(sem["pq_win_ready"], j + 1)
                for g in range(4):
                    c = g // 2
                    last = nc.tensor.matmul(bank(1, j % 2)[0:TT, g * BP:(g + 1) * BP], pq_win[j % 2][:, g, :],
                                            kT_all[0:HC, c, j::NTOK], start=True, stop=True)
                last.then_inc(sem["rel3_ps"], 1)
            pe.wait_ge(sem["rel2_copied"], NTOK)
            pe.wait_ge(sem["rel3_copied"], NTOK)

            def step1(n, a, b, c):
                if a is not None:
                    pe.wait_ge(sem["v_copied"], NT + a * 2 + 2)
                if b is not None:
                    turn(NT + b * 2)
                    values(NT + b * 2)
                if c is not None:
                    transpose_norm(4, c)
                    for u in range(2):
                        pe.wait_ge(xnT_s[4], c * 2 + u + 1)
                        project_tokens(bank(u, 2)[0:TT, 0:NE], xnT_b[:, u], slab("gate"))\
                            .then_inc(sem["gate_ps"], 1)
                if a is not None:
                    v_thirds(NT + a * 2)
                    scores(NT + a * 2)
                if b is not None:
                    project_out(NT + b * 2, slab("o1"), 0)
                if n is not None:
                    transpose_norm(3, n)
                    front_v(n)

            step1(0, None, None, None)
            step1(1, 0, None, None)
            step1(2, 1, 0, None)
            step1(3, 2, 1, 0)
            with pe.Fori(1, NP - 3) as i:
                step1(i + 3, i + 2, i + 1, i)
            step1(None, NP - 1, NP - 2, NP - 3)
            step1(None, None, NP - 1, NP - 2)
            step1(None, None, None, NP - 1)

            pe.wait_ge(sem["onehot"], NT)
            pe.wait_ge(sem["fills_ready"], 2)
            oh_all = oh.rearrange("p t e -> p (t e)")
            nc.tensor.matmul(bank(0, 0)[0:TT, 0:NT * NE], w("before")[0:TT, :], oh_all, start=True, stop=True)
            nc.tensor.matmul(bank(0, 1)[0:TT, 0:NT * NE], ones[0:TT, 0:TT], oh_all, start=True, stop=True)\
                .then_inc(sem["rank_ps"], 1)
            pe.wait_ge(sem["perm_ready"], 1)
            for t in range(NT):
                last = nc.tensor.matmul(bank(0, 2)[:, 0:NM], perm[:, t, :], tile_id[:, t, :],
                                        start=(t == 0), stop=(t == NT - 1))
            last.then_inc(sem["ids_ps"], 1)

            def expert_of(k):
                return pe.value_load(tile_expert[0:1, bass.ds(k, 1)], min_val=0, max_val=NE - 1)

            def turn_x(p, u, first=False):
                k = p * 2 + u
                pe.wait_ge(got_x[u], (p + 1) * 16)
                if not first:
                    pe.wait_ge(sem["hid_ready"], 2 * (k - 1))
                for c in range(2):
                    last = nc.tensor.transpose(bank(u, 1)[0:HC, c * TM:(c + 1) * TM],
                                               mx[:, u, c * HC:(c + 1) * HC], ident)
                last.then_inc(sem["x_turned_ps"], 1)

            def hidden(p, u, e, first=False):
                k = p * 2 + u
                pe.wait_ge(sem["x_turned"], k + 2)
                if not first:
                    pe.wait_ge(sem["moe_y"], k - 1)
                for half in range(2):
                    for c in range(2):
                        last = nc.tensor.matmul(bank(u, half)[:, 0:HID // 2], mxT[0:HC + c, u, c, :],
                                                w1[0:HC + c, bass.ds(e, 1), c, half * HID // 2:(half + 1) * HID // 2]
                                                .rearrange("p e n -> p (e n)"),
                                                start=(c == 0), stop=(c == 1))
                    last.then_inc(sem["hid_ps"], 1)

            def turn_hidden(p, u, first=False):
                k = p * 2 + u
                if not first:
                    pe.wait_ge(sem["hidT_ready"], 2 * (k - 1))
                for half in range(2):
                    pe.wait_ge(sem["hid_ready"], 2 * k + 1 + half)
                    for m in range(3):
                        at = (3 * half + m) * 128
                        last = nc.tensor.transpose(bank(u, 2 + half)[:, m * TM:(m + 1) * TM],
                                                   hid[:, u, at:at + 128], ident)
                    last.then_inc(sem["hidT_ps"], 1)

            def answer(p, u, e):
                k = p * 2 + u
                for m in range(KH):
                    if m % 3 == 0:
                        pe.wait_ge(sem["hidT_ready"], 2 * k + 1 + m // 3)
                    last = nc.tensor.matmul(bank(u, 0)[:, 0:C], hidT[:, u, m * TM:(m + 1) * TM],
                                            w2[:, bass.ds(e, 1), m, :].rearrange("p e n -> p (e n)"),
                                            start=(m == 0), stop=(m == KH - 1))
                last.then_inc(sem["moe_ps"], 1)

            def tiles(p, first=False):
                e0, e1, e2 = expert_of(p * 2), expert_of(p * 2 + 1), expert_of(p * 2 + 2)
                turn_hidden(p, 0, first)
                turn_x(p + 1, 0)
                hidden(p, 1, e1, first)
                answer(p, 0, e0)
                turn_hidden(p, 1, first)
                turn_x(p + 1, 1)
                hidden(p + 1, 0, e2)
                answer(p, 1, e1)

            pe.wait_ge(sem["moe_weights"], 16)
            turn_x(0, 0, True)
            turn_x(0, 1, True)
            pe.wait_ge(sem["ids_ready"], 2)
            hidden(0, 0, expert_of(0), True)
            tiles(0, True)
            with pe.Fori(1, NP - 1) as i:
                tiles(i)
            e0, e1 = expert_of(NM - 2), expert_of(NM - 1)
            turn_hidden(NP - 1, 0)
            hidden(NP - 1, 1, e1)
            answer(NP - 1, 0, e0)
            turn_hidden(NP - 1, 1)
            answer(NP - 1, 1, e1)

        @block.vector
        def _(dve):
            V = nc.vector

            def norm_stats(k, u, at, src):
                c0 = norm_at[k]
                plain(dve)
                V.bn_stats(col[0:TT, u, c0:c0 + 6], src).then_inc(stats[k], 1)
                dve.wait_ge(stats[k], at + 1)
                plain(dve)
                V.bn_aggr(col[0:TT, u, c0 + 8:c0 + 10], col[0:TT, u, c0:c0 + 6]).then_inc(mean[k], 1)

            def norm_apply(k, i, first=False):
                c0 = norm_at[k]
                for u in range(2):
                    t = i * 2 + u
                    dve.wait_ge(rstd[k], t + 1)
                    if k == 4 and not first:
                        dve.wait_ge(sem["xn_stored"], i * 16)
                    V.tensor_scalar(norm_out[k][:, u, :], hres[:, t, :], c1(u, c0 + 8), c1(u, c0 + 12),
                                    ALU.subtract, ALU.mult).then_inc(xn_s[k], 1)

            def add_residual(i, src_ps, src_at, h_sem, k, n=2):
                for u in range(2):
                    t = i * 2 + u
                    dve.wait_ge(src_ps, src_at + u + 1)
                    V.tensor_tensor(hres[:, t, :], bank(u, n)[0:TT, 0:C], hres[:, t, :], ALU.add)\
                        .then_inc(h_sem, 1)
                    dve.wait_ge(h_sem, t + 1)
                    norm_stats(k, u, t, hres[:, t, :])

            def v_spread(at0):
                m = w("third_mask")[0:TT, :].unsqueeze(1).unsqueeze(3).broadcast_to([TT, 4, 3, D])
                for u in range(2):
                    dve.wait_ge(sem["v_ps"], at0 + u + 1)
                    for b in range(GI):
                        src = bank(u, b // 2)[0:TT, (b % 2) * 256:(b % 2) * 256 + C]\
                            .rearrange("p (g h d) -> p g h d", g=4, h=3)
                        dst = vblk[:, u, 4 * b:4 * b + 4, 0:48].rearrange("p g (h d) -> p g h d", h=3)
                        V.tensor_tensor(dst, src, m, ALU.mult).then_inc(sem["vblk_ready"], 1)

            def centre(u, at, biased_sem, biased_at):
                s3 = sc_a[:, u, :].rearrange("p (s j) -> p s j", s=H)
                dve.wait_ge(biased_sem, biased_at)
                V.tensor_reduce(col[0:TT, u, 32:32 + H], s3, AX, ALU.max).then_inc(sem["row_max"], 1)
                dve.wait_ge(sem["row_max"], at + 1)
                V.tensor_tensor(s3, s3, col[0:TT, u, 32:32 + H].unsqueeze(2).broadcast_to([TT, H, NTOK]),
                                ALU.subtract).then_inc(sem["centred"], 1)

            def probabilities(at0):
                for u in range(2):
                    at = at0 + u
                    p3 = pr_a[:, u, :].rearrange("p (s j) -> p s j", s=H)
                    dve.wait_ge(sem["exped"], at + 1)
                    V.tensor_reduce(col[0:TT, u, 44:44 + H], p3, AX, ALU.add).then_inc(sem["row_sum"], 1)
                    dve.wait_ge(sem["row_sum"], 2 * at + 1)
                    V.reciprocal(col[0:TT, u, 44:44 + H], col[0:TT, u, 44:44 + H]).then_inc(sem["row_sum"], 1)
                    dve.wait_ge(sem["row_sum"], 2 * at + 2)
                    V.tensor_tensor(sc[:, u, :].rearrange("p (g h j) -> p h g j", g=4, h=3),
                                    pr_a[:, u, :].rearrange("p (h g j) -> p h g j", g=4, h=3),
                                    col[0:TT, u, 44:44 + H].rearrange("p (h g) -> p h g", g=4).unsqueeze(3)
                                    .broadcast_to([TT, 3, 4, NTOK]), ALU.mult).then_inc(sem["pn_ready"], 1)

            def spread_k(u, c, src, mask):
                return V.tensor_tensor(kblk[:, u, c], src.unsqueeze(1).broadcast_to([HC, 6, TT]),
                                       mask.unsqueeze(2).broadcast_to([HC, 6, TT]), ALU.mult)

            V.memset(f_q0[:], 0.0)
            V.memset(f_qc[HD0:128], 0.0)
            V.memset(f_q1[0:HD0], 0.0)
            V.memset(f_q2[HD0:128], 0.0)
            V.memset(f_k2[HD0:128], 0.0)
            V.memset(xnT_a[HC:HC + 1], 1.0)
            V.memset(xnT_b[HC:HC + 1], 1.0)
            V.memset(oT[HC:HC + 1], 1.0)
            V.memset(f_g1T[GH:GH + 1], 1.0)
            V.memset(f_oT[HD0:HD0 + 1, :, 1, :], 1.0)
            V.memset(qT_all[HC:HC + 1], 1.0).then_inc(sem["ones_ready"], 1)
            dve.wait_ge(sem["tok_consts"], 16)
            dve.wait_ge(sem["w_consts"], 16)
            for c in range(2):
                V.tensor_scalar(head_scaled[:, c, :], w("head_mask")[0:HC, :], w("head_scale")[0:HC, c:c + 1],
                                None, ALU.mult).then_inc(sem["masks_ready"], 1)
            for e in range(E0 - 1):
                V.tensor_copy(f_mask[:, e, :], w("causal")[0:TT, :]).then_inc(sem["masks_ready"], 1)
            V.tensor_tensor(f_mask[:, E0 - 1, :], w("causal")[0:TT, :], w("pos")[0:TT, :], ALU.add)\
                .then_inc(sem["masks_ready"], 1)
            dve.wait_ge(sem["masks_ready"], 5)
            dve.wait_ge(sem["ones_ready"], 1)

            g1 = tokw("g1").rearrange("p (k n) -> p k n", k=KF).unsqueeze(2).broadcast_to([128, KF, GI, NTOK])

            def weigh_pixels(i):
                for u in range(2):
                    dve.wait_ge(load_x[u], (i + 1) * 16)
                    V.tensor_tensor(xg[:, u, :].rearrange("p (k b n) -> p k b n", k=KF, b=GI),
                                    x_sb[:, u, :].rearrange("p (k b n) -> p k b n", k=KF, b=GI),
                                    g1, ALU.mult).then_inc(sem["xg_ready"], 1)

            def embed_scale(i):
                for u in range(2):
                    dve.wait_ge(sem["tok_ps"], i * 2 + u + 1)
                    V.scalar_tensor_tensor(out=col[0:TT, u, 8:8 + GI], in0=bank(u, 0)[0:TT, C:C + GI],
                                           scalar=TOK_EPS, in1=w("third_mask")[0:TT, :],
                                           op0=ALU.add, op1=ALU.mult, accum_out=c1(u, 0))\
                        .then_inc(sem["rms1_in"], 1)
                for u in range(2):
                    dve.wait_ge(sem["rms1"], i * 2 + u + 1)
                    V.scalar_tensor_tensor(out=y_sb[:, u, :], in0=bank(u, 0)[0:TT, 0:C], scalar=c1(u, 1),
                                           in1=tokw("tok_b")[0:TT, :], op0=ALU.mult, op1=ALU.add)\
                        .then_inc(sem["y_ready"], 1)

            def embed_norm(i):
                for u in range(2):
                    dve.wait_ge(sem["rms2_ps"], i * 2 + u + 1)
                    V.tensor_scalar(c1(u, 3), bank(u, 0)[0:TT, C:C + 1], TOK_EPS, None, ALU.add)\
                        .then_inc(sem["rms2_in"], 1)

            def embed_out(i):
                for u in range(2):
                    t = i * 2 + u
                    dve.wait_ge(sem["rms2"], t + 1)
                    V.scalar_tensor_tensor(out=hres[:, t, :], in0=y_sb[:, u, :], scalar=c1(u, 4),
                                           in1=tokw("g2")[0:TT, :], op0=ALU.mult, op1=ALU.mult)\
                        .then_inc(sem["h0"], 1)
                    dve.wait_ge(sem["h0"], t + 1)
                    norm_stats(0, u, t, hres[:, t, :])

            def spread_k0(i):
                for u in range(2):
                    dve.wait_ge(sem["k_ps"], i * 2 + u + 1)
                    k_src = bank(u, 0)[0:HC, 0:2 * TT].rearrange("p (c t) -> p c t", c=2)
                    for c in range(2):
                        last = spread_k(u, c, k_src[:, c], head_scaled[:, c])
                    last.then_inc(sem["kblk_ready"], 1)

            def mask_scores(i):
                for u in range(2):
                    t = i * 2 + u
                    dve.wait_ge(sem["s_ps"], t + 1)
                    V.tensor_tensor(sc_a[:, u, :].rearrange("p (s j) -> p s j", s=H),
                                    bank(u, 1)[0:TT, 0:H * NTOK].rearrange("p (s j) -> p s j", s=H),
                                    w("diag_mask")[0:TT, :].unsqueeze(1).broadcast_to([TT, H, NTOK]), ALU.add)\
                        .then_inc(sem["biased"], 1)
                    centre(u, t, sem["biased"], t + 1)

            def ffn_v_gate(i):
                for u in range(2):
                    dve.wait_ge(sem["f_vg_ps"], i * 2 + u + 1)
                    V.tensor_scalar(f_g1T[0:GH, u, :], bank(u, 2)[0:GH, 256:256 + TT], 0.0, None, ALU.max)\
                        .then_inc(sem["f_g1_ready"], 1)
                    V.tensor_copy(f_v[:, u, :], bank(u, 2)[0:TT, 0:C]).then_inc(sem["f_v_copied"], 1)

            def ffn_convolve(i):
                cv = w("conv")[0:HD0]
                for u in range(2):
                    t = i * 2 + u
                    q0 = f_q0[:, u, :].rearrange("p (b n) -> p b n", b=GI)
                    qa, qb = (f_qc[0:HD0, u, s, :].rearrange("p (b n) -> p b n", b=GI) for s in range(2))
                    dve.wait_ge(sem["f_q0_ready"], t + 1)
                    V.tensor_scalar(qa, q0[:, :, 0:NTOK], cv[:, 0:1], cv[:, 3:4], ALU.mult, ALU.add)\
                        .then_inc(sem["f_conv_step"], 1)
                    dve.wait_ge(sem["f_conv_step"], 2 * t + 1)
                    V.scalar_tensor_tensor(out=qb, in0=q0[:, :, 1:NTOK + 1], scalar=cv[:, 1:2], in1=qa,
                                           op0=ALU.mult, op1=ALU.add).then_inc(sem["f_conv_step"], 1)
                    dve.wait_ge(sem["f_conv_step"], 2 * t + 2)
                    V.scalar_tensor_tensor(out=qb, in0=q0[:, :, 2:NTOK + 2], scalar=cv[:, 2:3], in1=qb,
                                           op0=ALU.mult, op1=ALU.add).then_inc(sem["f_conv_ready"], 1)

            def ffn_centre(i):
                for u in range(2):
                    t = i * 2 + u
                    s3 = sc[:, u, 0:E0 * TT].rearrange("p (e j) -> p e j", e=E0)
                    mx = col[0:TT, u, 80:80 + E0]
                    dve.wait_ge(sem["f_s_ps"], t + 1)
                    V.scalar_tensor_tensor(out=sc[:, u, 0:E0 * TT], in0=bank(u, 3)[0:TT, 0:E0 * TT],
                                           scalar=1.0 / HD0 ** 0.5, in1=f_mask[:].rearrange("p e j -> p (e j)"),
                                           op0=ALU.mult, op1=ALU.add).then_inc(sem["f_biased"], 1)
                    dve.wait_ge(sem["f_biased"], t + 1)
                    V.tensor_reduce(mx, s3, AX, ALU.max).then_inc(sem["f_max"], 1)
                    dve.wait_ge(sem["f_max"], t + 1)
                    V.tensor_tensor(s3, s3, mx.unsqueeze(2).broadcast_to([TT, E0, TT]), ALU.subtract)\
                        .then_inc(sem["f_centred"], 1)

            def ffn_probabilities(i):
                for u in range(2):
                    t = i * 2 + u
                    p3 = pr[:, u, 0:E0 * TT].rearrange("p (e j) -> p e j", e=E0)
                    den = col[0:TT, u, 84:84 + E0]
                    dve.wait_ge(sem["f_exped"], t + 1)
                    V.tensor_reduce(den, p3, AX, ALU.add).then_inc(sem["f_sum"], 1)
                    dve.wait_ge(sem["f_sum"], t + 1)
                    dve.wait_ge(sem["gwsum"], t + 1)
                    V.tensor_scalar(den, den, gs[:, u, 40:41], None, ALU.mult).then_inc(sem["f_den"], 1)
                    dve.wait_ge(sem["f_den"], t + 1)
                    V.reciprocal(den, den).then_inc(sem["f_deninv"], 1)
                    dve.wait_ge(sem["f_deninv"], t + 1)
                    V.tensor_tensor(den, den, gs[:, u, 36:36 + E0], ALU.mult).then_inc(sem["f_factor"], 1)
                    dve.wait_ge(sem["f_factor"], t + 1)
                    V.tensor_tensor(p3, p3, den.unsqueeze(2).broadcast_to([TT, E0, TT]), ALU.mult)\
                        .then_inc(sem["f_pn"], 1)

            def keep_k(i):
                for u in range(2):
                    t = i * 2 + u
                    dve.wait_ge(sem["l1_k_ps"], t + 1)
                    V.tensor_copy(kT_all[0:HC, :, bass.ds(t * TT, TT)],
                                  bank(u, 2)[0:HC, 0:2 * TT].rearrange("p (c t) -> p c t", c=2))\
                        .then_inc(sem["l1_k_stored"], 1)

            def step(n, a, b):
                if a is not None:
                    embed_norm(a)
                    embed_out(a)
                    norm_apply(0, a)
                if b is not None:
                    add_residual(b, sem["y_ps"], b * 2, sem["h1"], 1)
                    norm_apply(1, b)
                if a is not None:
                    spread_k0(a)
                if b is not None:
                    ffn_v_gate(b)
                    ffn_convolve(b)
                if a is not None:
                    v_spread(a * 2)
                if b is not None:
                    ffn_centre(b)
                if n is not None:
                    weigh_pixels(n)
                if b is not None:
                    ffn_probabilities(b)
                if a is not None:
                    mask_scores(a)
                if b is not None:
                    add_residual(b, sem["f_y_ps"], b * 2, sem["h2"], 2)
                    norm_apply(2, b)
                if a is not None:
                    probabilities(a * 2)
                if n is not None:
                    embed_scale(n)
                if b is not None:
                    keep_k(b)

            step(0, None, None)
            dve.wait_ge(sem["fills_ready"], 5)
            dve.wait_ge(sem["w_late"], 16)
            step(1, 0, None)
            step(2, 1, 0)
            with dve.Fori(1, NP - 2) as i:
                step(i + 2, i + 1, i)
            step(None, NP - 1, NP - 2)
            step(None, None, NP - 1)

            dve.wait_ge(sem["relT_ps"], 1)
            for n, dst in enumerate((pkblk, pqblk)):
                src = bank(0, 0)[0:HC, 2 * n * REL:2 * (n + 1) * REL].rearrange("p (c r) -> p c r", c=2)
                for c in range(2):
                    last = V.tensor_tensor(dst[:, c], src[:, c].unsqueeze(1).broadcast_to([HC, 6, REL]),
                                           w("head_mask")[0:HC].unsqueeze(2).broadcast_to([HC, 6, REL]), ALU.mult)
                last.then_inc(sem["pkblk_ready"], 1)

            def window(j):
                for c in range(2):
                    src = pqblk[:, c, :, NTOK - 1 - j:2 * NTOK - 1 - j].rearrange("p (h g) i -> p g h i", h=3)
                    last = V.tensor_copy(
                        pq_win[j % 2][:, 2 * c:2 * c + 2, :].rearrange("p g (h i) -> p g h i", h=3), src)
                last.then_inc(sem["pq_win_ready"], 1)

            dve.wait_ge(sem["pkblk_ready"], 2)
            window(0)
            window(1)
            for j in range(NTOK):
                dve.wait_ge(sem["rel3_ps"], j + 1)
                if j + 2 < NTOK:
                    window(j + 2)
                V.tensor_copy(rel3_sb[:, :, :, j].rearrange("p b g -> p g b"),
                              bank(1, j % 2)[0:TT, 0:4 * BP].rearrange("p (g b) -> p g b", g=4))\
                    .then_inc(sem["rel3_copied"], 1)

            def bias_scores(i):
                for u in range(2):
                    t = i * 2 + u
                    dve.wait_ge(sem["s_ps"], NT + t + 1)
                    dve.wait_ge(sem["terms_added"], t + 1)
                    V.tensor_tensor(sc_a[:, u, :], bank(u, 1)[0:TT, 0:H * NTOK], rel_t[u][0], ALU.add)\
                        .then_inc(sem["biased2"], 1)
                    centre(u, NT + t, sem["biased2"], t + 1)

            def step1(n, a, b, c, first=False):
                if c is not None:
                    add_residual(c, sem["y_ps"], NT + c * 2, sem["h3"], 4, 0)
                    norm_apply(4, c, first)
                if n is not None:
                    for u in range(2):
                        norm_stats(3, u, n * 2 + u, hres[:, n * 2 + u, :])
                    if a is not None:
                        dve.wait_ge(xnT_ps[3], a * 2 + 2)
                    norm_apply(3, n)
                if c is not None:
                    choose_expert(c)
                if a is not None:
                    v_spread(NT + a * 2)
                    bias_scores(a)
                    probabilities(NT + a * 2)

            def choose_expert(i):
                for u in range(2):
                    t = i * 2 + u
                    lg = gs[:, u, 0:NE]
                    dve.wait_ge(sem["gate_ps"], t + 1)
                    V.tensor_tensor(lg, bank(u, 2)[0:TT, 0:NE], w("center")[0:TT, :], ALU.subtract)\
                        .then_inc(sem["choice_step"], 1)
                    dve.wait_ge(sem["choice_step"], 4 * t + 1)
                    V.tensor_reduce(gs[:, u, 4:5], lg, AX, ALU.max).then_inc(sem["choice_step"], 1)
                    dve.wait_ge(sem["choice_step"], 4 * t + 2)
                    V.scalar_tensor_tensor(out=gs[:, u, 8:8 + NE], in0=lg, scalar=gs[:, u, 4:5],
                                           in1=w("rank_down")[0:TT, :], op0=ALU.is_ge, op1=ALU.mult)\
                        .then_inc(sem["choice_step"], 1)
                    dve.wait_ge(sem["choice_step"], 4 * t + 3)
                    V.tensor_reduce(gs[:, u, 5:6], gs[:, u, 8:8 + NE], AX, ALU.max).then_inc(sem["choice_step"], 1)
                    dve.wait_ge(sem["choice_step"], 4 * t + 4)
                    V.tensor_scalar(oh[:, t, :], gs[:, u, 8:8 + NE], gs[:, u, 5:6], None, ALU.is_equal)\
                        .then_inc(sem["onehot"], 1)

            step1(0, None, None, None)
            step1(1, 0, None, None)
            step1(2, 1, 0, None)
            step1(3, 2, 1, 0, first=True)
            with dve.Fori(1, NP - 3) as i:
                step1(i + 3, i + 2, i + 1, i)
            step1(None, NP - 1, NP - 2, NP - 3)
            step1(None, None, NP - 1, NP - 2)
            step1(None, None, None, NP - 1)

            steps = [0]

            def sort_op(instruction):
                steps[0] += 1
                instruction.then_inc(sem["sort_step"], 1)
                dve.wait_ge(sem["sort_step"], steps[0])

            def by_expert(flat):
                return flat.rearrange("p (t e) -> p e t", e=NE)

            cnt3 = [cnt[:, n, :].rearrange("p (e t) -> p e t", e=NE) for n in range(2)]
            place3 = place.rearrange("p (e t) -> p e t", e=NE)
            dve.wait_ge(sem["rank_ps"], 1)
            sort_op(V.tensor_copy(cnt3[0], by_expert(bank(0, 1)[0:TT, 0:NT * NE])))
            sort_op(V.tensor_tensor(place3, by_expert(bank(0, 0)[0:TT, 0:NT * NE]), cnt3[0], ALU.subtract))
            shift, now = 1, 0
            while shift < NT:
                sort_op(V.tensor_copy(cnt3[1 - now][:, :, 0:shift], cnt3[now][:, :, 0:shift]))
                sort_op(V.tensor_tensor(cnt3[1 - now][:, :, shift:NT], cnt3[now][:, :, shift:NT],
                                        cnt3[now][:, :, 0:NT - shift], ALU.add))
                shift, now = 2 * shift, 1 - now
            sums = cnt3[now]
            sort_op(V.tensor_tensor(place3, place3, sums, ALU.add))
            tile_at = w("tile_at")[0:TT, :]
            sort_op(V.tensor_tensor(cnt3[1 - now], sums[:, :, NT - 1:NT].broadcast_to([TT, NE, NT]),
                                    tile_at.unsqueeze(1).broadcast_to([TT, NE, NM]), ALU.is_gt))
            sort_op(V.tensor_reduce(e_tiles, cnt3[1 - now], AX, ALU.add))
            sort_op(V.memset(e_start[:, 0:1], 0.0))
            for e in range(1, NE):
                sort_op(V.tensor_tensor(e_start[:, e:e + 1], e_start[:, e - 1:e], e_tiles[:, e - 1:e], ALU.add))
            tiles3 = cnt3[1 - now]
            sort_op(V.tensor_tensor(tiles3[:, 1:NE, :], w("tile_no")[0:TT, :].unsqueeze(1).broadcast_to([TT, NE - 1, NM]),
                                    e_start[:, 1:NE].unsqueeze(2).broadcast_to([TT, NE - 1, NM]), ALU.is_ge))
            sort_op(V.tensor_tensor(tiles3[:, 1, :], tiles3[:, 1, :], tiles3[:, 2, :], ALU.add))
            V.tensor_tensor(tile_expert[:], tiles3[0:1, 1, :], tiles3[0:1, 3, :], ALU.add).then_inc(sem["ids_ready"], 1)
            sort_op(V.scalar_tensor_tensor(out=place3, in0=e_start.unsqueeze(2).broadcast_to([TT, NE, NT]),
                                           scalar=float(TM), in1=place3, op0=ALU.mult, op1=ALU.add))
            sort_op(V.tensor_tensor(place3, place3, oh.rearrange("p t e -> p e t"), ALU.mult))
            sort_op(V.tensor_reduce(spot, place.rearrange("p (e t) -> p t e", e=NE), AX, ALU.add))
            sort_op(V.memset(reached[:, :, NM:NM + 1], 0.0))
            sort_op(V.tensor_tensor(reached[:, :, 0:NM], spot.unsqueeze(2).broadcast_to([TT, NT, NM]),
                                    tile_at.unsqueeze(1).broadcast_to([TT, NT, NM]), ALU.is_ge))
            sort_op(V.tensor_reduce(spot_in, reached[:, :, 0:NM], AX, ALU.add))
            sort_op(V.tensor_scalar(spot_in, spot_in, -float(TM), float(TM), ALU.mult, ALU.add))
            sort_op(V.tensor_tensor(spot_in, spot_in, spot, ALU.add))
            sort_op(V.tensor_tensor(tile_id, reached[:, :, 0:NM], reached[:, :, 1:NM + 1], ALU.subtract))
            sort_op(V.tensor_tensor(tile_id, tile_id, w("token_id")[0:TT, :].unsqueeze(2).broadcast_to([TT, NT, NM]),
                                    ALU.mult))
            V.tensor_tensor(perm, spot_in.unsqueeze(2).broadcast_to([TT, NT, TM]),
                            w("row_no")[0:TT, :].unsqueeze(1).broadcast_to([TT, NT, TM]), ALU.is_equal)\
                .then_inc(sem["perm_ready"], 1)
            dve.wait_ge(sem["ids_ps"], 1)
            sort_op(V.tensor_scalar(id_hole, bank(0, 2)[:, 0:NM], 0.0, NOWHERE, ALU.is_equal, ALU.mult))
            V.scalar_tensor_tensor(out=ids[:], in0=bank(0, 2)[:, 0:NM], scalar=-1.0, in1=id_hole,
                                   op0=ALU.add, op1=ALU.add).then_inc(sem["ids_ready"], 1)
            V.memset(mxT[HC:HC + 1], 1.0).then_inc(sem["x_turned"], 1)

            def copy_x(p, u, first=False):
                k = p * 2 + u
                dve.wait_ge(sem["x_turned_ps"], k + 1)
                if not first:
                    dve.wait_ge(sem["hid_ps"], 2 * (k - 1))
                V.tensor_copy(mxT[0:HC, u], bank(u, 1)[0:HC, 0:2 * TM].rearrange("p (c t) -> p c t", c=2))\
                    .then_inc(sem["x_turned"], 1)

            def copy_hidden(p, u, first=False):
                k = p * 2 + u
                if not first:
                    dve.wait_ge(sem["moe_ps"], k - 1)
                for half in range(2):
                    dve.wait_ge(sem["hidT_ps"], 2 * k + 1 + half)
                    V.tensor_copy(hidT[:, u, half * 3 * TM:(half + 1) * 3 * TM], bank(u, 2 + half)[:, 0:3 * TM])\
                        .then_inc(sem["hidT_ready"], 1)

            def add_bias(p, u, e, first=False):
                k = p * 2 + u
                dve.wait_ge(sem["moe_ps"], k + 1)
                if not first:
                    dve.wait_ge(put[u], p * 16)
                V.tensor_tensor(my[:, u, :], bank(u, 0)[:, 0:C],
                                w("b2").rearrange("p (e n) -> p e n", e=NE)[:, bass.ds(e, 1), :]
                                .rearrange("p e n -> p (e n)"), ALU.add).then_inc(sem["moe_y"], 1)
                dve.wait_ge(sem["moe_y"], k + 1)
                dve.wait_ge(got_h[u], (p + 1) * 16)
                V.tensor_tensor(my[:, u, :], my[:, u, :], mh[:, u, :], ALU.add).then_inc(sem["moe_sum"], 1)

            def expert_of(k):
                return dve.value_load(tile_expert[0:1, bass.ds(k, 1)], min_val=0, max_val=NE - 1)

            def tiles(p, first=False):
                e0, e1 = expert_of(p * 2), expert_of(p * 2 + 1)
                copy_hidden(p, 0, first)
                copy_x(p + 1, 0)
                add_bias(p, 0, e0, first)
                copy_hidden(p, 1, first)
                copy_x(p + 1, 1)
                add_bias(p, 1, e1, first)

            copy_x(0, 0, True)
            copy_x(0, 1, True)
            dve.wait_ge(sem["ids_ready"], 2)
            tiles(0, True)
            with dve.Fori(1, NP - 1) as i:
                tiles(i)
            for u in range(2):
                copy_hidden(NP - 1, u)
                add_bias(NP - 1, u, expert_of(NM - 2 + u))

        @block.scalar
        def _(act):
            A = nc.scalar

            def copy_norm(k, i):
                for u in range(2):
                    act.wait_ge(xnT_ps[k], i * 2 + u + 1)
                    A.activation(norm_outT[k][0:HC, u],
                                 bank(u, norm_bank[k])[0:HC, 0:2 * TT].rearrange("p (c t) -> p c t", c=2),
                                 ACT.Copy).then_inc(xnT_s[k], 1)

            def copy_v(at0, n, lo):
                for u in range(2):
                    act.wait_ge(sem["vq_ps"], at0 + u + 1)
                    A.activation(v_sb[:, u, :], bank(u, n)[0:TT, lo:lo + C], ACT.Copy).then_inc(sem["v_copied"], 1)

            def diagonal(u, c):
                return qz[:, u].rearrange("p c (b x) -> p c b x", b=GI)[:, c, :, 0:NTOK]

            def exponentials(at0, scale, slots=range(2)):
                for u in slots:
                    act.wait_ge(sem["centred"], at0 + u + 1)
                    A.activation(pr_a[:, u, :], sc_a[:, u, :], ACT.Exp, scale=scale).then_inc(sem["exped"], 1)

            def copy_turned(at0):
                for u in range(2):
                    act.wait_ge(sem["pt_ps"], at0 + u + 1)
                    own = pz[:, u].rearrange("p (b x) -> p b x", b=GI)[:, :, 0:4 * TT]\
                        .rearrange("p b (g t) -> p b g t", g=4)[:, :, :, 0:NTOK]
                    A.activation(own, bank(u, 2)[0:TT, 0:4 * TT].rearrange("p (g b n) -> p b g n", g=4, b=GI),
                                 ACT.Copy).then_inc(sem["pT_ready"], 1)

            def copy_values(at0):
                for u in range(2):
                    act.wait_ge(sem["o_ps"], at0 + u + 1)
                    A.activation(oT[0:HC, u], bank(u, 3)[0:HC, 0:2 * TT].rearrange("p (c t) -> p c t", c=2),
                                 ACT.Copy).then_inc(sem["oT_ready"], 1)

            def square_pixels(i):
                for u in range(2):
                    act.wait_ge(load_x[u], (i + 1) * 16)
                    for b in range(GI):
                        src = x_sb[:, u, :].rearrange("p (k b n) -> p k b n", k=KF, b=GI)[:, :, b, :]
                        A.activation(squares[:, u, b, :].rearrange("p (k n) -> p k n", k=KF), src, ACT.Square,
                                     accum_out=ssq[:, u, b:b + 1]).then_inc(sem["ssq_ready"], 1)

            def square_embedded(i):
                for u in range(2):
                    act.wait_ge(sem["y_ready"], i * 2 + u + 1)
                    A.activation(y_squares[:, u, :], y_sb[:, u, :], ACT.Square,
                                 accum_out=c1(u, 2)).then_inc(sem["ysum_ready"], 1)

            def copy_q(i):
                for u in range(2):
                    for c in range(2):
                        src = bank(u, 1)[0:HC, c * TT:(c + 1) * TT].rearrange("p (b n) -> p b n", b=GI)
                        last = A.activation(diagonal(u, c), src, ACT.Copy)
                    last.then_inc(sem["qz_ready"], 1)

            def ffn_copies(i):
                for u in range(2):
                    act.wait_ge(sem["f_qk_ps"], i * 2 + u + 1)
                    A.activation(f_q0[:, u, :].rearrange("p (b n) -> p b n", b=GI)[:, :, 1:NTOK + 1],
                                 bank(u, 3)[0:HD0, 0:TT].rearrange("p (b n) -> p b n", b=GI), ACT.Copy)\
                        .then_inc(sem["f_q0_ready"], 1)
                    A.activation(f_q1[HD0:128, u, :], bank(u, 3)[HD0:128, 0:TT], ACT.Copy)
                    A.activation(f_q2[0:HD0, u, :], bank(u, 3)[0:HD0, TT:2 * TT], ACT.Copy)
                    A.activation(f_k[:, u, :], bank(u, 3)[:, 2 * TT:3 * TT], ACT.Copy)
                    A.activation(f_k2[0:HD0, u, :], bank(u, 3)[0:HD0, 3 * TT:4 * TT], ACT.Copy)\
                        .then_inc(sem["f_copied"], 1)

            def ffn_gate_steps(i):
                for u in range(2):
                    act.wait_ge(sem["f_gate_ps"], i * 2 + u + 1)
                    A.activation(gs[:, u, 0:E0], bank(u, 2)[0:TT, 0:E0], ACT.Copy).then_inc(sem["f_logits"], 1)
                for u in range(2):
                    act.wait_ge(sem["gcentred"], i * 2 + u + 1)
                    A.activation(gs[:, u, 8:8 + E0], gs[:, u, 8:8 + E0], ACT.Exp,
                                 accum_out=gs[:, u, 12:13]).then_inc(sem["gexp"], 1)

            def ffn_exponentials(i):
                for u in range(2):
                    act.wait_ge(sem["gate_step"], i * 18 + u * 8 + 4)
                    A.activation(gs[:, u, 32:32 + E0], gs[:, u, 16:16 + E0], ACT.Exp).then_inc(sem["gexp2"], 1)
                for u in range(2):
                    act.wait_ge(sem["f_centred"], i * 2 + u + 1)
                    A.activation(pr[:, u, 0:E0 * TT], sc[:, u, 0:E0 * TT], ACT.Exp).then_inc(sem["f_exped"], 1)

            def ffn_copy_turned(i):
                for u in range(2):
                    act.wait_ge(sem["f_pt_ps"], i * 2 + u + 1)
                    A.activation(pT[:, u, 0:E0], bank(u, 2)[0:TT, 0:E0 * TT].rearrange("p (e t) -> p e t", e=E0),
                                 ACT.Copy).then_inc(sem["f_pT"], 1)

            def ffn_copy_values(i):
                for u in range(2):
                    act.wait_ge(sem["f_o_ps"], i * 2 + u + 1)
                    A.activation(f_oT[:, u, 0, :], bank(u, 3)[:, 0:TT], ACT.Copy)
                    A.activation(f_oT[0:HD0, u, 1, :], bank(u, 3)[0:HD0, TT:2 * TT], ACT.Copy)\
                        .then_inc(sem["f_oT"], 1)

            def keep_q(i):
                for u in range(2):
                    t = i * 2 + u
                    act.wait_ge(sem["l1_q_ps"], t + 1)
                    plain(act)
                    A.activation(qT_all[0:HC, :, bass.ds(t * TT, TT)],
                                 bank(u, 3)[0:HC, 0:2 * TT].rearrange("p (c t) -> p c t", c=2), ACT.Copy)\
                        .then_inc(sem["l1_q_stored"], 1)

            def step(n, a, b):
                if b is not None:
                    copy_turned(b * 2)
                    copy_values(b * 2)
                if a is not None:
                    copy_norm(0, a)
                    copy_v(a * 2, 1, 256)
                    copy_q(a)
                if b is not None:
                    copy_norm(1, b)
                    ffn_copies(b)
                    ffn_gate_steps(b)
                if n is not None:
                    square_pixels(n)
                if b is not None:
                    ffn_exponentials(b)
                    ffn_copy_turned(b)
                    ffn_copy_values(b)
                if a is not None:
                    exponentials(a * 2, 1.0)
                if b is not None:
                    copy_norm(2, b)
                if n is not None:
                    square_embedded(n)
                if b is not None:
                    keep_q(b)

            early = W_AT[W_PACK[EARLY][0]][0]
            act.dma_start(wc[:, 0:early], w_in[:, 0:early]).then_inc(sem["w_consts"], 16)
            act.dma_start(wc[:, early:], w_in[:, early:]).then_inc(sem["w_late"], 16)
            act.wait_ge(sem["ones_ready"], 1)
            step(0, None, None)
            act.wait_ge(sem["fills_ready"], 5)
            step(1, 0, None)
            step(2, 1, 0)
            with act.Fori(1, NP - 2) as i:
                step(i + 2, i + 1, i)
            step(None, NP - 1, NP - 2)
            step(None, None, NP - 1)

            rel2_rows = rel2.rearrange("t (b i) s -> (t b) i s", b=GI)
            for j in range(NTOK):
                act.wait_ge(sem["rel2_ps"], j + 1)
                if j >= 4:
                    act.wait_ge(rel2_out[j % 4], 16 * (j // 4))
                A.activation(rel2_buf[j % 4], bank(0, 2 + j % 2)[0:BP, 0:H * NTOK], ACT.Copy)\
                    .then_inc(sem["rel2_copied"], 1)
                act.wait_ge(sem["rel2_copied"], j + 1)
                act.dma_start(rel2_rows[:, j, :], rel2_buf[j % 4]).then_inc(rel2_out[j % 4], 16)
            act.wait_ge(sem["rel3_copied"], NTOK)
            rel3_rows = rel3.rearrange("t (b i) (h s) -> h i (t b) s", b=GI, h=3)
            for images, done in ((slice(0, 2 * GI), "rel3_first"), (slice(2 * GI, BP), "rel3_out")):
                for h in range(GI):
                    act.dma_start(rel3_rows[h][:, images, :],
                                  rel3_sb[h * NTOK:(h + 1) * NTOK, images].rearrange("p b g j -> p b (g j)"))\
                        .then_inc(sem[done], 16)

            def spread_q1(i):
                for u in range(2):
                    for c in range(2):
                        src = qT_all[0:HC, c, bass.ds((i * 2 + u) * TT, TT)].rearrange("p (b n) -> p b n", b=GI)
                        last = A.activation(diagonal(u, c), src, ACT.Copy)
                    last.then_inc(sem["qz_ready"], 1)

            def step1(n, a, b, c):
                scale = 1.0 / (3.0 * D) ** 0.5
                if b is not None:
                    copy_turned(NT + b * 2)
                if a is not None:
                    spread_q1(a)
                if b is not None:
                    copy_values(NT + b * 2)
                if c is not None:
                    copy_norm(4, c)
                if a is not None:
                    exponentials(NT + a * 2, scale, (0,))
                if n is not None:
                    copy_norm(3, n)
                if a is not None:
                    exponentials(NT + a * 2, scale, (1,))
                if n is not None:
                    copy_v(NT + n * 2, 2, 0)

            step1(0, None, None, None)
            step1(1, 0, None, None)
            step1(2, 1, 0, None)
            step1(3, 2, 1, 0)
            with act.Fori(1, NP - 3) as i:
                step1(i + 3, i + 2, i + 1, i)
            step1(None, NP - 1, NP - 2, NP - 3)
            step1(None, None, NP - 1, NP - 2)
            step1(None, None, None, NP - 1)

            def activate(p, u, first=False):
                k = p * 2 + u
                if not first:
                    act.wait_ge(sem["hidT_ps"], 2 * (k - 1))
                for half in range(2):
                    act.wait_ge(sem["hid_ps"], 2 * k + 1 + half)
                    A.activation(hid[:, u, half * HID // 2:(half + 1) * HID // 2], bank(u, half)[:, 0:HID // 2],
                                 ACT.Gelu).then_inc(sem["hid_ready"], 1)

            activate(0, 0, True)
            activate(0, 1, True)
            with act.Fori(1, NP) as i:
                for u in range(2):
                    activate(i, u)

        @block.gpsimd
        def _(pool):
            G = nc.gpsimd

            def power(k, i):
                c0 = norm_at[k]
                for u in range(2):
                    pool.wait_ge(mean[k], i * 2 + u + 1)
                    plain(pool)
                    G.tensor_scalar(c1(u, c0 + 11), c1(u, c0 + 9), LN_EPS, None, ALU.add).then_inc(rstd_in[k], 1)
                    pool.wait_ge(rstd_in[k], i * 2 + u + 1)
                    G.tensor_tensor(c1(u, c0 + 12), c1(u, c0 + 11), mhalf[0:TT], ALU.pow).then_inc(rstd[k], 1)

            def pixel_power(i):
                for u in range(2):
                    pool.wait_ge(sem["rms1_in"], i * 2 + u + 1)
                    G.tensor_tensor(c1(u, 1), c1(u, 0), mhalf[0:TT], ALU.pow).then_inc(sem["rms1"], 1)

            def embed_power(i):
                for u in range(2):
                    pool.wait_ge(sem["rms2_in"], i * 2 + u + 1)
                    G.tensor_tensor(c1(u, 4), c1(u, 3), mhalf[0:TT], ALU.pow).then_inc(sem["rms2"], 1)

            def gate(i):
                for u in range(2):
                    pool.wait_ge(sem["f_logits"], i * 2 + u + 1)
                    plain(pool)
                    G.tensor_scalar(gs[:, u, 5:6], gs[:, u, 0:1], gs[:, u, 1:2], gs[:, u, 2:3],
                                    ALU.max, ALU.max).then_inc(sem["gate_step"], 1)
                    pool.wait_ge(sem["gate_step"], i * 18 + u + 1)
                    plain(pool)
                    G.tensor_scalar(gs[:, u, 8:8 + E0], gs[:, u, 0:E0], gs[:, u, 5:6], None, ALU.subtract)\
                        .then_inc(sem["gcentred"], 1)
                for u in range(2):
                    t = i * 2 + u
                    at = i * 18 + 2 + u * 8
                    pool.wait_ge(sem["gexp"], t + 1)
                    G.tensor_tensor(gs[:, u, 13:14], gs[:, u, 12:13], mone[0:TT], ALU.pow)\
                        .then_inc(sem["gate_step"], 1)
                    pool.wait_ge(sem["gate_step"], at + 1)
                    plain(pool)
                    G.tensor_scalar(gs[:, u, 16:16 + E0], gs[:, u, 8:8 + E0], gs[:, u, 13:14], None,
                                    ALU.mult).then_inc(sem["gate_step"], 1)
                    pool.wait_ge(sem["gate_step"], at + 2)
                    plain(pool)
                    G.tensor_scalar(gs[:, u, 21:22], gs[:, u, 16:17], gs[:, u, 17:18], gs[:, u, 18:19],
                                    ALU.min, ALU.min).then_inc(sem["gate_step"], 1)
                    pool.wait_ge(sem["gate_step"], at + 3)
                    plain(pool)
                    G.tensor_scalar(gs[:, u, 24:24 + E0], gs[:, u, 16:16 + E0], gs[:, u, 21:22], None,
                                    ALU.is_le).then_inc(sem["gate_step"], 1)
                    pool.wait_ge(sem["gate_step"], at + 4)
                    G.tensor_tensor(gs[:, u, 28:28 + E0], gs[:, u, 24:24 + E0], w("rank_up")[0:TT, :], ALU.mult)\
                        .then_inc(sem["gate_step"], 1)
                    pool.wait_ge(sem["gate_step"], at + 5)
                    plain(pool)
                    G.tensor_scalar(gs[:, u, 45:46], gs[:, u, 28:29], gs[:, u, 29:30], gs[:, u, 30:31],
                                    ALU.max, ALU.max).then_inc(sem["gate_step"], 1)
                    pool.wait_ge(sem["gate_step"], at + 6)
                    plain(pool)
                    G.tensor_scalar(gs[:, u, 48:48 + E0], gs[:, u, 28:28 + E0], gs[:, u, 45:46], None,
                                    ALU.is_lt).then_inc(sem["gate_step"], 1)
                    pool.wait_ge(sem["gate_step"], at + 7)
                    pool.wait_ge(sem["gexp2"], t + 1)
                    G.tensor_tensor(gs[:, u, 36:36 + E0], gs[:, u, 32:32 + E0], gs[:, u, 48:48 + E0], ALU.mult)\
                        .then_inc(sem["gate_step"], 1)
                    pool.wait_ge(sem["gate_step"], at + 8)
                    plain(pool)
                    G.tensor_scalar(gs[:, u, 40:41], gs[:, u, 36:37], gs[:, u, 37:38], gs[:, u, 38:39],
                                    ALU.add, ALU.add).then_inc(sem["gwsum"], 1)

            def step(n, a, b):
                if a is not None:
                    embed_power(a)
                    power(0, a)
                if b is not None:
                    power(1, b)
                    gate(b)
                    power(2, b)
                if n is not None:
                    pixel_power(n)

            G.memset(mone[:], -1.0)
            G.memset(ones[:], 1.0).then_inc(sem["fills_ready"], 1)
            G.memset(mhalf[:], -0.5).then_inc(sem["fills_ready"], 1)
            for zeros in (vblk, qz, pz):
                G.memset(zeros[:], 0.0).then_inc(sem["fills_ready"], 1)
            pool.wait_ge(sem["fills_ready"], 2)
            pool.wait_ge(sem["w_consts"], 16)
            step(0, None, None)
            step(1, 0, None)
            pool.wait_ge(sem["w_late"], 16)
            step(2, 1, 0)
            with pool.Fori(1, NP - 2) as i:
                step(i + 2, i + 1, i)
            step(None, NP - 1, NP - 2)
            step(None, None, NP - 1)

            def spread_k1(i, first=False):
                for u in range(2):
                    t = i * 2 + u
                    if not first:
                        pool.wait_ge(sem["s_ps"], NT + t - 1)
                        plain(pool)
                    for c in range(2):
                        last = G.tensor_tensor(
                            kblk[:, u, c], kT_all[0:HC, c, bass.ds(t * TT, TT)].unsqueeze(1).broadcast_to([HC, 6, TT]),
                            w("head_mask")[0:HC].unsqueeze(2).broadcast_to([HC, 6, TT]), ALU.mult)
                    last.then_inc(sem["kblk_ready"], 1)

            def add_terms(i):
                for u in range(2):
                    pool.wait_ge(load_rel[u], (i + 1) * 32)
                    plain(pool)
                    G.tensor_tensor(rel_t[u][0], rel_t[u][0], rel_t[u][1], ALU.add).then_inc(sem["terms_added"], 1)

            def step1(n, a, c, first=False):
                if a is not None:
                    spread_k1(a, first)
                if c is not None:
                    power(4, c)
                if n is not None:
                    power(3, n)
                if a is not None:
                    add_terms(a)

            pool.wait_ge(sem["l1_k_stored"], NT)
            pool.wait_ge(sem["rel3_copied"], NTOK)
            step1(0, None, None)
            step1(1, 0, None, first=True)
            step1(2, 1, None)
            step1(3, 2, 0)
            with pool.Fori(1, NP - 3) as i:
                step1(i + 3, i + 2, i)
            step1(None, NP - 1, NP - 3)
            step1(None, None, NP - 2)
            step1(None, None, NP - 1)

            def fetch(dst, rows, idx, u, got):
                return G.indirect_dma_start(dst[:, u, :], None, rows[:, :],
                                            bass.IndirectOffsetOnAxis(ap=idx[:, u:u + 1], axis=0),
                                            bounds_check=NT_TOK - 1, oob_is_err=False).then_inc(got[u], 16)

            def fetch_x(p, u, first=False):
                k = p * 2 + u
                if not first:
                    pool.wait_ge(sem["x_turned_ps"], k - 1)
                    plain(pool)
                G.tensor_copy(idx_x[:, u:u + 1], ids[:, bass.ds(k, 1)]).then_inc(sem["idx_x_ready"], 1)
                pool.wait_ge(sem["idx_x_ready"], k + 1)
                plain(pool)
                fetch(mx, xn_rows, idx_x, u, got_x)

            def fetch_h(p, u, first=False):
                k = p * 2 + u
                if not first:
                    pool.wait_ge(sem["moe_sum"], k - 1)
                    plain(pool)
                    pool.wait_ge(put[u], p * 16)
                    plain(pool)
                G.tensor_copy(idx_h[:, u:u + 1], ids[:, bass.ds(k, 1)]).then_inc(sem["idx_h_ready"], 1)
                pool.wait_ge(sem["idx_h_ready"], k + 1)
                plain(pool)
                fetch(mh, h_rows, idx_h, u, got_h)

            def store(p, u):
                k = p * 2 + u
                pool.wait_ge(sem["moe_sum"], k + 1)
                plain(pool)
                G.indirect_dma_start(out[:, :], bass.IndirectOffsetOnAxis(ap=idx_h[:, u:u + 1], axis=0),
                                     my[:, u, :], None, bounds_check=NT_TOK - 1, oob_is_err=False)\
                    .then_inc(put[u], 16)

            pool.wait_ge(sem["ids_ready"], 2)
            G.memset(mx, 0.0).then_inc(sem["rows_clear"], 1)
            G.memset(mh, 0.0).then_inc(sem["rows_clear"], 1)
            pool.wait_ge(sem["rows_clear"], 2)
            pool.wait_ge(sem["xn_stored"], 16 * NP)
            pool.wait_ge(sem["h_stored"], 16 * NP)
            for u in range(2):
                fetch_x(0, u, True)
            for u in range(2):
                fetch_h(0, u, True)
            for u in range(2):
                fetch_x(1, u)
            with pool.Fori(0, NP - 2) as i:
                for u in range(2):
                    store(i, u)
                    fetch_x(i + 2, u)
                    fetch_h(i + 1, u)
            for u in range(2):
                store(NP - 2, u)
                fetch_h(NP - 1, u)
            for u in range(2):
                store(NP - 1, u)
            for u in range(2):
                pool.wait_ge(put[u], NP * 16)


_OUT_SHAPE = (NT_TOK, C)


def _put(pack, at, name, a, rows=0):
    lo, n = at[name]
    a = np.asarray(a, np.float32).reshape(a.shape[0], -1)
    assert a.shape[1] == n, (name, a.shape, n)
    pack[rows:rows + a.shape[0], lo:lo + n] = a


def _slab(weights, bias):
    n = weights.shape[1]
    out = np.zeros((HC + 1, 2, n), np.float32)
    out[0:HC] = weights.reshape(2, HC, n).transpose(1, 0, 2)
    out[HC, 1] = bias
    return out


def layout(a):
    x = a["x"]
    hw = IMG // PS
    x = x.reshape(B, CH, hw, PS, hw, PS).transpose(0, 2, 4, 3, 5, 1).reshape(B, NTOK, FEAT)
    x = np.concatenate([x, np.zeros((BP - B, NTOK, FEAT), np.float32)])
    x = x.reshape(NT, TT, KF, 128).transpose(0, 3, 2, 1).reshape(NT, 128, KF * TT)

    rows = np.arange(TT)
    img, tok = rows // NTOK, rows % NTOK
    tok_pack = np.zeros((128, TOK_COLS), np.float32)
    _put(tok_pack, TOK_AT, "wt", a["L0_tok_W"].T.reshape(KF, 128, C).transpose(1, 0, 2))
    _put(tok_pack, TOK_AT, "g1", a["L0_tok_g1"].T.reshape(KF, 128, NTOK).transpose(1, 0, 2))
    _put(tok_pack, TOK_AT, "tok_b", np.broadcast_to(a["L0_tok_b"], (TT, C)))
    _put(tok_pack, TOK_AT, "g2", np.tile(a["L0_tok_g2"], (GI, 1)))
    _put(tok_pack, TOK_AT, "ident", np.eye(128))
    _put(tok_pack, TOK_AT, "same_image", (img[:, None] == img) / (NTOK * C))
    _put(tok_pack, TOK_AT, "pixel_mean", np.full((128, TT), 1.0 / (NTOK * FEAT)))

    select = (tok[:, None, None] == tok) & (img[:, None, None] == np.arange(GI)[:, None])
    _put(tok_pack, TOK_AT, "select_image", select)

    wp = np.zeros((128, W_COLS), np.float32)
    wq, bq = a["L0_attn_w_qkv"], a["L0_attn_b_qkv"]
    fq, fb = a["L0_ffn_Wqk"], a["L0_ffn_bqk"]
    slabs = {
        "q0": (wq[:, :C], bq[:C]), "k0": (wq[:, C:2 * C], bq[C:2 * C]), "v0": (wq[:, 2 * C:], bq[2 * C:]),
        "o0": (a["L0_attn_w_proj"], a["L0_attn_b_proj"]),
        "fq": (fq[:, :C], fb[:C]), "fk": (fq[:, C:], fb[C:]),
        "fv": (a["L0_ffn_Wv"].transpose(1, 0, 2).reshape(C, C), a["L0_ffn_bv"].reshape(C)),
        "fg1": (a["L0_ffn_Wg1"], a["L0_ffn_bg1"]),
        "q1": (a["L1_attn_Wq"], a["L1_attn_bq"]), "k1": (a["L1_attn_Wk"], a["L1_attn_bk"]),
        "v1": (a["L1_attn_Wv"], a["L1_attn_bv"]), "o1": (a["L1_attn_Wo"], a["L1_attn_bo"]),
        "pk": (a["L1_attn_Wpk"], a["L1_attn_bpk"]), "pq": (a["L1_attn_Wpq"], a["L1_attn_bpq"]),
        "gate": (a["L1_ffn_gate_w"], a["L1_ffn_gate_b"]),
    }
    for name, (weights, bias) in slabs.items():
        _put(wp, W_AT, name, _slab(weights, bias))
    _put(wp, W_AT, "fg2", np.concatenate([a["L0_ffn_Wg2"], a["L0_ffn_bg2"][None]]))
    _put(wp, W_AT, "fpa", a["L0_ffn_Wp"][:128])
    _put(wp, W_AT, "fpb", np.concatenate([a["L0_ffn_Wp"][128:], a["L0_ffn_bp"][None]]))
    _put(wp, W_AT, "center", np.broadcast_to(a["L1_ffn_gate_center"], (TT, NE)))
    middle = (a["L1_attn_rel_table"].shape[0] - 1) // 2
    table = a["L1_attn_rel_table"][middle - NTOK + 1:middle + NTOK]
    _put(wp, W_AT, "relT", _slab(table.T, np.ones(REL, np.float32)))
    _put(wp, W_AT, "relrevT", _slab(table[::-1].T, np.ones(REL, np.float32)))
    head = np.array([3 * g + h for h in range(3) for g in range(2)])
    _put(wp, W_AT, "head_mask", (np.arange(HC)[:, None] // D == head).astype(np.float32))
    _put(wp, W_AT, "head_scale", np.repeat(a["L0_attn_scale"], D).reshape(2, HC).T)
    _put(wp, W_AT, "third_mask", (img[:, None] == np.arange(GI)).astype(np.float32))
    _put(wp, W_AT, "diag_mask", np.where((tok[:, None] == np.arange(NTOK)) & (tok[:, None] >= 1), NEG, 0.0))
    _put(wp, W_AT, "causal", np.where((img[:, None] == img) & (tok[None] <= tok[:, None]), 0.0, NEG))
    _put(wp, W_AT, "pos", np.tile(a["L0_ffn_pos_bias"][:NTOK, :NTOK], (GI, GI)))
    _put(wp, W_AT, "rank_up", np.broadcast_to(np.arange(1, E0 + 1), (TT, E0)))
    _put(wp, W_AT, "rank_down", np.broadcast_to(np.arange(NE, 0, -1), (TT, NE)))
    _put(wp, W_AT, "conv", np.concatenate([a["L0_ffn_conv_w"][:, 0], a["L0_ffn_conv_b"][:, None]], 1))
    _put(wp, W_AT, "b2", np.broadcast_to(a["L1_ffn_b2"].reshape(1, NE * C), (128, NE * C)))

    _put(wp, W_AT, "before", rows[:, None] < rows)
    _put(wp, W_AT, "token_id", 1 + TT * np.arange(NT) + rows[:, None])
    _put(wp, W_AT, "tile_at", np.broadcast_to(TM * np.arange(NM), (TT, NM)))
    _put(wp, W_AT, "tile_no", np.broadcast_to(np.arange(NM), (TT, NM)))
    _put(wp, W_AT, "row_no", np.broadcast_to(np.arange(TM), (TT, TM)))

    moe = np.zeros((128, BIG_COLS), np.float32)
    moe[:HC + 1, :2 * NE * HID] = np.stack([_slab(w1, b1) for w1, b1 in zip(a["L1_ffn_w1"], a["L1_ffn_b1"])],
                                           1).reshape(HC + 1, -1)
    moe[:, 2 * NE * HID:] = a["L1_ffn_w2"].reshape(NE, KH, 128, C).transpose(2, 0, 1, 3).reshape(128, -1)
    return {"x_in": np.ascontiguousarray(x), "tok_in": tok_pack, "w_in": wp, "moe_in": moe}


def program(nc, arrays):
    args = [nc.dram_tensor(n, v.shape, F32, kind="ExternalInput").ap() for n, v in arrays.items()]
    scratch = [nc.dram_tensor(n, (NT, TT, H * NTOK), F32).ap() for n in ("rel2_scratch", "rel3_scratch")]
    scratch += [nc.dram_tensor(n, (NT_TOK, C), F32).ap() for n in ("xn_rows", "h_rows")]
    out = nc.dram_tensor("out", _OUT_SHAPE, F32, kind="ExternalOutput").ap()
    build(nc, *args, *scratch, out)


def kernel(**inputs):
    import concourse.bacc as bacc
    from concourse.bass_utils import run_bass_kernel_spmd

    arrays = layout({k: np.asarray(v) for k, v in inputs.items()})
    nc = bacc.Bacc("TRN2", target_bir_lowering=False, num_devices=1)
    program(nc, arrays)
    got = run_bass_kernel_spmd(nc, [arrays], core_ids=[0]).results[0]["out"]
    return got.reshape(BP, NTOK, C)[:B]
```

```python
from contextlib import ExitStack

import numpy as np

import concourse.bass as bass
from concourse import mybir

F32 = mybir.dt.float32
U32 = mybir.dt.uint32
BF16 = mybir.dt.bfloat16
ALU = mybir.AluOpType
ACT = mybir.ActivationFunctionType
AX = mybir.AxisListType.X

B, CH, IMG, PS = 64, 3, 96, 16
NTOK = (IMG // PS) ** 2
FEAT = CH * PS * PS
KF = FEAT // 128
C = 192
HC = C // 2
H, D = 12, 16
GI = 3
TT = GI * NTOK
NT = 2 * -(-B // (2 * GI))
BP = NT * GI
NP = NT // 2
TM = 128
NT_TOK = NT * TT
E0, HD0, GH = 3, 64, 32
NE, HID = 4, 768
KH = HID // 128
NM = (NT_TOK + NE * (TM - 1)) // TM
NOWHERE = float(2 ** 20)
DIGIT = 64
assert NM == NT and NT_TOK < DIGIT * 256
REL = 2 * NTOK - 1
NEG = -1.0e30
TOK_EPS, LN_EPS = 1e-4, 1e-5

TOK_PACK = [("wt", KF * C), ("g1", KF * NTOK), ("tok_b", C), ("g2", C), ("ident", 128),
            ("same_image", TT), ("pixel_mean", TT),
            ("select_image", GI * TT)]
SLABS = ["o0", "fq", "fk", "fv", "q1", "k1", "v1", "o1", "pk", "pq"]
W_PACK = [("q0", 2 * C), ("k0", 2 * C), ("v0", 2 * C), ("head_mask", 6), ("head_scale", 2),
          ("third_mask", GI), ("diag_mask", NTOK), ("causal", TT), ("pos", TT)]
EARLY = len(W_PACK)
W_PACK += [(n, 2 * C) for n in SLABS] + [
    ("fg1", 2 * GH), ("fg2", E0), ("fpa", C), ("fpb", C), ("gate", 2 * NE), ("center", NE),
    ("relT", 2 * REL), ("relrevT", 2 * REL), ("rank_up", E0),
    ("rank_down", NE), ("conv", 4), ("b2", NE * C),
    ("before", TT), ("id_high", NT), ("id_low", NT), ("tile_at", NM), ("row_no", TM)]
BIG_COLS = 2 * NE * HID + NE * KH * C


def columns(pack):
    at, out = 0, {}
    for name, n in pack:
        out[name] = (at, n)
        at += n
    return out, at


TOK_AT, TOK_COLS = columns(TOK_PACK)
W_AT, W_COLS = columns(W_PACK)


def build(nc, x_in, tok_in, w_in, moe_in, rel2, rel3, xn_rows, h_rows, out):
    ctx = ExitStack()
    with ctx:
        def sb(name, shape, dtype=F32):
            return ctx.enter_context(nc.sbuf_tensor(name, shape, dtype))

        names = """tok_consts w_consts w_late moe_weights load_x0 load_x1 xg_ready ssq_ready tok_ps
            rms1_in rms1 y_ready ysum_ready rms2_ps rms2_in rms2 masks_ready ones_ready fills_ready
            stats0 stats1 stats2 stats3 stats4 mean0 mean1 mean2 mean3 mean4
            rstd_in0 rstd_in1 rstd_in2 rstd_in3 rstd_in4 rstd0 rstd1 rstd2 rstd3 rstd4
            xn0 xn1 xn2 xn3 xn4 xnT_ps0 xnT_ps1 xnT_ps2 xnT_ps3 xnT_ps4 xnT0 xnT1 xnT2 xnT3 xnT4
            h0 h1 h2 h3 vq_ps k_ps v_copied qz_ready kblk_ready v_ps vblk_ready s_ps biased biased2
            row_max centred exped row_sum pn_ready pt_ps pT_ready o_ps oT_ready y_ps
            f_qk_ps f_g1_ps f_v_ps f_copied f_v_copied f_g1_ready f_conv_step f_conv_ready f_q0_ready
            f_gate_ps f_logits f_s_ps f_biased f_centred f_exped f_sum f_factor f_pn f_pt_ps
            f_pT f_o_ps f_oT f_y_ps gate_step gcentred gexp gexp2
            gwsum f_den f_deninv l1_q_ps l1_k_ps l1_q_stored l1_k_stored
            relT_ps pkblk_ready pq_win_ready rel2_ps rel2_copied rel2_out0 rel2_out1 rel2_out2 rel2_out3
            rel3_ps rel3_copied rel3_first rel3_out terms_added load_rel0 load_rel1
            gate_ps choice_step onehot xn_stored h_stored
            rank_ps sort_step perm_ready ids_ps ids_ready rows_clear
            idx_x_ready idx_h_ready got_x0 got_x1 got_h0 got_h1 x_turned_ps x_turned
            hid_ps hid_ready hidT_ps hidT_ready moe_ps moe_y moe_sum put0 put1""".split()
        sem = {n: ctx.enter_context(nc.semaphore(n)) for n in names}

        tokc = sb("tokc", [128, TOK_COLS])
        wc = sb("wc", [128, W_COLS])
        big = sb("big", [128, BIG_COLS])

        def tokw(name):
            a, n = TOK_AT[name]
            return tokc[:, a:a + n]

        def w(name):
            a, n = W_AT[name]
            return wc[:, a:a + n]

        def slab(name):
            return w(name).rearrange("p (c n) -> p c n", c=2)

        x_sb = sb("x_sb", [128, 2, KF * TT])
        xg = sb("xg", [128, 2, KF * TT])
        ssq = sb("ssq", [128, 2, GI])
        y_sb = sb("y_sb", [TT, 2, C])
        col = sb("col", [128, 2, 96])
        xn_a = sb("xn_a", [TT, 2, C])
        xnT_a = sb("xnT_a", [HC + 1, 2, 2, TT])
        qz = sb("qz", [HC, 2, 2, GI * (TT + NTOK)])
        kblk = sb("kblk", [HC, 2, 2, 6, TT])
        vblk = sb("vblk", [TT, 2, 12, 96])
        sc_a = sb("sc_a", [TT, 2, H * NTOK])
        pr_a = sb("pr_a", [TT, 2, H * NTOK])
        xn_b = sb("xn_b", [TT, 2, C])
        xnT_b = sb("xnT_b", [HC + 1, 2, 2, TT])
        sc = sb("sc", [TT, 2, H * NTOK])
        pr = sb("pr", [TT, 2, H * NTOK])
        pT = sb("pT", [TT, 2, E0, TT])
        pz = sb("pz", [TT, 2, GI * (4 * TT + NTOK)])
        oT = sb("oT", [HC + 1, 2, 2, TT])
        gs = sb("gs", [TT, 2, 64])
        head_scaled = sb("head_scaled", [HC, 2, 6])
        hres = sb("hres", [TT, NT, C])
        qT_all = sb("qT_all", [128, 2, NT * TT])
        kT_all = sb("kT_all", [128, 2, NT * TT])
        oh = sb("oh", [TT, NT, NE])
        ids = sb("ids", [128, NM], U32)
        tile_expert = sb("tile_expert", [1, NM], U32)
        idx_x = sb("idx_x", [128, 2], U32)
        idx_h = sb("idx_h", [128, 2], U32)
        mhalf = sb("mhalf", [128, 1])
        mone = sb("mone", [128, 1])
        ones = sb("ones", [128, TT])

        free_at = [0]

        def in_big(rows, *shape):
            n = 1
            for d in shape:
                n *= d
            v = big[0:rows, free_at[0]:free_at[0] + n]
            free_at[0] += n
            if len(shape) == 2:
                return v.rearrange("p (a b) -> p a b", a=shape[0])
            if len(shape) == 3:
                return v.rearrange("p (a b c) -> p a b c", a=shape[0], b=shape[1])
            return v

        squares = in_big(128, 2, GI, KF * NTOK)
        y_squares = in_big(TT, 2, C)
        f_mask = in_big(TT, E0, TT)
        f_q0 = in_big(HD0, 2, GI * (NTOK + 2))
        f_qc = in_big(128, 2, 2, TT)
        f_q1 = in_big(128, 2, TT)
        f_q2 = in_big(128, 2, TT)
        f_k = in_big(128, 2, TT)
        f_k2 = in_big(128, 2, TT)
        f_v = in_big(TT, 2, C)
        f_g1T = in_big(GH + 1, 2, TT)
        f_oT = in_big(128, 2, 2, TT)
        n_rel3 = BP * 4 * NTOK
        rel3_sb = big[0:TT, 0:n_rel3].rearrange("p (b g j) -> p b g j", b=BP, g=4)
        pkblk = big[0:HC, n_rel3:n_rel3 + 12 * REL].rearrange("p (c s r) -> p c s r", c=2, s=6)
        w1 = big[:, 0:2 * NE * HID].rearrange("p (e c n) -> p e c n", e=NE, c=2)
        w2 = big[:, 2 * NE * HID:].rearrange("p (e k n) -> p e k n", e=NE, k=KH)

        pqblk = xg[0:HC].rearrange("p u n -> p (u n)")[:, 0:12 * REL].rearrange("p (c s r) -> p c s r", c=2, s=6)
        rel2_buf = [sc[0:BP, 0, :], sc[0:BP, 1, :], pr[0:BP, 0, :], pr[0:BP, 1, :]]
        rel_t = [[buf[0:TT, u, 0:H * NTOK] for buf in (xg, x_sb)] for u in range(2)]
        v_sb = y_sb
        pq_win = [kblk[:, n // 2, n % 2, 0:4, :] for n in range(4)]
        sort_at, moe_at = [0], [0]

        def view(flat, at, rows, *shape):
            n = 1
            for d in shape:
                n *= d
            v = flat[0:rows, at[0]:at[0] + n]
            at[0] += n
            assert at[0] <= 2 * NT_TOK
            if len(shape) == 2:
                return v.rearrange("p (a b) -> p a b", a=shape[0])
            if len(shape) == 3:
                return v.rearrange("p (a b c) -> p a b c", a=shape[0], b=shape[1])
            return v

        q_flat = qT_all.rearrange("p c t -> p (c t)")
        k_flat = kT_all.rearrange("p c t -> p (c t)")
        perm = view(q_flat, sort_at, TT, NT * TM // 2).bitcast(BF16)\
            .rearrange("p (t r) -> p t r", t=NT)
        reached = view(q_flat, sort_at, TT, NT, NM + 1)
        in_tile = view(q_flat, sort_at, TT, NT, NM)
        tile_id = view(q_flat, sort_at, TT, NT * NM).bitcast(BF16)\
            .rearrange("p (t d m) -> p t d m", t=NT, d=2)
        cnt = view(q_flat, sort_at, TT, 2, NE * NT)
        place = view(q_flat, sort_at, TT, NE * NT)
        e_tiles = view(q_flat, sort_at, TT, NE)
        e_start = view(q_flat, sort_at, TT, NE)
        spot = view(q_flat, sort_at, TT, NT)
        spot_in = view(q_flat, sort_at, TT, NT)
        id_low = view(q_flat, sort_at, 128, NM)
        id_sum = view(q_flat, sort_at, 128, NM)
        id_hole = view(q_flat, sort_at, 128, NM)
        mx = view(k_flat, moe_at, 128, 2, C)
        mh = view(k_flat, moe_at, 128, 2, C)
        my = view(k_flat, moe_at, 128, 2, C)
        mxT = view(k_flat, moe_at, HC + 1, 2, 2, TM)
        hid = view(k_flat, moe_at, 128, 2, HID)
        hidT = view(k_flat, moe_at, 128, 2, HID)
        ps = ctx.enter_context(nc.psum_tensor("ps", [128, 8, 512], F32))

        def bank(u, n):
            return ps[:, 4 * u + n, :]

        def c1(u, n, rows=TT):
            return col[0:rows, u, n:n + 1]

        wt = tokw("wt").rearrange("p (k n) -> p k n", k=KF)
        ident = tokw("ident")
        load_x = [sem["load_x0"], sem["load_x1"]]
        load_rel = [sem["load_rel0"], sem["load_rel1"]]
        got_x, got_h, put = ([sem["%s%d" % (n, u)] for u in range(2)] for n in ("got_x", "got_h", "put"))
        rel2_out = [sem["rel2_out%d" % q] for q in range(4)]
        stats, mean, rstd_in, rstd, xn_s, xnT_ps, xnT_s = (
            [sem["%s%d" % (n, k)] for k in range(5)]
            for n in ("stats", "mean", "rstd_in", "rstd", "xn", "xnT_ps", "xnT"))
        norm_at = [16, 64, 64, 16, 64]
        norm_out = [xn_a, xn_b, xn_b, xn_a, xn_b]
        norm_outT = [xnT_a, xnT_b, xnT_b, xnT_a, xnT_b]
        norm_bank = [1, 3, 3, 3, 1]
        block = ctx.enter_context(nc.Block())

        def plain(eng):
            eng.nop(nofuse=True)


        @block.sync
        def _(sp):
            sp.dma_start(tokc[:], tok_in).then_inc(sem["tok_consts"], 16)
            for u in range(2):
                sp.dma_start(x_sb[:, u, :], x_in[u]).then_inc(load_x[u], 16)
            with sp.Fori(1, NP) as i:
                for u in range(2):
                    before = (i - 1) * 2 + u
                    sp.wait_ge(sem["xg_ready"], before + 1)
                    plain(sp)
                    sp.wait_ge(sem["ssq_ready"], GI * (before + 1))
                    plain(sp)
                    sp.dma_start(x_sb[:, u, :], x_in[i * 2 + u]).then_inc(load_x[u], 16)
            for q in range(4):
                sp.wait_ge(rel2_out[q], 16 * (NTOK // 4))
            sp.wait_ge(sem["rel3_first"], 16 * GI)
            for u in range(2):
                sp.dma_start(rel_t[u][0], rel2[u]).then_inc(load_rel[u], 16)
                sp.dma_start(rel_t[u][1], rel3[u]).then_inc(load_rel[u], 16)
            sp.wait_ge(sem["rel3_out"], 16 * GI)
            sp.dma_start(big[:], moe_in).then_inc(sem["moe_weights"], 16)

            def load_terms(i):
                for u in range(2):
                    sp.wait_ge(sem["biased2"], (i - 1) * 2 + u + 1)
                    plain(sp)
                    sp.dma_start(rel_t[u][0], rel2[i * 2 + u]).then_inc(load_rel[u], 16)
                    sp.dma_start(rel_t[u][1], rel3[i * 2 + u]).then_inc(load_rel[u], 16)

            def store_rows(i):
                pair = bass.ds(i * 2, 2)
                sp.wait_ge(sem["h3"], i * 2 + 2)
                plain(sp)
                sp.dma_start(h_rows.rearrange("(t p) c -> p t c", p=TT)[:, pair, :], hres[:, pair, :])\
                    .then_inc(sem["h_stored"], 16)
                sp.wait_ge(xn_s[4], i * 2 + 2)
                plain(sp)
                sp.dma_start(xn_rows.rearrange("(t p) c -> p t c", p=TT)[:, pair, :], xn_b[:])\
                    .then_inc(sem["xn_stored"], 16)

            load_terms(1)
            load_terms(2)
            with sp.Fori(3, NP) as i:
                store_rows(i - 3)
                load_terms(i)
            store_rows(NP - 3)
            store_rows(NP - 2)
            store_rows(NP - 1)

        @block.tensor
        def _(pe):
            def project_tokens(dst, lhs, weights):
                for c in range(2):
                    rows = HC + c
                    last = nc.tensor.matmul(dst, lhs[0:rows, c, :], weights[0:rows, c, :],
                                            start=(c == 0), stop=(c == 1))
                return last

            def project_features(dst, weights, lo, n, rhs):
                for c in range(2):
                    rows = HC + c
                    last = nc.tensor.matmul(dst, weights[0:rows, c, lo:lo + n], rhs[0:rows, c, :],
                                            start=(c == 0), stop=(c == 1))
                return last

            def embed(i, u):
                t = i * 2 + u
                pe.wait_ge(sem["xg_ready"], t + 1)
                for k in range(KF):
                    nc.tensor.matmul(bank(u, 0)[0:TT, 0:C], xg[:, u, k * TT:(k + 1) * TT],
                                     wt[:, k, :], start=(k == 0), stop=(k == KF - 1))
                pe.wait_ge(sem["ssq_ready"], GI * (t + 1))
                nc.tensor.matmul(bank(u, 0)[0:TT, C:C + GI], tokw("pixel_mean"), ssq[:, u, :],
                                 start=True, stop=True).then_inc(sem["tok_ps"], 1)

            def embed_square(i):
                for u in range(2):
                    pe.wait_ge(sem["ysum_ready"], i * 2 + u + 1)
                    nc.tensor.matmul(bank(u, 0)[0:TT, C:C + 1], tokw("same_image")[0:TT, :],
                                     c1(u, 2), start=True, stop=True).then_inc(sem["rms2_ps"], 1)

            def transpose_norm(k, i, slots=range(2)):
                for u in slots:
                    pe.wait_ge(xn_s[k], i * 2 + u + 1)
                    for c in range(2):
                        last = nc.tensor.transpose(bank(u, norm_bank[k])[0:HC, c * TT:(c + 1) * TT],
                                                   norm_out[k][:, u, c * HC:(c + 1) * HC], ident[0:TT, 0:TT])
                    last.then_inc(xnT_ps[k], 1)

            def front_vq(i, u):
                pe.wait_ge(xnT_s[0], i * 2 + u + 1)
                project_tokens(bank(u, 1)[0:TT, 256:256 + C], xnT_a[:, u], slab("v0"))
                for m in range(2):
                    last = project_features(bank(u, 1)[0:HC, m * TT:(m + 1) * TT], slab("q0"), m * HC, HC, xnT_a[:, u])
                last.then_inc(sem["vq_ps"], 1)

            def front_k(u):
                for m in range(2):
                    last = project_features(bank(u, 0)[0:HC, m * TT:(m + 1) * TT], slab("k0"), m * HC, HC, xnT_a[:, u])
                last.then_inc(sem["k_ps"], 1)

            def front_v(i, slots):
                for u in slots:
                    pe.wait_ge(xnT_s[3], i * 2 + u + 1)
                    project_tokens(bank(u, 3)[0:TT, 256:256 + C], xnT_a[:, u], slab("v1"))\
                        .then_inc(sem["vq_ps"], 1)

            def v_thirds(at0):
                for u in range(2):
                    pe.wait_ge(sem["v_copied"], at0 + u + 1)
                    pe.wait_ge(sem["qz_ready"], at0 + u + 1)
                    pe.wait_ge(sem["kblk_ready"], at0 + u + 1)
                    for b in range(GI):
                        dst = bank(u, b // 2)[0:TT, (b % 2) * 256:(b % 2) * 256 + C]
                        last = nc.tensor.matmul(dst, tokw("select_image")[0:TT, b * TT:(b + 1) * TT],
                                                v_sb[:, u, :], start=True, stop=True)
                    last.then_inc(sem["v_ps"], 1)

            def scores(at0):
                for u in range(2):
                    pe.wait_ge(sem["vblk_ready"], GI * (at0 + u + 1))
                    s_out = bank(u, 1)[0:TT, 0:H * NTOK].rearrange("p (h g j) -> p h g j", h=3, g=4)
                    for c in range(2):
                        for b in range(GI):
                            rhs = kblk[:, u, c, :, b * NTOK:(b + 1) * NTOK]\
                                .rearrange("p (h g) j -> p h g j", h=3)
                            last = nc.tensor.matmul(s_out[:, :, 2 * c:2 * c + 2, :],
                                                    qz[:, u, c, b * TT:(b + 1) * TT], rhs,
                                                    start=(b == 0), stop=(b == GI - 1))
                    last.then_inc(sem["s_ps"], 1)

            def turn(at0, bank_read=None, slots=range(2)):
                for u in slots:
                    if bank_read is not None:
                        pe.wait_ge(bank_read, at0 + u - 1)
                    pe.wait_ge(sem["pn_ready"], at0 + u + 1)
                    for g in range(4):
                        last = nc.tensor.transpose(bank(u, 2)[0:TT, g * TT:(g + 1) * TT],
                                                   sc[:, u, g * TT:(g + 1) * TT], ident[0:TT, 0:TT])
                    last.then_inc(sem["pt_ps"], 1)

            def values(at0, slots=range(2)):
                for u in slots:
                    pe.wait_ge(sem["pT_ready"], at0 + u + 1)
                    vflat = vblk[:, u].rearrange("p m x -> p (m x)")
                    for c in range(2):
                        for n in range(2 * GI):
                            b, gg = n // 2, n % 2
                            first = (b * 4 + 2 * c + gg) * HC - gg * 48
                            at = (b * 4 + 2 * c + gg) * TT
                            last = nc.tensor.matmul(bank(u, 3)[0:HC, c * TT:(c + 1) * TT],
                                                    vflat[:, first:first + HC], pz[:, u, at:at + TT],
                                                    start=(n == 0), stop=(n == 2 * GI - 1))
                    last.then_inc(sem["o_ps"], 1)

            def project_out(at0, weights, n, slots=range(2)):
                for u in slots:
                    pe.wait_ge(sem["oT_ready"], at0 + u + 1)
                    project_tokens(bank(u, n)[0:TT, 0:C], oT[:, u], weights).then_inc(sem["y_ps"], 1)

            def ffn_gate_qkv(i):
                for u in range(2):
                    pe.wait_ge(xnT_s[1], i * 2 + u + 1)
                    project_features(bank(u, 2)[0:GH, 256:256 + TT], slab("fg1"), 0, GH, xnT_b[:, u])\
                        .then_inc(sem["f_g1_ps"], 1)
                for u in range(2):
                    for n, name in enumerate(("fq", "fk")):
                        project_features(bank(u, 3)[0:128, 2 * n * TT:(2 * n + 1) * TT], slab(name), 0, 128,
                                         xnT_b[:, u])
                        last = project_features(bank(u, 3)[0:HD0, (2 * n + 1) * TT:(2 * n + 2) * TT],
                                                slab(name), 128, HD0, xnT_b[:, u])
                    last.then_inc(sem["f_qk_ps"], 1)
                    pe.wait_ge(sem["f_g1_ready"], i * 2 + u + 1)
                    nc.tensor.matmul(bank(u, 2)[0:TT, 0:E0], f_g1T[:, u, :], w("fg2")[0:GH + 1, :],
                                     start=True, stop=True).then_inc(sem["f_gate_ps"], 1)
                for u in range(2):
                    pe.wait_ge(sem["f_logits"], i * 2 + u + 1)
                    project_tokens(bank(u, 2)[0:TT, 0:C], xnT_b[:, u], slab("fv")).then_inc(sem["f_v_ps"], 1)

            def ffn_scores(i):
                for u in range(2):
                    pe.wait_ge(sem["f_copied"], i * 2 + u + 1)
                    pe.wait_ge(sem["f_conv_ready"], i * 2 + u + 1)
                    for e, (q, k) in enumerate(((f_qc[:, u, 1, :], f_k[:, u, :]), (f_q1[:, u, :], f_k[:, u, :]),
                                                (f_q2[:, u, :], f_k2[:, u, :]))):
                        last = nc.tensor.matmul(bank(u, 3)[0:TT, e * TT:(e + 1) * TT], q, k,
                                                start=True, stop=True)
                    last.then_inc(sem["f_s_ps"], 1)

            def ffn_turn(i):
                for u in range(2):
                    pe.wait_ge(sem["f_pn"], i * 2 + u + 1)
                    pe.wait_ge(sem["f_v_copied"], i * 2 + u + 1)
                    for e in range(E0):
                        last = nc.tensor.transpose(bank(u, 2)[0:TT, e * TT:(e + 1) * TT],
                                                   pr[:, u, e * TT:(e + 1) * TT], ident[0:TT, 0:TT])
                    last.then_inc(sem["f_pt_ps"], 1)

            def ffn_values(i):
                for u in range(2):
                    pe.wait_ge(sem["f_pT"], i * 2 + u + 1)
                    for e in range(E0):
                        lo = HD0 * (e % 2)
                        last = nc.tensor.matmul(bank(u, 3)[lo:lo + HD0, (e // 2) * TT:(e // 2 + 1) * TT],
                                                f_v[:, u, e * HD0:(e + 1) * HD0], pT[:, u, e, :],
                                                start=True, stop=True)
                    last.then_inc(sem["f_o_ps"], 1)

            def ffn_out(i):
                for u in range(2):
                    pe.wait_ge(sem["f_oT"], i * 2 + u + 1)
                    nc.tensor.matmul(bank(u, 2)[0:TT, 0:C], f_oT[:, u, 0, :], w("fpa"), start=True, stop=False)
                    nc.tensor.matmul(bank(u, 2)[0:TT, 0:C], f_oT[0:HD0 + 1, u, 1, :], w("fpb")[0:HD0 + 1, :],
                                     start=False, stop=True).then_inc(sem["f_y_ps"], 1)

            def next_qk(i, slots):
                for u in slots:
                    pe.wait_ge(xnT_s[2], i * 2 + u + 1)
                    for name, n, done in (("q1", 3, "l1_q_ps"), ("k1", 1 + u, "l1_k_ps")):
                        for m in range(2):
                            last = project_features(bank(u, n)[0:HC, m * TT:(m + 1) * TT], slab(name), m * HC, HC,
                                                    xnT_b[:, u])
                        last.then_inc(sem[done], 1)

            def step(n, a, b, after=True):
                if b is not None:
                    values(b * 2, (0,))
                    turn(b * 2, sem["l1_k_stored"] if after else None, (1,))
                if a is not None:
                    embed_square(a)
                if b is not None:
                    values(b * 2, (1,))
                    project_out(b * 2, slab("o0"), 2, (0,))
                if a is not None:
                    transpose_norm(0, a, (0,))
                if b is not None:
                    project_out(b * 2, slab("o0"), 2, (1,))
                if a is not None:
                    transpose_norm(0, a, (1,))
                    front_vq(a, 0)
                    front_k(0)
                    front_vq(a, 1)
                if b is not None:
                    transpose_norm(1, b, (0,))
                if a is not None:
                    front_k(1)
                if b is not None:
                    transpose_norm(1, b, (1,))
                    ffn_gate_qkv(b)
                if a is not None:
                    v_thirds(a * 2)
                if b is not None:
                    ffn_scores(b)
                if a is not None:
                    scores(a * 2)
                if n is not None:
                    embed(n, 0)
                if b is not None:
                    ffn_turn(b)
                    ffn_values(b)
                    ffn_out(b)
                if n is not None:
                    embed(n, 1)
                if b is not None:
                    transpose_norm(2, b, (0,))
                    next_qk(b, (0,))
                    transpose_norm(2, b, (1,))
                if a is not None:
                    turn(a * 2, None, (0,))
                if b is not None:
                    next_qk(b, (1,))

            pe.wait_ge(sem["tok_consts"], 16)
            pe.wait_ge(sem["w_consts"], 16)
            pe.wait_ge(sem["ones_ready"], 1)
            step(0, None, None)
            step(1, 0, None)
            pe.wait_ge(sem["w_late"], 16)
            step(2, 1, 0, after=False)
            with pe.Fori(1, NP - 2) as i:
                step(i + 2, i + 1, i)
            step(None, NP - 1, NP - 2)
            step(None, None, NP - 1)

            for n, (name, table) in enumerate((("pk", "relrevT"), ("pq", "relT"))):
                for m in range(2):
                    last = project_features(bank(0, 0)[0:HC, (2 * n + m) * REL:(2 * n + m + 1) * REL],
                                            slab(name), m * HC, HC, slab(table))
            last.then_inc(sem["relT_ps"], 1)
            pe.wait_ge(sem["pkblk_ready"], 2)
            pe.wait_ge(sem["l1_q_stored"], NT)
            pe.wait_ge(sem["l1_k_stored"], NT)
            def rel2_scores(j):
                if j >= 4:
                    pe.wait_ge(sem["rel2_copied"], j - 3)
                dst = bank(0, j % 4)[0:BP, 0:H * NTOK].rearrange("p (h g j) -> p h g j", h=3, g=4)
                for c in range(2):
                    rhs = pkblk[:, c, :, NTOK - 1 - j:2 * NTOK - 1 - j].rearrange("p (h g) j -> p h g j", h=3)
                    last = nc.tensor.matmul(dst[:, :, 2 * c:2 * c + 2, :], qT_all[0:HC, c, j::NTOK], rhs,
                                            start=True, stop=True)
                last.then_inc(sem["rel2_ps"], 1)

            def rel3_scores(j):
                if j >= 4:
                    pe.wait_ge(sem["rel3_copied"], j - 3)
                pe.wait_ge(sem["pq_win_ready"], j + 1)
                for g in range(4):
                    last = nc.tensor.matmul(bank(1, j % 4)[0:TT, g * BP:(g + 1) * BP], pq_win[j % 4][:, g, :],
                                            kT_all[0:HC, g // 2, j::NTOK], start=True, stop=True)
                last.then_inc(sem["rel3_ps"], 1)

            for first in range(0, NTOK, 4):
                for j in range(first, first + 4):
                    rel2_scores(j)
                for j in range(first, first + 4):
                    rel3_scores(j)
            pe.wait_ge(sem["rel2_copied"], NTOK)
            pe.wait_ge(sem["rel3_copied"], NTOK)

            def step1(n, a, b, c):
                for u in range(2):
                    if a is not None:
                        pe.wait_ge(sem["v_copied"], NT + a * 2 + u + 1)
                    if b is not None:
                        if u == 1:
                            turn(NT + b * 2, slots=(1,))
                        values(NT + b * 2, (u,))
                if c is not None:
                    transpose_norm(4, c)
                    for u in range(2):
                        pe.wait_ge(xnT_s[4], c * 2 + u + 1)
                        project_tokens(bank(u, 2)[0:TT, 0:NE], xnT_b[:, u], slab("gate"))\
                            .then_inc(sem["gate_ps"], 1)
                if a is not None:
                    v_thirds(NT + a * 2)
                    scores(NT + a * 2)
                if n is not None:
                    if b is not None:
                        pe.wait_ge(sem["oT_ready"], NT + b * 2 + 2)
                    transpose_norm(3, n)
                if b is not None:
                    project_out(NT + b * 2, slab("o1"), 0)
                if n is not None:
                    front_v(n, (0,))
                if a is not None:
                    turn(NT + a * 2, slots=(0,))
                if n is not None:
                    front_v(n, (1,))

            step1(0, None, None, None)
            step1(1, 0, None, None)
            step1(2, 1, 0, None)
            step1(3, 2, 1, 0)
            with pe.Fori(1, NP - 3) as i:
                step1(i + 3, i + 2, i + 1, i)
            step1(None, NP - 1, NP - 2, NP - 3)
            step1(None, None, NP - 1, NP - 2)
            step1(None, None, None, NP - 1)

            pe.wait_ge(sem["onehot"], NT)
            pe.wait_ge(sem["fills_ready"], 2)
            oh_all = oh.rearrange("p t e -> p (t e)")
            nc.tensor.matmul(bank(0, 0)[0:TT, 0:NT * NE], w("before")[0:TT, :], oh_all, start=True, stop=True)
            nc.tensor.matmul(bank(0, 1)[0:TT, 0:NT * NE], ones[0:TT, 0:TT], oh_all, start=True, stop=True)\
                .then_inc(sem["rank_ps"], 1)
            for t in range(NT):
                if t % NP == 0:
                    pe.wait_ge(sem["perm_ready"], 3 + t // NP)
                last = nc.tensor.matmul(bank(0, 2)[:, 0:2 * NM], perm[:, t, :],
                                        tile_id[:, t].rearrange("p d m -> p (d m)"),
                                        start=(t == 0), stop=(t == NT - 1))
            last.then_inc(sem["ids_ps"], 1)

            def expert_of(k):
                return pe.value_load(tile_expert[0:1, bass.ds(k, 1)], min_val=0, max_val=NE - 1)

            def turn_x(p, u, first=False):
                k = p * 2 + u
                pe.wait_ge(got_x[u], (p + 1) * 16)
                if not first:
                    pe.wait_ge(sem["hid_ready"], 2 * (k - 1))
                for c in range(2):
                    last = nc.tensor.transpose(bank(u, 1)[0:HC, c * TM:(c + 1) * TM],
                                               mx[:, u, c * HC:(c + 1) * HC], ident)
                last.then_inc(sem["x_turned_ps"], 1)

            def hidden(p, u, e, first=False):
                k = p * 2 + u
                pe.wait_ge(sem["x_turned"], k + 2)
                if not first:
                    pe.wait_ge(sem["moe_y"], k - 1)
                for half in range(2):
                    for c in range(2):
                        last = nc.tensor.matmul(bank(u, half)[:, 0:HID // 2], mxT[0:HC + c, u, c, :],
                                                w1[0:HC + c, bass.ds(e, 1), c, half * HID // 2:(half + 1) * HID // 2]
                                                .rearrange("p e n -> p (e n)"),
                                                start=(c == 0), stop=(c == 1))
                    last.then_inc(sem["hid_ps"], 1)

            def turn_hidden(p, u, first=False):
                k = p * 2 + u
                if not first:
                    pe.wait_ge(sem["hidT_ready"], 2 * (k - 1))
                for half in range(2):
                    pe.wait_ge(sem["hid_ready"], 2 * k + 1 + half)
                    for m in range(3):
                        at = (3 * half + m) * 128
                        last = nc.tensor.transpose(bank(u, 2 + half)[:, m * TM:(m + 1) * TM],
                                                   hid[:, u, at:at + 128], ident)
                    last.then_inc(sem["hidT_ps"], 1)

            def answer(p, u, e):
                k = p * 2 + u
                for m in range(KH):
                    if m % 3 == 0:
                        pe.wait_ge(sem["hidT_ready"], 2 * k + 1 + m // 3)
                    last = nc.tensor.matmul(bank(u, 0)[:, 0:C], hidT[:, u, m * TM:(m + 1) * TM],
                                            w2[:, bass.ds(e, 1), m, :].rearrange("p e n -> p (e n)"),
                                            start=(m == 0), stop=(m == KH - 1))
                last.then_inc(sem["moe_ps"], 1)

            def tiles(p, first=False):
                e0, e1, e2 = expert_of(p * 2), expert_of(p * 2 + 1), expert_of(p * 2 + 2)
                turn_hidden(p, 0, first)
                turn_x(p + 1, 0)
                hidden(p, 1, e1, first)
                answer(p, 0, e0)
                turn_hidden(p, 1, first)
                turn_x(p + 1, 1)
                hidden(p + 1, 0, e2)
                answer(p, 1, e1)

            pe.wait_ge(sem["moe_weights"], 16)
            turn_x(0, 0, True)
            turn_x(0, 1, True)
            pe.wait_ge(sem["ids_ready"], 2)
            hidden(0, 0, expert_of(0), True)
            tiles(0, True)
            with pe.Fori(1, NP - 1) as i:
                tiles(i)
            e0, e1 = expert_of(NM - 2), expert_of(NM - 1)
            turn_hidden(NP - 1, 0)
            hidden(NP - 1, 1, e1)
            answer(NP - 1, 0, e0)
            turn_hidden(NP - 1, 1)
            answer(NP - 1, 1, e1)

        @block.vector
        def _(dve):
            V = nc.vector

            def norm_stats(k, u, at, src):
                c0 = norm_at[k]
                plain(dve)
                V.bn_stats(col[0:TT, u, c0:c0 + 6], src).then_inc(stats[k], 1)
                dve.wait_ge(stats[k], at + 1)
                plain(dve)
                V.bn_aggr(col[0:TT, u, c0 + 8:c0 + 10], col[0:TT, u, c0:c0 + 6]).then_inc(mean[k], 1)

            def norm_apply(k, i, first=False):
                c0 = norm_at[k]
                for u in range(2):
                    t = i * 2 + u
                    dve.wait_ge(rstd[k], t + 1)
                    if k == 4 and not first:
                        dve.wait_ge(sem["xn_stored"], i * 16)
                    V.tensor_scalar(norm_out[k][:, u, :], hres[:, t, :], c1(u, c0 + 8), c1(u, c0 + 12),
                                    ALU.subtract, ALU.mult).then_inc(xn_s[k], 1)

            def add_residual(i, src_ps, src_at, h_sem, k, n=2, slots=range(2)):
                for u in slots:
                    t = i * 2 + u
                    dve.wait_ge(src_ps, src_at + u + 1)
                    V.tensor_tensor(hres[:, t, :], bank(u, n)[0:TT, 0:C], hres[:, t, :], ALU.add)\
                        .then_inc(h_sem, 1)
                    dve.wait_ge(h_sem, t + 1)
                    norm_stats(k, u, t, hres[:, t, :])

            def v_spread(at0):
                m = w("third_mask")[0:TT, :].unsqueeze(1).unsqueeze(3).broadcast_to([TT, 4, 3, D])
                for u in range(2):
                    dve.wait_ge(sem["v_ps"], at0 + u + 1)
                    for b in range(GI):
                        src = bank(u, b // 2)[0:TT, (b % 2) * 256:(b % 2) * 256 + C]\
                            .rearrange("p (g h d) -> p g h d", g=4, h=3)
                        dst = vblk[:, u, 4 * b:4 * b + 4, 0:48].rearrange("p g (h d) -> p g h d", h=3)
                        V.tensor_tensor(dst, src, m, ALU.mult).then_inc(sem["vblk_ready"], 1)

            def centre(u, at, biased_sem, biased_at):
                s3 = sc_a[:, u, :].rearrange("p (s j) -> p s j", s=H)
                dve.wait_ge(biased_sem, biased_at)
                V.tensor_reduce(col[0:TT, u, 32:32 + H], s3, AX, ALU.max).then_inc(sem["row_max"], 1)
                dve.wait_ge(sem["row_max"], at + 1)
                V.tensor_tensor(s3, s3, col[0:TT, u, 32:32 + H].unsqueeze(2).broadcast_to([TT, H, NTOK]),
                                ALU.subtract).then_inc(sem["centred"], 1)

            def probabilities(at0, slots=range(2)):
                for u in slots:
                    at = at0 + u
                    p3 = pr_a[:, u, :].rearrange("p (s j) -> p s j", s=H)
                    dve.wait_ge(sem["exped"], at + 1)
                    V.tensor_reduce(col[0:TT, u, 44:44 + H], p3, AX, ALU.add).then_inc(sem["row_sum"], 1)
                    dve.wait_ge(sem["row_sum"], 2 * at + 1)
                    V.reciprocal(col[0:TT, u, 44:44 + H], col[0:TT, u, 44:44 + H]).then_inc(sem["row_sum"], 1)
                    dve.wait_ge(sem["row_sum"], 2 * at + 2)
                    V.tensor_tensor(sc[:, u, :].rearrange("p (g h j) -> p h g j", g=4, h=3),
                                    pr_a[:, u, :].rearrange("p (h g j) -> p h g j", g=4, h=3),
                                    col[0:TT, u, 44:44 + H].rearrange("p (h g) -> p h g", g=4).unsqueeze(3)
                                    .broadcast_to([TT, 3, 4, NTOK]), ALU.mult).then_inc(sem["pn_ready"], 1)

            def spread_k(u, c, src, mask):
                return V.tensor_tensor(kblk[:, u, c], src.unsqueeze(1).broadcast_to([HC, 6, TT]),
                                       mask.unsqueeze(2).broadcast_to([HC, 6, TT]), ALU.mult)

            V.memset(f_q0[:], 0.0)
            V.memset(f_qc[HD0:128], 0.0)
            V.memset(f_q1[0:HD0], 0.0)
            V.memset(f_q2[HD0:128], 0.0)
            V.memset(f_k2[HD0:128], 0.0)
            V.memset(xnT_a[HC:HC + 1], 1.0)
            V.memset(xnT_b[HC:HC + 1], 1.0)
            V.memset(oT[HC:HC + 1], 1.0)
            V.memset(f_g1T[GH:GH + 1], 1.0)
            V.memset(f_oT[HD0:HD0 + 1, :, 1, :], 1.0).then_inc(sem["ones_ready"], 1)
            dve.wait_ge(sem["tok_consts"], 16)
            dve.wait_ge(sem["w_consts"], 16)
            for c in range(2):
                V.tensor_scalar(head_scaled[:, c, :], w("head_mask")[0:HC, :], w("head_scale")[0:HC, c:c + 1],
                                None, ALU.mult).then_inc(sem["masks_ready"], 1)
            for e in range(E0 - 1):
                V.tensor_copy(f_mask[:, e, :], w("causal")[0:TT, :]).then_inc(sem["masks_ready"], 1)
            V.tensor_tensor(f_mask[:, E0 - 1, :], w("causal")[0:TT, :], w("pos")[0:TT, :], ALU.add)\
                .then_inc(sem["masks_ready"], 1)
            dve.wait_ge(sem["masks_ready"], 5)
            dve.wait_ge(sem["ones_ready"], 1)

            g1 = tokw("g1").rearrange("p (k n) -> p k n", k=KF).unsqueeze(2).broadcast_to([128, KF, GI, NTOK])

            def weigh_pixels(i):
                for u in range(2):
                    dve.wait_ge(load_x[u], (i + 1) * 16)
                    V.tensor_tensor(xg[:, u, :].rearrange("p (k b n) -> p k b n", k=KF, b=GI),
                                    x_sb[:, u, :].rearrange("p (k b n) -> p k b n", k=KF, b=GI),
                                    g1, ALU.mult).then_inc(sem["xg_ready"], 1)

            def pixel_scale(i):
                for u in range(2):
                    dve.wait_ge(sem["tok_ps"], i * 2 + u + 1)
                    V.scalar_tensor_tensor(out=col[0:TT, u, 8:8 + GI], in0=bank(u, 0)[0:TT, C:C + GI],
                                           scalar=TOK_EPS, in1=w("third_mask")[0:TT, :],
                                           op0=ALU.add, op1=ALU.mult, accum_out=c1(u, 0))\
                        .then_inc(sem["rms1_in"], 1)

            def embed_scale(i):
                for u in range(2):
                    dve.wait_ge(sem["rms1"], i * 2 + u + 1)
                    V.scalar_tensor_tensor(out=y_sb[:, u, :], in0=bank(u, 0)[0:TT, 0:C], scalar=c1(u, 1),
                                           in1=tokw("tok_b")[0:TT, :], op0=ALU.mult, op1=ALU.add)\
                        .then_inc(sem["y_ready"], 1)

            def embed_norm(i):
                for u in range(2):
                    dve.wait_ge(sem["rms2_ps"], i * 2 + u + 1)
                    V.tensor_scalar(c1(u, 3), bank(u, 0)[0:TT, C:C + 1], TOK_EPS, None, ALU.add)\
                        .then_inc(sem["rms2_in"], 1)

            def embed_out(i):
                for u in range(2):
                    t = i * 2 + u
                    dve.wait_ge(sem["rms2"], t + 1)
                    V.scalar_tensor_tensor(out=hres[:, t, :], in0=y_sb[:, u, :], scalar=c1(u, 4),
                                           in1=tokw("g2")[0:TT, :], op0=ALU.mult, op1=ALU.mult)\
                        .then_inc(sem["h0"], 1)
                    dve.wait_ge(sem["h0"], t + 1)
                    norm_stats(0, u, t, hres[:, t, :])

            def spread_k0(i):
                for u in range(2):
                    dve.wait_ge(sem["k_ps"], i * 2 + u + 1)
                    k_src = bank(u, 0)[0:HC, 0:2 * TT].rearrange("p (c t) -> p c t", c=2)
                    for c in range(2):
                        last = spread_k(u, c, k_src[:, c], head_scaled[:, c])
                    last.then_inc(sem["kblk_ready"], 1)

            def mask_scores(i, slots):
                for u in slots:
                    t = i * 2 + u
                    dve.wait_ge(sem["s_ps"], t + 1)
                    V.tensor_tensor(sc_a[:, u, :].rearrange("p (s j) -> p s j", s=H),
                                    bank(u, 1)[0:TT, 0:H * NTOK].rearrange("p (s j) -> p s j", s=H),
                                    w("diag_mask")[0:TT, :].unsqueeze(1).broadcast_to([TT, H, NTOK]), ALU.add)\
                        .then_inc(sem["biased"], 1)
                    centre(u, t, sem["biased"], t + 1)

            def ffn_gate_hidden(i):
                for u in range(2):
                    dve.wait_ge(sem["f_g1_ps"], i * 2 + u + 1)
                    V.tensor_scalar(f_g1T[0:GH, u, :], bank(u, 2)[0:GH, 256:256 + TT], 0.0, None, ALU.max)\
                        .then_inc(sem["f_g1_ready"], 1)

            def ffn_v(i):
                for u in range(2):
                    dve.wait_ge(sem["f_v_ps"], i * 2 + u + 1)
                    V.tensor_copy(f_v[:, u, :], bank(u, 2)[0:TT, 0:C]).then_inc(sem["f_v_copied"], 1)

            def ffn_convolve(i):
                cv = w("conv")[0:HD0]
                for u in range(2):
                    t = i * 2 + u
                    q0 = f_q0[:, u, :].rearrange("p (b n) -> p b n", b=GI)
                    qa, qb = (f_qc[0:HD0, u, s, :].rearrange("p (b n) -> p b n", b=GI) for s in range(2))
                    dve.wait_ge(sem["f_q0_ready"], t + 1)
                    V.tensor_scalar(qa, q0[:, :, 0:NTOK], cv[:, 0:1], cv[:, 3:4], ALU.mult, ALU.add)\
                        .then_inc(sem["f_conv_step"], 1)
                    dve.wait_ge(sem["f_conv_step"], 2 * t + 1)
                    V.scalar_tensor_tensor(out=qb, in0=q0[:, :, 1:NTOK + 1], scalar=cv[:, 1:2], in1=qa,
                                           op0=ALU.mult, op1=ALU.add).then_inc(sem["f_conv_step"], 1)
                    dve.wait_ge(sem["f_conv_step"], 2 * t + 2)
                    V.scalar_tensor_tensor(out=qb, in0=q0[:, :, 2:NTOK + 2], scalar=cv[:, 2:3], in1=qb,
                                           op0=ALU.mult, op1=ALU.add).then_inc(sem["f_conv_ready"], 1)

            def ffn_centre(i):
                for u in range(2):
                    t = i * 2 + u
                    s3 = sc[:, u, 0:E0 * TT].rearrange("p (e j) -> p e j", e=E0)
                    mx = col[0:TT, u, 80:80 + E0]
                    dve.wait_ge(sem["f_s_ps"], t + 1)
                    V.scalar_tensor_tensor(out=sc[:, u, 0:E0 * TT], in0=bank(u, 3)[0:TT, 0:E0 * TT],
                                           scalar=1.0 / HD0 ** 0.5, in1=f_mask[:].rearrange("p e j -> p (e j)"),
                                           op0=ALU.mult, op1=ALU.add).then_inc(sem["f_biased"], 1)
                    dve.wait_ge(sem["f_biased"], 2 * t + 1)
                    V.tensor_reduce(mx, s3, AX, ALU.max).then_inc(sem["f_biased"], 1)
                    dve.wait_ge(sem["f_biased"], 2 * t + 2)
                    V.tensor_tensor(s3, s3, mx.unsqueeze(2).broadcast_to([TT, E0, TT]), ALU.subtract)\
                        .then_inc(sem["f_centred"], 1)

            def ffn_probabilities(i):
                for u in range(2):
                    t = i * 2 + u
                    p3 = pr[:, u, 0:E0 * TT].rearrange("p (e j) -> p e j", e=E0)
                    den = col[0:TT, u, 84:84 + E0]
                    dve.wait_ge(sem["f_exped"], t + 1)
                    V.tensor_reduce(den, p3, AX, ALU.add).then_inc(sem["f_sum"], 1)
                    dve.wait_ge(sem["f_sum"], t + 1)
                    dve.wait_ge(sem["gwsum"], t + 1)
                    V.tensor_scalar(den, den, gs[:, u, 40:41], None, ALU.mult).then_inc(sem["f_den"], 1)
                    dve.wait_ge(sem["f_den"], t + 1)
                    V.reciprocal(den, den).then_inc(sem["f_deninv"], 1)
                    dve.wait_ge(sem["f_deninv"], t + 1)
                    V.tensor_tensor(den, den, gs[:, u, 36:36 + E0], ALU.mult).then_inc(sem["f_factor"], 1)
                    dve.wait_ge(sem["f_factor"], t + 1)
                    V.tensor_tensor(p3, p3, den.unsqueeze(2).broadcast_to([TT, E0, TT]), ALU.mult)\
                        .then_inc(sem["f_pn"], 1)

            def keep_k(i, slots):
                for u in slots:
                    t = i * 2 + u
                    dve.wait_ge(sem["l1_k_ps"], t + 1)
                    V.tensor_copy(kT_all[0:HC, :, bass.ds(t * TT, TT)],
                                  bank(u, 1 + u)[0:HC, 0:2 * TT].rearrange("p (c t) -> p c t", c=2))\
                        .then_inc(sem["l1_k_stored"], 1)

            def step(n, a, b):
                if a is not None:
                    embed_norm(a)
                    embed_out(a)
                    norm_apply(0, a)
                if n is not None:
                    weigh_pixels(n)
                if b is not None:
                    add_residual(b, sem["y_ps"], b * 2, sem["h1"], 1)
                    norm_apply(1, b)
                if a is not None:
                    spread_k0(a)
                if b is not None:
                    ffn_gate_hidden(b)
                    ffn_convolve(b)
                if a is not None:
                    v_spread(a * 2)
                if b is not None:
                    ffn_v(b)
                    ffn_centre(b)
                    ffn_probabilities(b)
                if a is not None:
                    mask_scores(a, (0,))
                if b is not None:
                    add_residual(b, sem["f_y_ps"], b * 2, sem["h2"], 2)
                    norm_apply(2, b)
                if n is not None:
                    pixel_scale(n)
                if a is not None:
                    probabilities(a * 2, (0,))
                if b is not None:
                    keep_k(b, (0,))
                if a is not None:
                    mask_scores(a, (1,))
                    probabilities(a * 2, (1,))
                if b is not None:
                    keep_k(b, (1,))
                if n is not None:
                    embed_scale(n)

            step(0, None, None)
            dve.wait_ge(sem["fills_ready"], 5)
            dve.wait_ge(sem["w_late"], 16)
            step(1, 0, None)
            step(2, 1, 0)
            with dve.Fori(1, NP - 2) as i:
                step(i + 2, i + 1, i)
            step(None, NP - 1, NP - 2)
            step(None, None, NP - 1)

            dve.wait_ge(sem["relT_ps"], 1)
            for n, dst in enumerate((pkblk, pqblk)):
                src = bank(0, 0)[0:HC, 2 * n * REL:2 * (n + 1) * REL].rearrange("p (c r) -> p c r", c=2)
                for c in range(2):
                    last = V.tensor_tensor(dst[:, c], src[:, c].unsqueeze(1).broadcast_to([HC, 6, REL]),
                                           w("head_mask")[0:HC].unsqueeze(2).broadcast_to([HC, 6, REL]), ALU.mult)
                last.then_inc(sem["pkblk_ready"], 1)

            def window(j):
                for c in range(2):
                    src = pqblk[:, c, :, NTOK - 1 - j:2 * NTOK - 1 - j].rearrange("p (h g) i -> p g h i", h=3)
                    last = V.tensor_copy(
                        pq_win[j % 4][:, 2 * c:2 * c + 2, :].rearrange("p g (h i) -> p g h i", h=3), src)
                last.then_inc(sem["pq_win_ready"], 1)

            dve.wait_ge(sem["pkblk_ready"], 2)
            for j in range(4):
                window(j)
            for j in range(NTOK):
                dve.wait_ge(sem["rel3_ps"], j + 1)
                if j + 4 < NTOK:
                    window(j + 4)
                V.tensor_copy(rel3_sb[:, :, :, j].rearrange("p b g -> p g b"),
                              bank(1, j % 4)[0:TT, 0:4 * BP].rearrange("p (g b) -> p g b", g=4))\
                    .then_inc(sem["rel3_copied"], 1)

            def bias_scores(i, slots):
                for u in slots:
                    t = i * 2 + u
                    dve.wait_ge(sem["s_ps"], NT + t + 1)
                    dve.wait_ge(sem["terms_added"], t + 1)
                    V.tensor_tensor(sc_a[:, u, :], bank(u, 1)[0:TT, 0:H * NTOK], rel_t[u][0], ALU.add)\
                        .then_inc(sem["biased2"], 1)
                    centre(u, NT + t, sem["biased2"], t + 1)

            def step1(n, a, b, c, first=False):
                if c is not None:
                    add_residual(c, sem["y_ps"], NT + c * 2, sem["h3"], 4, 0)
                    norm_apply(4, c, first)
                if n is not None:
                    for u in range(2):
                        norm_stats(3, u, n * 2 + u, hres[:, n * 2 + u, :])
                    if a is not None:
                        dve.wait_ge(xnT_ps[3], a * 2 + 2)
                    norm_apply(3, n)
                if c is not None:
                    gate_scores(c)
                if a is not None:
                    v_spread(NT + a * 2)
                if c is not None:
                    choose_expert(c)
                if a is not None:
                    for u in range(2):
                        bias_scores(a, (u,))
                        probabilities(NT + a * 2, (u,))

            def gate_scores(i):
                for u in range(2):
                    dve.wait_ge(sem["gate_ps"], i * 2 + u + 1)
                    V.tensor_tensor(gs[:, u, 0:NE], bank(u, 2)[0:TT, 0:NE], w("center")[0:TT, :], ALU.subtract)\
                        .then_inc(sem["choice_step"], 1)

            def choose_expert(i):
                for u in range(2):
                    t = i * 2 + u
                    at = i * 8 + 2 + 3 * u
                    lg = gs[:, u, 0:NE]
                    if u == 0:
                        dve.wait_ge(sem["choice_step"], at)
                    V.tensor_reduce(gs[:, u, 4:5], lg, AX, ALU.max).then_inc(sem["choice_step"], 1)
                    dve.wait_ge(sem["choice_step"], at + 1)
                    V.scalar_tensor_tensor(out=gs[:, u, 8:8 + NE], in0=lg, scalar=gs[:, u, 4:5],
                                           in1=w("rank_down")[0:TT, :], op0=ALU.is_ge, op1=ALU.mult)\
                        .then_inc(sem["choice_step"], 1)
                    dve.wait_ge(sem["choice_step"], at + 2)
                    V.tensor_reduce(gs[:, u, 5:6], gs[:, u, 8:8 + NE], AX, ALU.max).then_inc(sem["choice_step"], 1)
                    dve.wait_ge(sem["choice_step"], at + 3)
                    V.tensor_scalar(oh[:, t, :], gs[:, u, 8:8 + NE], gs[:, u, 5:6], None, ALU.is_equal)\
                        .then_inc(sem["onehot"], 1)

            step1(0, None, None, None)
            step1(1, 0, None, None)
            step1(2, 1, 0, None)
            step1(3, 2, 1, 0, first=True)
            with dve.Fori(1, NP - 3) as i:
                step1(i + 3, i + 2, i + 1, i)
            step1(None, NP - 1, NP - 2, NP - 3)
            step1(None, None, NP - 1, NP - 2)
            step1(None, None, None, NP - 1)

            steps = [0]

            def sort_op(instruction):
                steps[0] += 1
                instruction.then_inc(sem["sort_step"], 1)
                dve.wait_ge(sem["sort_step"], steps[0])

            def by_expert(flat):
                return flat.rearrange("p (t e) -> p e t", e=NE)

            cnt3 = [cnt[:, n, :].rearrange("p (e t) -> p e t", e=NE) for n in range(2)]
            place3 = place.rearrange("p (e t) -> p e t", e=NE)
            dve.wait_ge(sem["rank_ps"], 1)
            sort_op(V.tensor_copy(cnt3[0], by_expert(bank(0, 1)[0:TT, 0:NT * NE])))
            sort_op(V.tensor_tensor(place3, by_expert(bank(0, 0)[0:TT, 0:NT * NE]), cnt3[0], ALU.subtract))
            shift, now = 1, 0
            while shift < NT:
                sort_op(V.tensor_copy(cnt3[1 - now][:, :, 0:shift], cnt3[now][:, :, 0:shift]))
                sort_op(V.tensor_tensor(cnt3[1 - now][:, :, shift:NT], cnt3[now][:, :, shift:NT],
                                        cnt3[now][:, :, 0:NT - shift], ALU.add))
                shift, now = 2 * shift, 1 - now
            sums = cnt3[now]
            sort_op(V.tensor_tensor(place3, place3, sums, ALU.add))
            tile_at = w("tile_at")[0:TT, :]
            sort_op(V.tensor_tensor(cnt3[1 - now], sums[:, :, NT - 1:NT].broadcast_to([TT, NE, NT]),
                                    tile_at.unsqueeze(1).broadcast_to([TT, NE, NM]), ALU.is_gt))
            sort_op(V.tensor_reduce(e_tiles, cnt3[1 - now], AX, ALU.add))
            sort_op(V.memset(e_start[:, 0:1], 0.0))
            for e in range(1, NE):
                sort_op(V.scalar_tensor_tensor(out=e_start[:, e:e + 1], in0=e_tiles[:, e - 1:e], scalar=float(TM),
                                               in1=e_start[:, e - 1:e], op0=ALU.mult, op1=ALU.add))
            tiles3 = cnt3[1 - now]
            sort_op(V.tensor_tensor(tiles3[:, 1:NE, :], tile_at.unsqueeze(1).broadcast_to([TT, NE - 1, NM]),
                                    e_start[:, 1:NE].unsqueeze(2).broadcast_to([TT, NE - 1, NM]), ALU.is_ge))
            sort_op(V.tensor_tensor(tiles3[:, 1, :], tiles3[:, 1, :], tiles3[:, 2, :], ALU.add))
            V.tensor_tensor(tile_expert[:], tiles3[0:1, 1, :], tiles3[0:1, 3, :], ALU.add).then_inc(sem["ids_ready"], 1)
            sort_op(V.tensor_tensor(place3, e_start.unsqueeze(2).broadcast_to([TT, NE, NT]), place3, ALU.add))
            sort_op(V.tensor_tensor(place3, place3, oh.rearrange("p t e -> p e t"), ALU.mult))
            sort_op(V.tensor_reduce(spot, place.rearrange("p (e t) -> p t e", e=NE), AX, ALU.add))
            sort_op(V.memset(reached[:, :, NM:NM + 1], 0.0))
            sort_op(V.tensor_tensor(reached[:, :, 0:NM], spot.unsqueeze(2).broadcast_to([TT, NT, NM]),
                                    tile_at.unsqueeze(1).broadcast_to([TT, NT, NM]), ALU.is_ge))
            sort_op(V.tensor_reduce(spot_in, reached[:, :, 0:NM], AX, ALU.add))
            sort_op(V.tensor_scalar(spot_in, spot_in, -float(TM), float(TM), ALU.mult, ALU.add))
            sort_op(V.tensor_tensor(spot_in, spot_in, spot, ALU.add))
            sort_op(V.tensor_tensor(in_tile, reached[:, :, 0:NM], reached[:, :, 1:NM + 1], ALU.subtract))
            for d, digit in enumerate(("id_high", "id_low")):
                V.tensor_tensor(tile_id[:, :, d], in_tile, w(digit)[0:TT, :].unsqueeze(2).broadcast_to([TT, NT, NM]),
                                ALU.mult).then_inc(sem["perm_ready"], 1)
            for part in range(2):
                of = slice(part * NP, (part + 1) * NP)
                V.tensor_tensor(perm[:, of], spot_in[:, of].unsqueeze(2).broadcast_to([TT, NP, TM]),
                                w("row_no")[0:TT, :].unsqueeze(1).broadcast_to([TT, NP, TM]), ALU.is_equal)\
                    .then_inc(sem["perm_ready"], 1)
            dve.wait_ge(sem["ids_ps"], 1)
            sort_op(V.tensor_copy(id_low[:], bank(0, 2)[:, NM:2 * NM]))
            sort_op(V.scalar_tensor_tensor(out=id_sum, in0=bank(0, 2)[:, 0:NM], scalar=float(DIGIT), in1=id_low,
                                           op0=ALU.mult, op1=ALU.add))
            sort_op(V.tensor_scalar(id_hole, id_sum, 0.0, NOWHERE, ALU.is_equal, ALU.mult))
            V.scalar_tensor_tensor(out=ids[:], in0=id_sum, scalar=-1.0, in1=id_hole,
                                   op0=ALU.add, op1=ALU.add).then_inc(sem["ids_ready"], 1)
            V.memset(mxT[HC:HC + 1], 1.0).then_inc(sem["x_turned"], 1)

            def copy_x(p, u, first=False):
                k = p * 2 + u
                dve.wait_ge(sem["x_turned_ps"], k + 1)
                if not first:
                    dve.wait_ge(sem["hid_ps"], 2 * (k - 1))
                V.tensor_copy(mxT[0:HC, u], bank(u, 1)[0:HC, 0:2 * TM].rearrange("p (c t) -> p c t", c=2))\
                    .then_inc(sem["x_turned"], 1)

            def copy_hidden(p, u, first=False):
                k = p * 2 + u
                if not first:
                    dve.wait_ge(sem["moe_ps"], k - 1)
                for half in range(2):
                    dve.wait_ge(sem["hidT_ps"], 2 * k + 1 + half)
                    V.tensor_copy(hidT[:, u, half * 3 * TM:(half + 1) * 3 * TM], bank(u, 2 + half)[:, 0:3 * TM])\
                        .then_inc(sem["hidT_ready"], 1)

            def add_bias(p, u, e, first=False):
                k = p * 2 + u
                dve.wait_ge(sem["moe_ps"], k + 1)
                if not first:
                    dve.wait_ge(put[u], p * 16)
                V.tensor_tensor(my[:, u, :], bank(u, 0)[:, 0:C],
                                w("b2").rearrange("p (e n) -> p e n", e=NE)[:, bass.ds(e, 1), :]
                                .rearrange("p e n -> p (e n)"), ALU.add).then_inc(sem["moe_y"], 1)
                dve.wait_ge(sem["moe_y"], k + 1)
                dve.wait_ge(got_h[u], (p + 1) * 16)
                V.tensor_tensor(my[:, u, :], my[:, u, :], mh[:, u, :], ALU.add).then_inc(sem["moe_sum"], 1)

            def expert_of(k):
                return dve.value_load(tile_expert[0:1, bass.ds(k, 1)], min_val=0, max_val=NE - 1)

            def tiles(p, first=False):
                e0, e1 = expert_of(p * 2), expert_of(p * 2 + 1)
                copy_hidden(p, 0, first)
                copy_x(p + 1, 0)
                add_bias(p, 0, e0, first)
                copy_hidden(p, 1, first)
                copy_x(p + 1, 1)
                add_bias(p, 1, e1, first)

            copy_x(0, 0, True)
            copy_x(0, 1, True)
            dve.wait_ge(sem["ids_ready"], 2)
            tiles(0, True)
            with dve.Fori(1, NP - 1) as i:
                tiles(i)
            for u in range(2):
                copy_hidden(NP - 1, u)
                add_bias(NP - 1, u, expert_of(NM - 2 + u))

        @block.scalar
        def _(act):
            A = nc.scalar

            def copy_norm(k, i):
                for u in range(2):
                    act.wait_ge(xnT_ps[k], i * 2 + u + 1)
                    A.activation(norm_outT[k][0:HC, u],
                                 bank(u, norm_bank[k])[0:HC, 0:2 * TT].rearrange("p (c t) -> p c t", c=2),
                                 ACT.Copy).then_inc(xnT_s[k], 1)

            def copy_v(at0, n, lo, slots=range(2)):
                for u in slots:
                    act.wait_ge(sem["vq_ps"], at0 + u + 1)
                    A.activation(v_sb[:, u, :], bank(u, n)[0:TT, lo:lo + C], ACT.Copy).then_inc(sem["v_copied"], 1)

            def diagonal(u, c):
                return qz[:, u].rearrange("p c (b x) -> p c b x", b=GI)[:, c, :, 0:NTOK]

            def exponentials(at0, scale, slots=range(2)):
                for u in slots:
                    act.wait_ge(sem["centred"], at0 + u + 1)
                    A.activation(pr_a[:, u, :], sc_a[:, u, :], ACT.Exp, scale=scale).then_inc(sem["exped"], 1)

            def copy_turned(at0, slots=range(2)):
                for u in slots:
                    act.wait_ge(sem["pt_ps"], at0 + u + 1)
                    own = pz[:, u].rearrange("p (b x) -> p b x", b=GI)[:, :, 0:4 * TT]\
                        .rearrange("p b (g t) -> p b g t", g=4)[:, :, :, 0:NTOK]
                    A.activation(own, bank(u, 2)[0:TT, 0:4 * TT].rearrange("p (g b n) -> p b g n", g=4, b=GI),
                                 ACT.Copy).then_inc(sem["pT_ready"], 1)

            def copy_values(at0):
                for u in range(2):
                    act.wait_ge(sem["o_ps"], at0 + u + 1)
                    A.activation(oT[0:HC, u], bank(u, 3)[0:HC, 0:2 * TT].rearrange("p (c t) -> p c t", c=2),
                                 ACT.Copy).then_inc(sem["oT_ready"], 1)

            def square_pixels(i):
                for u in range(2):
                    act.wait_ge(load_x[u], (i + 1) * 16)
                    for b in range(GI):
                        src = x_sb[:, u, :].rearrange("p (k b n) -> p k b n", k=KF, b=GI)[:, :, b, :]
                        A.activation(squares[:, u, b, :].rearrange("p (k n) -> p k n", k=KF), src, ACT.Square,
                                     accum_out=ssq[:, u, b:b + 1]).then_inc(sem["ssq_ready"], 1)

            def square_embedded(i):
                for u in range(2):
                    act.wait_ge(sem["y_ready"], i * 2 + u + 1)
                    A.activation(y_squares[:, u, :], y_sb[:, u, :], ACT.Square,
                                 accum_out=c1(u, 2)).then_inc(sem["ysum_ready"], 1)

            def copy_q(i):
                for u in range(2):
                    for c in range(2):
                        src = bank(u, 1)[0:HC, c * TT:(c + 1) * TT].rearrange("p (b n) -> p b n", b=GI)
                        last = A.activation(diagonal(u, c), src, ACT.Copy)
                    last.then_inc(sem["qz_ready"], 1)

            def ffn_copies(i):
                for u in range(2):
                    act.wait_ge(sem["f_gate_ps"], i * 2 + u + 1)
                    A.activation(gs[:, u, 0:E0], bank(u, 2)[0:TT, 0:E0], ACT.Copy).then_inc(sem["f_logits"], 1)
                    act.wait_ge(sem["f_qk_ps"], i * 2 + u + 1)
                    A.activation(f_q0[:, u, :].rearrange("p (b n) -> p b n", b=GI)[:, :, 1:NTOK + 1],
                                 bank(u, 3)[0:HD0, 0:TT].rearrange("p (b n) -> p b n", b=GI), ACT.Copy)\
                        .then_inc(sem["f_q0_ready"], 1)
                    A.activation(f_q1[HD0:128, u, :], bank(u, 3)[HD0:128, 0:TT], ACT.Copy)
                    A.activation(f_q2[0:HD0, u, :], bank(u, 3)[0:HD0, TT:2 * TT], ACT.Copy)
                    A.activation(f_k[:, u, :], bank(u, 3)[:, 2 * TT:3 * TT], ACT.Copy)
                    A.activation(f_k2[0:HD0, u, :], bank(u, 3)[0:HD0, 3 * TT:4 * TT], ACT.Copy)\
                        .then_inc(sem["f_copied"], 1)

            def ffn_gate_steps(i):
                for u in range(2):
                    act.wait_ge(sem["gcentred"], i * 2 + u + 1)
                    A.activation(gs[:, u, 8:8 + E0], gs[:, u, 8:8 + E0], ACT.Exp,
                                 accum_out=gs[:, u, 12:13]).then_inc(sem["gexp"], 1)

            def ffn_exponentials(i):
                for u in range(2):
                    act.wait_ge(sem["gate_step"], i * 18 + u * 8 + 4)
                    A.activation(gs[:, u, 32:32 + E0], gs[:, u, 16:16 + E0], ACT.Exp).then_inc(sem["gexp2"], 1)
                for u in range(2):
                    act.wait_ge(sem["f_centred"], i * 2 + u + 1)
                    A.activation(pr[:, u, 0:E0 * TT], sc[:, u, 0:E0 * TT], ACT.Exp).then_inc(sem["f_exped"], 1)

            def ffn_copy_turned(i):
                for u in range(2):
                    act.wait_ge(sem["f_pt_ps"], i * 2 + u + 1)
                    A.activation(pT[:, u, 0:E0], bank(u, 2)[0:TT, 0:E0 * TT].rearrange("p (e t) -> p e t", e=E0),
                                 ACT.Copy).then_inc(sem["f_pT"], 1)

            def ffn_copy_values(i):
                for u in range(2):
                    act.wait_ge(sem["f_o_ps"], i * 2 + u + 1)
                    A.activation(f_oT[:, u, 0, :], bank(u, 3)[:, 0:TT], ACT.Copy)
                    A.activation(f_oT[0:HD0, u, 1, :], bank(u, 3)[0:HD0, TT:2 * TT], ACT.Copy)\
                        .then_inc(sem["f_oT"], 1)

            def keep_q(i, slots):
                for u in slots:
                    t = i * 2 + u
                    act.wait_ge(sem["l1_q_ps"], t + 1)
                    plain(act)
                    A.activation(qT_all[0:HC, :, bass.ds(t * TT, TT)],
                                 bank(u, 3)[0:HC, 0:2 * TT].rearrange("p (c t) -> p c t", c=2), ACT.Copy)\
                        .then_inc(sem["l1_q_stored"], 1)

            def step(n, a, b):
                if a is not None:
                    square_embedded(a)
                if b is not None:
                    copy_turned(b * 2, (1,))
                    copy_values(b * 2)
                if a is not None:
                    copy_norm(0, a)
                    copy_v(a * 2, 1, 256)
                    copy_q(a)
                if b is not None:
                    copy_norm(1, b)
                    ffn_copies(b)
                    ffn_gate_steps(b)
                if n is not None:
                    square_pixels(n)
                if b is not None:
                    ffn_exponentials(b)
                    ffn_copy_turned(b)
                    ffn_copy_values(b)
                if a is not None:
                    exponentials(a * 2, 1.0, (0,))
                if b is not None:
                    copy_norm(2, b)
                    keep_q(b, (0,))
                if a is not None:
                    copy_turned(a * 2, (0,))
                    exponentials(a * 2, 1.0, (1,))
                if b is not None:
                    keep_q(b, (1,))

            early = W_AT[W_PACK[EARLY][0]][0]
            act.dma_start(wc[:, 0:early], w_in[:, 0:early]).then_inc(sem["w_consts"], 16)
            act.wait_ge(load_x[1], 16)
            act.dma_start(wc[:, early:], w_in[:, early:]).then_inc(sem["w_late"], 16)
            act.wait_ge(sem["ones_ready"], 1)
            step(0, None, None)
            act.wait_ge(sem["fills_ready"], 5)
            step(1, 0, None)
            step(2, 1, 0)
            with act.Fori(1, NP - 2) as i:
                step(i + 2, i + 1, i)
            step(None, NP - 1, NP - 2)
            step(None, None, NP - 1)

            rel2_rows = rel2.rearrange("t (b i) s -> (t b) i s", b=GI)
            for j in range(NTOK):
                act.wait_ge(sem["rel2_ps"], j + 1)
                if j >= 4:
                    act.wait_ge(rel2_out[j % 4], 16 * (j // 4))
                A.activation(rel2_buf[j % 4], bank(0, j % 4)[0:BP, 0:H * NTOK], ACT.Copy)\
                    .then_inc(sem["rel2_copied"], 1)
                act.wait_ge(sem["rel2_copied"], j + 1)
                act.dma_start(rel2_rows[:, j, :], rel2_buf[j % 4]).then_inc(rel2_out[j % 4], 16)
            act.wait_ge(sem["rel3_copied"], NTOK)
            rel3_rows = rel3.rearrange("t (b i) (h s) -> h i (t b) s", b=GI, h=3)
            for images, done in ((slice(0, 2 * GI), "rel3_first"), (slice(2 * GI, BP), "rel3_out")):
                for h in range(GI):
                    act.dma_start(rel3_rows[h][:, images, :],
                                  rel3_sb[h * NTOK:(h + 1) * NTOK, images].rearrange("p b g j -> p b (g j)"))\
                        .then_inc(sem[done], 16)

            def spread_q1(i):
                for u in range(2):
                    for c in range(2):
                        src = qT_all[0:HC, c, bass.ds((i * 2 + u) * TT, TT)].rearrange("p (b n) -> p b n", b=GI)
                        last = A.activation(diagonal(u, c), src, ACT.Copy)
                    last.then_inc(sem["qz_ready"], 1)

            def step1(n, a, b, c):
                scale = 1.0 / (3.0 * D) ** 0.5
                if b is not None:
                    copy_turned(NT + b * 2, (1,))
                if a is not None:
                    spread_q1(a)
                if b is not None:
                    copy_values(NT + b * 2)
                if c is not None:
                    copy_norm(4, c)
                if a is not None:
                    exponentials(NT + a * 2, scale, (0,))
                if n is not None:
                    copy_norm(3, n)
                    copy_v(NT + n * 2, 3, 256, (0,))
                if a is not None:
                    copy_turned(NT + a * 2, (0,))
                if n is not None:
                    copy_v(NT + n * 2, 3, 256, (1,))
                if a is not None:
                    exponentials(NT + a * 2, scale, (1,))

            step1(0, None, None, None)
            step1(1, 0, None, None)
            step1(2, 1, 0, None)
            step1(3, 2, 1, 0)
            with act.Fori(1, NP - 3) as i:
                step1(i + 3, i + 2, i + 1, i)
            step1(None, NP - 1, NP - 2, NP - 3)
            step1(None, None, NP - 1, NP - 2)
            step1(None, None, None, NP - 1)

            def activate(p, u, first=False):
                k = p * 2 + u
                if not first:
                    act.wait_ge(sem["hidT_ps"], 2 * (k - 1))
                for half in range(2):
                    act.wait_ge(sem["hid_ps"], 2 * k + 1 + half)
                    A.activation(hid[:, u, half * HID // 2:(half + 1) * HID // 2], bank(u, half)[:, 0:HID // 2],
                                 ACT.Gelu).then_inc(sem["hid_ready"], 1)

            activate(0, 0, True)
            activate(0, 1, True)
            with act.Fori(1, NP) as i:
                for u in range(2):
                    activate(i, u)

        @block.gpsimd
        def _(pool):
            G = nc.gpsimd

            def power(k, i):
                c0 = norm_at[k]
                for u in range(2):
                    pool.wait_ge(mean[k], i * 2 + u + 1)
                    plain(pool)
                    G.tensor_scalar(c1(u, c0 + 11), c1(u, c0 + 9), LN_EPS, None, ALU.add).then_inc(rstd_in[k], 1)
                    pool.wait_ge(rstd_in[k], i * 2 + u + 1)
                    G.tensor_tensor(c1(u, c0 + 12), c1(u, c0 + 11), mhalf[0:TT], ALU.pow).then_inc(rstd[k], 1)

            def pixel_power(i):
                for u in range(2):
                    pool.wait_ge(sem["rms1_in"], i * 2 + u + 1)
                    G.tensor_tensor(c1(u, 1), c1(u, 0), mhalf[0:TT], ALU.pow).then_inc(sem["rms1"], 1)

            def embed_power(i):
                for u in range(2):
                    pool.wait_ge(sem["rms2_in"], i * 2 + u + 1)
                    G.tensor_tensor(c1(u, 4), c1(u, 3), mhalf[0:TT], ALU.pow).then_inc(sem["rms2"], 1)

            def gate(i):
                for u in range(2):
                    pool.wait_ge(sem["f_logits"], i * 2 + u + 1)
                    plain(pool)
                    G.tensor_scalar(gs[:, u, 5:6], gs[:, u, 0:1], gs[:, u, 1:2], gs[:, u, 2:3],
                                    ALU.max, ALU.max).then_inc(sem["gate_step"], 1)
                    pool.wait_ge(sem["gate_step"], i * 18 + u + 1)
                    plain(pool)
                    G.tensor_scalar(gs[:, u, 8:8 + E0], gs[:, u, 0:E0], gs[:, u, 5:6], None, ALU.subtract)\
                        .then_inc(sem["gcentred"], 1)
                for u in range(2):
                    t = i * 2 + u
                    at = i * 18 + 2 + u * 8
                    pool.wait_ge(sem["gexp"], t + 1)
                    G.tensor_tensor(gs[:, u, 13:14], gs[:, u, 12:13], mone[0:TT], ALU.pow)\
                        .then_inc(sem["gate_step"], 1)
                    pool.wait_ge(sem["gate_step"], at + 1)
                    plain(pool)
                    G.tensor_scalar(gs[:, u, 16:16 + E0], gs[:, u, 8:8 + E0], gs[:, u, 13:14], None,
                                    ALU.mult).then_inc(sem["gate_step"], 1)
                    pool.wait_ge(sem["gate_step"], at + 2)
                    plain(pool)
                    G.tensor_scalar(gs[:, u, 21:22], gs[:, u, 16:17], gs[:, u, 17:18], gs[:, u, 18:19],
                                    ALU.min, ALU.min).then_inc(sem["gate_step"], 1)
                    pool.wait_ge(sem["gate_step"], at + 3)
                    plain(pool)
                    G.tensor_scalar(gs[:, u, 24:24 + E0], gs[:, u, 16:16 + E0], gs[:, u, 21:22], None,
                                    ALU.is_le).then_inc(sem["gate_step"], 1)
                    pool.wait_ge(sem["gate_step"], at + 4)
                    G.tensor_tensor(gs[:, u, 28:28 + E0], gs[:, u, 24:24 + E0], w("rank_up")[0:TT, :], ALU.mult)\
                        .then_inc(sem["gate_step"], 1)
                    pool.wait_ge(sem["gate_step"], at + 5)
                    plain(pool)
                    G.tensor_scalar(gs[:, u, 45:46], gs[:, u, 28:29], gs[:, u, 29:30], gs[:, u, 30:31],
                                    ALU.max, ALU.max).then_inc(sem["gate_step"], 1)
                    pool.wait_ge(sem["gate_step"], at + 6)
                    plain(pool)
                    G.tensor_scalar(gs[:, u, 48:48 + E0], gs[:, u, 28:28 + E0], gs[:, u, 45:46], None,
                                    ALU.is_lt).then_inc(sem["gate_step"], 1)
                    pool.wait_ge(sem["gate_step"], at + 7)
                    pool.wait_ge(sem["gexp2"], t + 1)
                    G.tensor_tensor(gs[:, u, 36:36 + E0], gs[:, u, 32:32 + E0], gs[:, u, 48:48 + E0], ALU.mult)\
                        .then_inc(sem["gate_step"], 1)
                    pool.wait_ge(sem["gate_step"], at + 8)
                    plain(pool)
                    G.tensor_scalar(gs[:, u, 40:41], gs[:, u, 36:37], gs[:, u, 37:38], gs[:, u, 38:39],
                                    ALU.add, ALU.add).then_inc(sem["gwsum"], 1)

            def step(n, a, b):
                if a is not None:
                    embed_power(a)
                    power(0, a)
                if b is not None:
                    power(1, b)
                    gate(b)
                    power(2, b)
                if n is not None:
                    pixel_power(n)

            G.memset(mone[:], -1.0)
            G.memset(ones[:], 1.0).then_inc(sem["fills_ready"], 1)
            G.memset(mhalf[:], -0.5).then_inc(sem["fills_ready"], 1)
            for zeros in (vblk, qz, pz):
                G.memset(zeros[:], 0.0).then_inc(sem["fills_ready"], 1)
            pool.wait_ge(sem["fills_ready"], 2)
            pool.wait_ge(sem["w_consts"], 16)
            step(0, None, None)
            step(1, 0, None)
            pool.wait_ge(sem["w_late"], 16)
            step(2, 1, 0)
            with pool.Fori(1, NP - 2) as i:
                step(i + 2, i + 1, i)
            step(None, NP - 1, NP - 2)
            step(None, None, NP - 1)

            def spread_k1(i, first=False):
                for u in range(2):
                    t = i * 2 + u
                    if not first:
                        pool.wait_ge(sem["s_ps"], NT + t - 1)
                        plain(pool)
                    for c in range(2):
                        last = G.tensor_tensor(
                            kblk[:, u, c], kT_all[0:HC, c, bass.ds(t * TT, TT)].unsqueeze(1).broadcast_to([HC, 6, TT]),
                            w("head_mask")[0:HC].unsqueeze(2).broadcast_to([HC, 6, TT]), ALU.mult)
                    last.then_inc(sem["kblk_ready"], 1)

            def add_terms(i):
                for u in range(2):
                    pool.wait_ge(load_rel[u], (i + 1) * 32)
                    plain(pool)
                    G.tensor_tensor(rel_t[u][0], rel_t[u][0], rel_t[u][1], ALU.add).then_inc(sem["terms_added"], 1)

            def step1(n, a, c, first=False):
                if a is not None:
                    spread_k1(a, first)
                if c is not None:
                    power(4, c)
                if n is not None:
                    power(3, n)
                if a is not None:
                    add_terms(a)

            pool.wait_ge(sem["l1_k_stored"], NT)
            pool.wait_ge(sem["rel3_copied"], NTOK)
            step1(0, None, None)
            step1(1, 0, None, first=True)
            step1(2, 1, None)
            step1(3, 2, 0)
            with pool.Fori(1, NP - 3) as i:
                step1(i + 3, i + 2, i)
            step1(None, NP - 1, NP - 3)
            step1(None, None, NP - 2)
            step1(None, None, NP - 1)

            def fetch(dst, rows, idx, u, got):
                return G.indirect_dma_start(dst[:, u, :], None, rows[:, :],
                                            bass.IndirectOffsetOnAxis(ap=idx[:, u:u + 1], axis=0),
                                            bounds_check=NT_TOK - 1, oob_is_err=False).then_inc(got[u], 16)

            def fetch_x(p, u, first=False):
                k = p * 2 + u
                if not first:
                    pool.wait_ge(sem["x_turned_ps"], k - 1)
                    plain(pool)
                G.tensor_copy(idx_x[:, u:u + 1], ids[:, bass.ds(k, 1)]).then_inc(sem["idx_x_ready"], 1)
                pool.wait_ge(sem["idx_x_ready"], k + 1)
                plain(pool)
                fetch(mx, xn_rows, idx_x, u, got_x)

            def fetch_h(p, u, first=False):
                k = p * 2 + u
                if not first:
                    pool.wait_ge(sem["moe_sum"], k - 1)
                    plain(pool)
                    pool.wait_ge(put[u], p * 16)
                    plain(pool)
                G.tensor_copy(idx_h[:, u:u + 1], ids[:, bass.ds(k, 1)]).then_inc(sem["idx_h_ready"], 1)
                pool.wait_ge(sem["idx_h_ready"], k + 1)
                plain(pool)
                fetch(mh, h_rows, idx_h, u, got_h)

            def store(p, u):
                k = p * 2 + u
                pool.wait_ge(sem["moe_sum"], k + 1)
                plain(pool)
                G.indirect_dma_start(out[:, :], bass.IndirectOffsetOnAxis(ap=idx_h[:, u:u + 1], axis=0),
                                     my[:, u, :], None, bounds_check=NT_TOK - 1, oob_is_err=False)\
                    .then_inc(put[u], 16)

            pool.wait_ge(sem["onehot"], NT)
            G.memset(mx, 0.0).then_inc(sem["rows_clear"], 1)
            G.memset(mh, 0.0).then_inc(sem["rows_clear"], 1)
            pool.wait_ge(sem["rows_clear"], 2)
            pool.wait_ge(sem["ids_ready"], 2)
            pool.wait_ge(sem["xn_stored"], 16 * NP)
            pool.wait_ge(sem["h_stored"], 16 * NP)
            for u in range(2):
                fetch_x(0, u, True)
            for u in range(2):
                fetch_h(0, u, True)
            for u in range(2):
                fetch_x(1, u)
            with pool.Fori(0, NP - 2) as i:
                for u in range(2):
                    store(i, u)
                    fetch_x(i + 2, u)
                    fetch_h(i + 1, u)
            for u in range(2):
                store(NP - 2, u)
                fetch_h(NP - 1, u)
            for u in range(2):
                store(NP - 1, u)
            for u in range(2):
                pool.wait_ge(put[u], NP * 16)


_OUT_SHAPE = (NT_TOK, C)


def _put(pack, at, name, a, rows=0):
    lo, n = at[name]
    a = np.asarray(a, np.float32).reshape(a.shape[0], -1)
    assert a.shape[1] == n, (name, a.shape, n)
    pack[rows:rows + a.shape[0], lo:lo + n] = a


def _slab(weights, bias):
    n = weights.shape[1]
    out = np.zeros((HC + 1, 2, n), np.float32)
    out[0:HC] = weights.reshape(2, HC, n).transpose(1, 0, 2)
    out[HC, 1] = bias
    return out


def layout(a):
    x = a["x"]
    hw = IMG // PS
    x = x.reshape(B, CH, hw, PS, hw, PS).transpose(0, 2, 4, 3, 5, 1).reshape(B, NTOK, FEAT)
    x = np.concatenate([x, np.zeros((BP - B, NTOK, FEAT), np.float32)])
    x = x.reshape(NT, TT, KF, 128).transpose(0, 3, 2, 1).reshape(NT, 128, KF * TT)

    rows = np.arange(TT)
    img, tok = rows // NTOK, rows % NTOK
    tok_pack = np.zeros((128, TOK_COLS), np.float32)
    _put(tok_pack, TOK_AT, "wt", a["L0_tok_W"].T.reshape(KF, 128, C).transpose(1, 0, 2))
    _put(tok_pack, TOK_AT, "g1", a["L0_tok_g1"].T.reshape(KF, 128, NTOK).transpose(1, 0, 2))
    _put(tok_pack, TOK_AT, "tok_b", np.broadcast_to(a["L0_tok_b"], (TT, C)))
    _put(tok_pack, TOK_AT, "g2", np.tile(a["L0_tok_g2"], (GI, 1)))
    _put(tok_pack, TOK_AT, "ident", np.eye(128))
    _put(tok_pack, TOK_AT, "same_image", (img[:, None] == img) / (NTOK * C))
    _put(tok_pack, TOK_AT, "pixel_mean", np.full((128, TT), 1.0 / (NTOK * FEAT)))

    select = (tok[:, None, None] == tok) & (img[:, None, None] == np.arange(GI)[:, None])
    _put(tok_pack, TOK_AT, "select_image", select)

    wp = np.zeros((128, W_COLS), np.float32)
    wq, bq = a["L0_attn_w_qkv"], a["L0_attn_b_qkv"]
    fq, fb = a["L0_ffn_Wqk"], a["L0_ffn_bqk"]
    slabs = {
        "q0": (wq[:, :C], bq[:C]), "k0": (wq[:, C:2 * C], bq[C:2 * C]), "v0": (wq[:, 2 * C:], bq[2 * C:]),
        "o0": (a["L0_attn_w_proj"], a["L0_attn_b_proj"]),
        "fq": (fq[:, :C], fb[:C]), "fk": (fq[:, C:], fb[C:]),
        "fv": (a["L0_ffn_Wv"].transpose(1, 0, 2).reshape(C, C), a["L0_ffn_bv"].reshape(C)),
        "fg1": (a["L0_ffn_Wg1"], a["L0_ffn_bg1"]),
        "q1": (a["L1_attn_Wq"], a["L1_attn_bq"]), "k1": (a["L1_attn_Wk"], a["L1_attn_bk"]),
        "v1": (a["L1_attn_Wv"], a["L1_attn_bv"]), "o1": (a["L1_attn_Wo"], a["L1_attn_bo"]),
        "pk": (a["L1_attn_Wpk"], a["L1_attn_bpk"]), "pq": (a["L1_attn_Wpq"], a["L1_attn_bpq"]),
        "gate": (a["L1_ffn_gate_w"], a["L1_ffn_gate_b"]),
    }
    for name, (weights, bias) in slabs.items():
        _put(wp, W_AT, name, _slab(weights, bias))
    _put(wp, W_AT, "fg2", np.concatenate([a["L0_ffn_Wg2"], a["L0_ffn_bg2"][None]]))
    _put(wp, W_AT, "fpa", a["L0_ffn_Wp"][:128])
    _put(wp, W_AT, "fpb", np.concatenate([a["L0_ffn_Wp"][128:], a["L0_ffn_bp"][None]]))
    _put(wp, W_AT, "center", np.broadcast_to(a["L1_ffn_gate_center"], (TT, NE)))
    middle = (a["L1_attn_rel_table"].shape[0] - 1) // 2
    table = a["L1_attn_rel_table"][middle - NTOK + 1:middle + NTOK]
    _put(wp, W_AT, "relT", _slab(table.T, np.ones(REL, np.float32)))
    _put(wp, W_AT, "relrevT", _slab(table[::-1].T, np.ones(REL, np.float32)))
    head = np.array([3 * g + h for h in range(3) for g in range(2)])
    _put(wp, W_AT, "head_mask", (np.arange(HC)[:, None] // D == head).astype(np.float32))
    _put(wp, W_AT, "head_scale", np.repeat(a["L0_attn_scale"], D).reshape(2, HC).T)
    _put(wp, W_AT, "third_mask", (img[:, None] == np.arange(GI)).astype(np.float32))
    _put(wp, W_AT, "diag_mask", np.where((tok[:, None] == np.arange(NTOK)) & (tok[:, None] >= 1), NEG, 0.0))
    _put(wp, W_AT, "causal", np.where((img[:, None] == img) & (tok[None] <= tok[:, None]), 0.0, NEG))
    _put(wp, W_AT, "pos", np.tile(a["L0_ffn_pos_bias"][:NTOK, :NTOK], (GI, GI)))
    _put(wp, W_AT, "rank_up", np.broadcast_to(np.arange(1, E0 + 1), (TT, E0)))
    _put(wp, W_AT, "rank_down", np.broadcast_to(np.arange(NE, 0, -1), (TT, NE)))
    _put(wp, W_AT, "conv", np.concatenate([a["L0_ffn_conv_w"][:, 0], a["L0_ffn_conv_b"][:, None]], 1))
    _put(wp, W_AT, "b2", np.broadcast_to(a["L1_ffn_b2"].reshape(1, NE * C), (128, NE * C)))

    _put(wp, W_AT, "before", rows[:, None] < rows)
    token_id = 1 + TT * np.arange(NT) + rows[:, None]
    _put(wp, W_AT, "id_high", token_id // DIGIT)
    _put(wp, W_AT, "id_low", token_id % DIGIT)
    _put(wp, W_AT, "tile_at", np.broadcast_to(TM * np.arange(NM), (TT, NM)))
    _put(wp, W_AT, "row_no", np.broadcast_to(np.arange(TM), (TT, TM)))

    moe = np.zeros((128, BIG_COLS), np.float32)
    moe[:HC + 1, :2 * NE * HID] = np.stack([_slab(w1, b1) for w1, b1 in zip(a["L1_ffn_w1"], a["L1_ffn_b1"])],
                                           1).reshape(HC + 1, -1)
    moe[:, 2 * NE * HID:] = a["L1_ffn_w2"].reshape(NE, KH, 128, C).transpose(2, 0, 1, 3).reshape(128, -1)
    return {"x_in": np.ascontiguousarray(x), "tok_in": tok_pack, "w_in": wp, "moe_in": moe}


def program(nc, arrays):
    args = [nc.dram_tensor(n, v.shape, F32, kind="ExternalInput").ap() for n, v in arrays.items()]
    scratch = [nc.dram_tensor(n, (NT, TT, H * NTOK), F32).ap() for n in ("rel2_scratch", "rel3_scratch")]
    scratch += [nc.dram_tensor(n, (NT_TOK, C), F32).ap() for n in ("xn_rows", "h_rows")]
    out = nc.dram_tensor("out", _OUT_SHAPE, F32, kind="ExternalOutput").ap()
    build(nc, *args, *scratch, out)


def kernel(**inputs):
    import concourse.bacc as bacc
    from concourse.bass_utils import run_bass_kernel_spmd

    arrays = layout({k: np.asarray(v) for k, v in inputs.items()})
    nc = bacc.Bacc("TRN2", target_bir_lowering=False, num_devices=1)
    program(nc, arrays)
    got = run_bass_kernel_spmd(nc, [arrays], core_ids=[0]).results[0]["out"]
    return got.reshape(BP, NTOK, C)[:B]
```
